# Optimizing a Trainium2 kernel written in Bass

```python
import numpy as np
import jax
import jax.numpy as jnp

def _softmax(x, axis=-1):
    return jax.nn.softmax(x, axis=axis)

def _gelu(x):
    return jax.nn.gelu(x, approximate=True)

def _silu(x):
    return jax.nn.silu(x)

def _sigmoid(x):
    return jax.nn.sigmoid(x)

def _layernorm(x, axis=-1, eps=1e-05):
    m = jnp.mean(x, axis=axis, keepdims=True)
    v = jnp.var(x, axis=axis, keepdims=True)
    return (x - m) / jnp.sqrt(v + eps)

def _scatter_add(tgt, idx, src, axis=0):
    return tgt.at[idx].add(src)

def _segment_sum(src, seg, n):
    return jax.ops.segment_sum(src, seg, n)
kernel_name = 'mk_gnn_ffn_d1_gnn_r8_bbc4ae'

def setup_inputs(seed: int=0):
    np.random.seed(seed)
    _w = jnp.asarray

    def _rec_inputs():
        import jax
        import jax.numpy as jnp
        _gk = jax.random.key(seed)
        x = -0.0003929 + 0.9999 * jax.random.normal(jax.random.fold_in(_gk, 1), (6250, 256), jnp.float32)
        _s = jax.random.randint(jax.random.fold_in(_gk, 2), (50000,), 0, 6250, jnp.int32)
        _d = jax.random.randint(jax.random.fold_in(_gk, 3), (50000,), 0, 6250, jnp.int32)
        _loop = jnp.arange(6250, dtype=jnp.int32)
        src = jnp.concatenate([_s, _d, _loop])
        dst = jnp.concatenate([_d, _s, _loop])
        _o = jnp.argsort(dst, stable=True)
        src = src[_o]
        dst = dst[_o]
        edge_weight = 0.00540447 + 1.00226 * jax.random.normal(jax.random.fold_in(_gk, 12), (106250,), jnp.float32)
        return (x, src, dst, edge_weight)
    x, src, dst, edge_weight = _rec_inputs()

    def _L0_gnn_setup():
        import jax, jax.numpy as jnp
        import numpy as np
        from itertools import combinations
        NDIM = 256
        BATCH = 8192

        def _build_mat(rots, idx_i, idx_j, ndim):

            def step(mat, t):
                i, j, theta = t
                c = jnp.cos(theta)
                s = jnp.sin(theta)
                ri = mat[i]
                rj = mat[j]
                mat = mat.at[i].set(c * ri - s * rj)
                mat = mat.at[j].set(s * ri + c * rj)
                return (mat, None)
            mat0 = jnp.eye(ndim, dtype=rots.dtype)
            mat, _ = jax.lax.scan(step, mat0, (idx_i, idx_j, rots))
            return mat.T
        key = jax.random.key(seed)
        k1, k2 = jax.random.split(key)
        pairs = np.array(list(combinations(range(NDIM), 2)), dtype=np.int32)
        return {'x': jax.random.normal(k1, (BATCH, NDIM), dtype=jnp.float32), 'rots': jax.random.normal(k2, (pairs.shape[0],), dtype=jnp.float32), 'idx_i': jnp.asarray(pairs[:, 0]), 'idx_j': jnp.asarray(pairs[:, 1])}
    _L0_gnn_all = _L0_gnn_setup()
    _L0_gnn_in = {k: v for k, v in _L0_gnn_all.items() if k in ()}
    del _L0_gnn_all

    def _L0_ffn_setup():
        import jax, jax.numpy as jnp
        import numpy as np
        DIM = 256
        H = 8
        D = 64
        G = 64
        INNER = H * D
        SCALE = D ** (-0.5)
        key = jax.random.key(seed)
        ks = jax.random.split(key, 12)
        B, N = (4, 2048)
        x = jax.random.normal(ks[0], (B, N, DIM), dtype=jnp.float32)
        s = lambda fan_in: 1.0 / np.sqrt(fan_in)
        W_fx = jax.random.normal(ks[1], (DIM, INNER), dtype=jnp.float32) * s(DIM)
        b_fx = jnp.zeros((INNER,), dtype=jnp.float32)
        W_x = jax.random.normal(ks[2], (DIM, INNER), dtype=jnp.float32) * s(DIM)
        b_x = jnp.zeros((INNER,), dtype=jnp.float32)
        A = jax.random.normal(ks[3], (G, D), dtype=jnp.float32)
        Q, _ = jnp.linalg.qr(A.T)
        W_slice = Q[:, :G].astype(jnp.float32)
        b_slice = jnp.zeros((G,), dtype=jnp.float32)
        W_q = jax.random.normal(ks[4], (D, D), dtype=jnp.float32) * s(D)
        W_k = jax.random.normal(ks[5], (D, D), dtype=jnp.float32) * s(D)
        W_v = jax.random.normal(ks[6], (D, D), dtype=jnp.float32) * s(D)
        W_out = jax.random.normal(ks[7], (INNER, DIM), dtype=jnp.float32) * s(INNER)
        b_out = jnp.zeros((DIM,), dtype=jnp.float32)
        temperature = jnp.ones((1, H, 1, 1), dtype=jnp.float32) * 0.5
        return {'x': x, 'W_fx': W_fx, 'b_fx': b_fx, 'W_x': W_x, 'b_x': b_x, 'W_slice': W_slice, 'b_slice': b_slice, 'W_q': W_q, 'W_k': W_k, 'W_v': W_v, 'W_out': W_out, 'b_out': b_out, 'temperature': temperature}
    _L0_ffn_all = _L0_ffn_setup()
    _L0_ffn_in = {k: v for k, v in _L0_ffn_all.items() if k in ('W_fx', 'b_fx', 'W_x', 'b_x', 'W_slice', 'b_slice', 'W_q', 'W_k', 'W_v', 'W_out', 'b_out', 'temperature')}
    del _L0_ffn_all
    return {'x': x, 'src': src, 'dst': dst, 'edge_weight': edge_weight, 'L0_ffn_W_fx': _L0_ffn_in['W_fx'], 'L0_ffn_b_fx': _L0_ffn_in['b_fx'], 'L0_ffn_W_x': _L0_ffn_in['W_x'], 'L0_ffn_b_x': _L0_ffn_in['b_x'], 'L0_ffn_W_slice': _L0_ffn_in['W_slice'], 'L0_ffn_b_slice': _L0_ffn_in['b_slice'], 'L0_ffn_W_q': _L0_ffn_in['W_q'], 'L0_ffn_W_k': _L0_ffn_in['W_k'], 'L0_ffn_W_v': _L0_ffn_in['W_v'], 'L0_ffn_W_out': _L0_ffn_in['W_out'], 'L0_ffn_b_out': _L0_ffn_in['b_out'], 'L0_ffn_temperature': _L0_ffn_in['temperature']}

def reference(x, src, dst, edge_weight, L0_ffn_W_fx, L0_ffn_b_fx, L0_ffn_W_x, L0_ffn_b_x, L0_ffn_W_slice, L0_ffn_b_slice, L0_ffn_W_q, L0_ffn_W_k, L0_ffn_W_v, L0_ffn_W_out, L0_ffn_b_out, L0_ffn_temperature):
    import jax
    import jax.numpy as jnp

    def _L0_gnn_ref(x, rots, idx_i, idx_j):
        import jax, jax.numpy as jnp
        import numpy as np
        from itertools import combinations
        NDIM = 256
        BATCH = 8192

        def _build_mat(rots, idx_i, idx_j, ndim):

            def step(mat, t):
                i, j, theta = t
                c = jnp.cos(theta)
                s = jnp.sin(theta)
                ri = mat[i]
                rj = mat[j]
                mat = mat.at[i].set(c * ri - s * rj)
                mat = mat.at[j].set(s * ri + c * rj)
                return (mat, None)
            mat0 = jnp.eye(ndim, dtype=rots.dtype)
            mat, _ = jax.lax.scan(step, mat0, (idx_i, idx_j, rots))
            return mat.T
        m = _build_mat(rots, idx_i, idx_j, x.shape[-1])
        return x @ m

    def _L0_ffn_ref(x, W_fx, b_fx, W_x, b_x, W_slice, b_slice, W_q, W_k, W_v, W_out, b_out, temperature):
        import jax, jax.numpy as jnp
        import numpy as np
        DIM = 256
        H = 8
        D = 64
        G = 64
        INNER = H * D
        SCALE = D ** (-0.5)
        B, N, _ = x.shape
        fx_mid = (x @ W_fx + b_fx).reshape(B, N, H, D).transpose(0, 2, 1, 3)
        x_mid = (x @ W_x + b_x).reshape(B, N, H, D).transpose(0, 2, 1, 3)
        temp = jnp.clip(temperature, 0.1, 5.0)
        slice_weights = jax.nn.softmax((x_mid @ W_slice + b_slice) / temp, axis=-1)
        slice_norm = slice_weights.sum(axis=2)
        slice_token = jnp.einsum('bhnc,bhng->bhgc', fx_mid, slice_weights)
        slice_token = slice_token / (slice_norm[..., None] + 1e-05)
        q = slice_token @ W_q
        k = slice_token @ W_k
        v = slice_token @ W_v
        attn = jax.nn.softmax(jnp.einsum('bhgc,bhkc->bhgk', q, k) * SCALE, axis=-1)
        out_slice = jnp.einsum('bhgk,bhkc->bhgc', attn, v)
        out_x = jnp.einsum('bhgc,bhng->bhnc', out_slice, slice_weights)
        out_x = out_x.transpose(0, 2, 1, 3).reshape(B, N, INNER)
        return out_x @ W_out + b_out
    x = x + _L0_gnn_ref(_layernorm(x, axis=-1), edge_weight, src, dst)
    x = x + _L0_ffn_ref(_layernorm(x, axis=-1)[None], L0_ffn_W_fx, L0_ffn_b_fx, L0_ffn_W_x, L0_ffn_b_x, L0_ffn_W_slice, L0_ffn_b_slice, L0_ffn_W_q, L0_ffn_W_k, L0_ffn_W_v, L0_ffn_W_out, L0_ffn_b_out, L0_ffn_temperature)[0]
    return x

_drawn_inputs = setup_inputs


def setup_inputs(seed=0):
    import zlib

    import numpy as np

    out = dict(_drawn_inputs(seed))
    spreads = {'L0_ffn_b_fx': (0.0, 0.1),
     'L0_ffn_b_x': (0.0, 0.8),
     'L0_ffn_b_slice': (0.0, 0.8),
     'L0_ffn_b_out': (0.0, 0.1),
     'L0_ffn_temperature': (0.5, 0.6)}
    factors = {'L0_ffn_W_fx': 4.582,
     'L0_ffn_W_x': 8.0,
     'L0_ffn_W_slice': 8.0,
     'L0_ffn_W_q': 8.0,
     'L0_ffn_W_k': 8.0}
    for name, (base, spread) in spreads.items():
        noise = np.random.default_rng([zlib.crc32(name.encode()), seed]).standard_normal(out[name].shape)
        drawn = base * np.exp(spread * noise) if base else spread * noise
        out[name] = jnp.asarray(drawn.astype(out[name].dtype))
    for name, factor in factors.items():
        out[name] = (out[name] * factor).astype(out[name].dtype)
    return out
```

```python
from contextlib import ExitStack

import concourse.bass as bass
from concourse import mybir

F32 = mybir.dt.float32
I32 = mybir.dt.int32
BF16 = mybir.dt.bfloat16
ALU = mybir.AluOpType
ACT = mybir.ActivationFunctionType
AX = mybir.AxisListType

P = 128
ROUND = 1.5 * 2.0 ** 23
TWO_PI = 6.283185307179586
PI_LOW = 3.1415925
TWO_PI_A, TWO_PI_B = 6.28125, 0.0019350051879882812
TWO_PI_C = TWO_PI - TWO_PI_A - TWO_PI_B
EPS = 1e-5


class Chain:

    def __init__(self, engine, sem):
        self.engine, self.sem, self.n, self.turn, self.per = engine, sem, 0, None, 0

    def loop(self, turn, per):
        self.base, self.turn, self.per, self.n = self.n, turn, per, 0

    def link(self, instruction):
        self.n += 1
        instruction.then_inc(self.sem, 1)
        at = self.n if self.turn is None else self.turn * self.per + (self.base + self.n)
        self.engine.wait_ge(self.sem, at)

    def close(self, turns):
        self.n, self.turn = self.base + self.per * turns, None


def divisor(n):
    return max(k for k in range(1, P + 1) if n % k == 0)


def build(nc, x, src, dst, theta, w_fx, b_fx, w_x, b_x, w_slice, b_slice, w_q, w_k, w_v, w_out, b_out,
          temperature, out, debug=None):
    N, D = x.shape
    EDGES = src.shape[0]
    INNER = w_fx.shape[1]
    G = w_slice.shape[0]
    H = INNER // G
    K2 = D // P
    PAIRS = INNER // P
    ROWS = divisor(EDGES)
    STEPS = EDGES // ROWS
    TERMS = 2 * STEPS
    TABLE = ROWS * TERMS
    TP = divisor(N)
    NT = N // TP
    GB = 4
    OVERLAP = P - 1
    LEVELS = 7
    GROUP_RANKS = GB * OVERLAP
    MAX_GROUPS = (TABLE - 1) // GROUP_RANKS + 1
    SHIFTS = (TERMS - 1).bit_length()

    with ExitStack() as whole:
        def keep(name, shape, dt=F32):
            return whole.enter_context(nc.sbuf_tensor(name, shape, dt))

        x_sb = keep("x_sb", [TP, NT, D])
        iota_row = keep("iota_row", [P, D])
        pcol = keep("pcol", [P, 1])
        ident = keep("ident", [P, P])
        mat_t = keep("mat_t", [P, K2, D])

        d_table = nc.dram_tensor("d_table", [TABLE, 1], I32, kind="Internal")
        term_table = nc.dram_tensor("term_table", [TABLE, 4], F32, kind="Internal")

        with ExitStack() as rot:
            def keep2(name, shape, dt=F32):
                return rot.enter_context(nc.sbuf_tensor(name, shape, dt))

            ident_bf = keep2("ident_bf", [P, P], BF16)
            strict = keep2("strict", [P, P])
            neg_sub = keep2("neg_sub", [P, P])
            level_mask = keep2("level_mask", [P, LEVELS, P])
            first_mask = keep2("first_mask", [P, 1])
            second_mask = keep2("second_mask", [P, 1])
            rank = keep2("rank", [P, GB])
            row_start = keep2("row_start", [P, ROWS + 1])
            row_gap = keep2("row_gap", [P, ROWS + 1])
            groups_i = keep2("groups_i", [1, 1], I32)

            edges_phase(nc, locals())
            rotations_phase(nc, locals())
        ffn(nc, locals())


def edges_phase(nc, v):
    P_, ROWS, STEPS, TERMS, TABLE = P, v["ROWS"], v["STEPS"], v["TERMS"], v["TABLE"]
    D, LEVELS, SHIFTS = v["D"], v["LEVELS"], v["SHIFTS"]
    GB, OVERLAP, TP, NT = v["GB"], v["OVERLAP"], v["TP"], v["NT"]
    x, src, dst, theta = v["x"], v["src"], v["dst"], v["theta"]
    x_sb, iota_row, pcol, ident = v["x_sb"], v["iota_row"], v["pcol"], v["ident"]
    ident_bf, strict, neg_sub, level_mask = v["ident_bf"], v["strict"], v["neg_sub"], v["level_mask"]
    first_mask, second_mask, rank = v["first_mask"], v["second_mask"], v["rank"]
    row_start, row_gap, groups_i = v["row_start"], v["row_gap"], v["groups_i"]
    d_table, term_table = v["d_table"], v["term_table"]

    with ExitStack() as ctx:
        def sb(name, shape, dt=F32):
            return ctx.enter_context(nc.sbuf_tensor(name, shape, dt))

        def sem(name):
            return ctx.enter_context(nc.semaphore(name))

        src_i = sb("src_i", [ROWS, STEPS], I32)
        dst_i = sb("dst_i", [ROWS, STEPS], I32)
        th = sb("th", [ROWS, STEPS])
        src_f = sb("src_f", [ROWS, STEPS])
        dst_f = sb("dst_f", [ROWS, STEPS])
        turns = sb("turns", [ROWS, STEPS])
        sine = sb("sine", [ROWS, STEPS])
        half_sine = sb("half_sine", [ROWS, STEPS])
        valid = sb("valid", [ROWS, STEPS, 2])
        record = sb("record", [ROWS, STEPS, 2, 4])
        count = sb("count", [ROWS, TERMS])
        place = sb("place", [ROWS, TERMS])
        shift_d = sb("shift_d", [ROWS, TERMS], I32)
        moved = sb("moved", [ROWS, TERMS], I32)
        row_i = sb("row_i", [P, P], I32)
        col_i = sb("col_i", [P, P], I32)
        pcol_i = sb("pcol_i", [P, 1], I32)
        at_least = sb("at_least", [P, LEVELS, P])
        is_last = sb("is_last", [P, 1])
        is_first = sb("is_first", [P, 1])
        before = sb("before", [P, ROWS + 1])
        follows = sb("follows", [P, ROWS + 1])
        total_bc = sb("total_bc", [ROWS, P])
        groups_f = sb("groups_f", [1, 1])
        offsets_ps = ctx.enter_context(nc.psum_tensor("offsets_ps", [P, 512], F32))
        counts_ps = ctx.enter_context(nc.psum_tensor("counts_ps", [P, 512], F32))

        indices_loaded, angles_loaded, x_loaded = sem("indices_loaded"), sem("angles_loaded"), sem("x_loaded")
        iotas, dve_chain, reduced, sines = sem("iotas"), sem("dve_chain_1"), sem("reduced"), sem("sines")
        totals_ready, offsets_ready = sem("totals_ready"), sem("offsets_ready")
        shifts_ready, records_ready, stored = sem("shifts_ready"), sem("records_ready"), sem("stored")
        block = ctx.enter_context(nc.Block())

        @block.sync
        def _(sp):
            sp.dma_start(src_i[:, :], src.rearrange("(p f) -> p f", p=ROWS)).then_inc(indices_loaded, 16)
            sp.dma_start(dst_i[:, :], dst.rearrange("(p f) -> p f", p=ROWS)).then_inc(indices_loaded, 16)
            sp.dma_start(th[:, :], theta.rearrange("(p f) -> p f", p=ROWS)).then_inc(angles_loaded, 16)
            sp.dma_start(x_sb[:, :, :], x.rearrange("(t p) d -> p t d", p=TP)).then_inc(x_loaded, 16)
            sp.wait_ge(records_ready, 1)
            sp.dma_start(term_table.rearrange("(p f) c -> p (f c)", p=ROWS),
                         record[:, :, :, :].rearrange("p s t c -> p (s t c)")).then_inc(stored, 16)
            sp.wait_ge(shifts_ready, 1)
            sp.dma_start(d_table.rearrange("(p f) c -> p (f c)", p=ROWS), shift_d[:, :]).then_inc(stored, 16)
            sp.wait_ge(stored, 32)
            sp.wait_ge(x_loaded, 16)

        @block.gpsimd
        def _(pool):
            pool.iota(row_i[:, :], [[1, P]], base=0, channel_multiplier=0).then_inc(iotas, 1)
            pool.iota(col_i[:, :], [[0, P]], base=0, channel_multiplier=1).then_inc(iotas, 1)
            pool.iota(pcol_i[:, :], [[1, 1]], base=0, channel_multiplier=1).then_inc(iotas, 1)
            pool.iota(iota_row[:, :], [[1, D]], base=0, channel_multiplier=0,
                      allow_small_or_imprecise_dtypes=True).then_inc(iotas, 1)
            pool.iota(rank[:, :], [[OVERLAP, GB]], base=0, channel_multiplier=1,
                      allow_small_or_imprecise_dtypes=True).then_inc(iotas, 1)
            pool.iota(place[:, :], [[1, TERMS]], base=1, channel_multiplier=0,
                      allow_small_or_imprecise_dtypes=True).then_inc(iotas, 1)

        @block.vector
        def _(dve):
            link = Chain(dve, dve_chain).link
            dve.wait_ge(iotas, 6)
            link(dve.tensor_copy(pcol[:, :], pcol_i[:, :]))
            link(dve.tensor_scalar(ident[:, :], iota_row[:, 0:P], pcol[:, 0:1], None, ALU.is_equal))
            dve.tensor_copy(ident_bf[:, :], ident[:, :])
            dve.tensor_scalar(is_last[:, :], pcol[:, :], float(P - 1), None, ALU.is_equal)
            dve.tensor_scalar(is_first[:, :], pcol[:, :], 0.0, None, ALU.is_equal)
            dve.tensor_scalar(first_mask[:, :], pcol[:, :], float(P - 1), None, ALU.is_lt)
            dve.tensor_scalar(before[:, :], iota_row[:, 0:ROWS + 1], pcol[:, 0:1], None, ALU.is_gt)
            link(dve.tensor_scalar(strict[:, :], iota_row[:, 0:P], pcol[:, 0:1], None, ALU.is_lt))
            dve.tensor_tensor(second_mask[:, :], is_last[:, :], is_first[:, :], ALU.subtract)
            dve.tensor_scalar(follows[:, :], iota_row[:, 0:ROWS + 1], 1.0, pcol[:, 0:1], ALU.subtract,
                              ALU.is_equal)
            link(dve.tensor_scalar(neg_sub[:, :], iota_row[:, 0:P], 1.0, pcol[:, 0:1], ALU.add, ALU.is_equal))
            link(dve.tensor_scalar(neg_sub[:, :], neg_sub[:, :], -1.0, None, ALU.mult))
            link(dve.tensor_tensor(row_i[:, :], row_i[:, :], col_i[:, :], ALU.bitwise_xor))
            for level in range(LEVELS):
                last = dve.scalar_tensor_tensor(at_least[:, level, :], row_i[:, :], float(2 ** level),
                                                strict[:, :], ALU.is_ge, ALU.mult)
            link(last)
            dve.tensor_tensor(level_mask[:, 0:LEVELS - 1, :], at_least[:, 0:LEVELS - 1, :],
                              at_least[:, 1:LEVELS, :], ALU.subtract)
            dve.tensor_copy(level_mask[:, LEVELS - 1, :], at_least[:, LEVELS - 1, :])

            dve.wait_ge(indices_loaded, 32)
            dve.tensor_copy(src_f[:, :], src_i[:, :])
            link(dve.tensor_copy(dst_f[:, :], dst_i[:, :]))
            dve.tensor_tensor(turns[:, :], src_f[:, :], dst_f[:, :], ALU.not_equal)
            link(dve.tensor_scalar(valid[:, :, 1], dst_f[:, :], float(D), None, ALU.is_lt))
            link(dve.scalar_tensor_tensor(valid[:, :, 0], src_f[:, :], float(D), turns[:, :],
                                          ALU.is_lt, ALU.mult))
            flat_valid = valid[:, :, :].rearrange("p s t -> p (s t)")
            link(dve.tensor_tensor_scan(count[:, :], flat_valid, flat_valid, 0.0, ALU.add, ALU.max))
            link(dve.tensor_copy(total_bc[:, :], count[:, TERMS - 1:TERMS].to_broadcast([ROWS, P])))
            dve.tensor_copy(follows[:, :], follows[:, :]).then_inc(totals_ready, 1)
            link(dve.tensor_tensor(count[:, :], place[:, :], count[:, :], ALU.subtract))
            link(dve.tensor_tensor(shift_d[:, :], count[:, :], flat_valid, ALU.mult))

            dve.wait_ge(angles_loaded, 16)
            link(dve.tensor_scalar(turns[:, :], th[:, :], 1.0 / TWO_PI, ROUND, ALU.mult, ALU.add))
            link(dve.tensor_scalar(turns[:, :], turns[:, :], ROUND, None, ALU.subtract))
            for part in (TWO_PI_A, TWO_PI_B, TWO_PI_C):
                link(dve.scalar_tensor_tensor(th[:, :], turns[:, :], -part, th[:, :], ALU.mult, ALU.add))
            dve.tensor_scalar(th[:, :], th[:, :], PI_LOW, -PI_LOW, ALU.min, ALU.max).then_inc(reduced, 1)

            link(dve.tensor_scalar(src_f[:, :], src_f[:, :], float(D - 1), None, ALU.min))
            link(dve.tensor_scalar(dst_f[:, :], dst_f[:, :], float(D - 1), None, ALU.min))
            dve.tensor_copy(record[:, :, 0, 0], src_f[:, :])
            dve.tensor_copy(record[:, :, 0, 1], dst_f[:, :])
            dve.tensor_copy(record[:, :, 1, 1], src_f[:, :])
            link(dve.scalar_tensor_tensor(record[:, :, 1, 0], valid[:, :, 0], float(D), dst_f[:, :],
                                          ALU.mult, ALU.add))

            def shift(level):
                by = 2 ** level
                link(dve.tensor_scalar(moved[:, :], shift_d[:, :], by, None, ALU.bitwise_and))
                link(dve.scalar_tensor_tensor(moved[:, :], moved[:, :], 0.0, shift_d[:, :],
                                              ALU.is_gt, ALU.mult))
                link(dve.tensor_tensor(shift_d[:, :], shift_d[:, :], moved[:, :], ALU.subtract))
                return dve.tensor_tensor(shift_d[:, 0:TERMS - by], shift_d[:, 0:TERMS - by],
                                         moved[:, by:TERMS], ALU.max)

            link(shift(0))
            dve.wait_ge(sines, 2)
            dve.tensor_scalar(record[:, :, 0, 3], sine[:, :], -1.0, None, ALU.mult)
            dve.tensor_copy(record[:, :, 1, 3], sine[:, :])
            link(dve.tensor_scalar(turns[:, :], half_sine[:, :], -2.0, None, ALU.mult))
            link(dve.tensor_tensor(record[:, :, 0, 2], turns[:, :], half_sine[:, :], ALU.mult))
            dve.tensor_copy(record[:, :, 1, 2], record[:, :, 0, 2]).then_inc(records_ready, 1)
            for level in range(1, SHIFTS):
                step = shift(level)
                if level < SHIFTS - 1:
                    link(step)
            step.then_inc(shifts_ready, 1)

            dve.wait_ge(offsets_ready, 1)
            dve.tensor_copy(row_start[:, :], offsets_ps[:, 0:ROWS + 1])
            dve.tensor_scalar(row_gap[:, :], counts_ps[:, 0:ROWS + 1], -1.0, float(TERMS), ALU.mult, ALU.add)
            link(dve.tensor_scalar(groups_f[:, :], offsets_ps[0:1, ROWS:ROWS + 1], 1.0, 0.5,
                                   ALU.max, ALU.subtract))
            link(dve.tensor_scalar(groups_f[:, :], groups_f[:, :], 1.0 / (GB * OVERLAP), 0.5,
                                   ALU.mult, ALU.subtract))
            link(dve.tensor_scalar(groups_f[:, :], groups_f[:, :], ROUND, None, ALU.add))
            link(dve.tensor_scalar(groups_i[:, :], groups_f[:, :], ROUND, 1.0, ALU.subtract, ALU.add))

        @block.scalar
        def _(act):
            act.wait_ge(reduced, 1)
            act.activation(sine[:, :], th[:, :], ACT.Sin).then_inc(sines, 1)
            act.activation(half_sine[:, :], th[:, :], ACT.Sin, scale=0.5).then_inc(sines, 1)

        @block.tensor
        def _(pe):
            pe.wait_ge(totals_ready, 1)
            pe.matmul(offsets_ps[:, 0:ROWS + 1], total_bc[:, :], before[0:ROWS, :], start=True, stop=True)
            pe.matmul(counts_ps[:, 0:ROWS + 1], total_bc[:, :], follows[0:ROWS, :], start=True,
                      stop=True).then_inc(offsets_ready, 1)


def rotations_phase(nc, v):
    D, GB, K2, ROWS, LEVELS, OVERLAP = v["D"], v["GB"], v["K2"], v["ROWS"], v["LEVELS"], v["OVERLAP"]
    TABLE, MAX_GROUPS, GROUP_RANKS = v["TABLE"], v["MAX_GROUPS"], v["GROUP_RANKS"]
    iota_row, pcol, ident, mat_t = v["iota_row"], v["pcol"], v["ident"], v["mat_t"]
    ident_bf, strict, neg_sub, level_mask = v["ident_bf"], v["strict"], v["neg_sub"], v["level_mask"]
    first_mask, second_mask, rank = v["first_mask"], v["second_mask"], v["rank"]
    row_start, row_gap, groups_i = v["row_start"], v["row_gap"], v["groups_i"]
    d_table, term_table = v["d_table"], v["term_table"]
    UP = LEVELS - 1
    APPLY = 4
    assert APPLY == GB

    with ExitStack() as ctx:
        def sb(name, shape, dt=F32):
            return ctx.enter_context(nc.sbuf_tensor(name, shape, dt))

        def ps(name, shape):
            return ctx.enter_context(nc.psum_tensor(name, shape, F32))

        def sem(name):
            return ctx.enter_context(nc.semaphore(name))

        index_f = sb("index_f", [P, GB])
        index_i = sb("index_i", [P, GB], I32)
        gathered_d = sb("gathered_d", [P, GB], I32)
        term_i = sb("term_i", [P, GB], I32)
        raw = sb("raw", [P, GB, 4])
        look = sb("look", [P, ROWS - 1])
        look_sum = sb("look_sum", [P, GB])
        second = sb("second", [P, GB])
        target = sb("target", [P, GB])
        other = sb("other", [P, GB])
        active = sb("active", [P, GB])
        present = sb("present", [P, GB])
        coef = sb("coef", [P, GB, 2])
        target_bc = sb("target_bc", [P, GB, P], BF16)
        vt = sb("vt", [P, GB, D])
        vt_other = sb("vt_other", [P, GB, D])
        lower = sb("lower", [P, GB, P])
        lower_b = sb("lower_b", [P, GB, P])
        lower_mask = sb("lower_mask", [P, GB, P])
        lower_level = sb("lower_level", [P, LEVELS, GB, P])
        t_sb = sb("t_sb", [P, GB, P])
        s_sb = sb("s_sb", [P, GB, P])
        y_sb = sb("y_sb", [P, GB, P])
        rt_sb = sb("rt_sb", [P, K2, GB, P])
        u_sb = sb("u_sb", [P, GB, D])
        w_sb = sb("w_sb", [P, D])
        m_sb = sb("m_sb", [P, K2, D])

        target_ps = ps("target_ps", [P, GB, P])
        y_ps = ps("y_ps", [P, GB, P])
        s_ps = ps("s_ps", [P, GB, P])
        t_ps = ps("t_ps", [P, GB, P])
        rt_ps = [ps(f"rt_ps{h}", [P, GB, P]) for h in range(K2)]
        w_ps = ps("w_ps", [P, 2, D])
        m_ps = ps("m_ps", [P, K2, D])

        chain = sem("dve_chain_2")
        index_ready, d_gathered = sem("index_ready"), sem("d_gathered")
        term_ready, raw_gathered = sem("term_ready"), sem("raw_gathered")
        decoded, target_bc_ready, targets_done = sem("decoded"), sem("target_bc_ready"), sem("targets_done")
        vt_ready, lower_ready, masked = sem("vt_ready"), sem("lower_ready"), sem("masked")
        t0_ready, y_done, s_done, t_done = sem("t0_ready"), sem("y_done"), sem("s_done"), sem("t_done")
        y_copied, s_copied, t_copied = sem("y_copied"), sem("s_copied"), sem("t_copied")
        rt_done, rt_copied, u_ready = sem("rt_done"), sem("rt_copied"), sem("u_ready")
        w_done, w_copied, m_done, m_copied = sem("w_done"), sem("w_copied"), sem("m_done"), sem("m_copied")
        start_ready, mt_done, gathers_begun = sem("start_ready"), sem("mt_done"), sem("gathers_begun")
        block = ctx.enter_context(nc.Block())

        def groups(engine):
            return engine.value_load(groups_i[0:1, 0:1], min_val=1, max_val=MAX_GROUPS)

        @block.gpsimd
        def _(pool):
            def gather_d():
                pool.sem_inc(gathers_begun, 1)
                for b in range(GB):
                    pool.indirect_dma_start(
                        out=gathered_d[:, b:b + 1], out_offset=None, in_=d_table[:, :],
                        in_offset=bass.IndirectOffsetOnAxis(ap=index_i[:, b:b + 1], axis=0)
                    ).then_inc(d_gathered, 16)

            def gather_terms():
                pool.sem_inc(gathers_begun, 1)
                for b in range(GB):
                    pool.indirect_dma_start(
                        out=raw[:, b, :], out_offset=None, in_=term_table[:, :],
                        in_offset=bass.IndirectOffsetOnAxis(ap=term_i[:, b:b + 1], axis=0)
                    ).then_inc(raw_gathered, 16)

            n = groups(pool)
            pool.wait_ge(index_ready, 1)
            gather_d()
            pool.wait_ge(term_ready, 1)
            gather_terms()
            with pool.Fori(0, n) as i:
                pool.wait_ge(index_ready, i + 2)
                gather_d()
                pool.wait_ge(lower_ready, i + 1)
                for level in range(1, LEVELS):
                    pool.tensor_tensor(lower_level[:, level, :, :], lower[:, :, :],
                                       level_mask[:, level, :].unsqueeze(1).to_broadcast([P, GB, P]),
                                       ALU.mult).then_inc(masked, 1)
                pool.wait_ge(term_ready, i + 2)
                gather_terms()
            pool.wait_ge(raw_gathered, n * (16 * GB) + 16 * GB)

        @block.vector
        def _(dve):
            c = Chain(dve, chain)
            link = c.link

            def find_index():
                for b in range(GB):
                    last = dve.scalar_tensor_tensor(look[:, :], row_start[:, 1:ROWS], rank[:, b:b + 1],
                                                    row_gap[:, 1:ROWS], ALU.is_le, ALU.mult,
                                                    accum_out=look_sum[:, b:b + 1])
                    link(last)
                link(dve.tensor_tensor(index_f[:, :], look_sum[:, :], rank[:, :], ALU.add))
                link(dve.tensor_scalar(index_f[:, :], index_f[:, :], float(TABLE - 1), None, ALU.min))
                dve.tensor_copy(index_i[:, :], index_f[:, :]).then_inc(index_ready, 1)

            def find_term(turn):
                dve.wait_ge(d_gathered, turn * (16 * GB) + 16 * GB)
                dve.tensor_tensor(term_i[:, :], index_f[:, :], gathered_d[:, :],
                                  ALU.add).then_inc(term_ready, 1)

            n = groups(dve)
            dve.memset(u_sb[:, :, :], 0.0)
            dve.memset(rt_sb[:, :, :, :], 0.0)
            for h in range(K2):
                last = dve.tensor_scalar(m_sb[:, h, :], iota_row[:, :], float(-h * P), pcol[:, 0:1],
                                         ALU.add, ALU.is_equal)
            last.then_inc(start_ready, 1)
            find_index()
            find_term(0)
            with dve.Fori(0, n) as i:
                c.loop(i, 15)
                dve.wait_ge(raw_gathered, i * (16 * GB) + 16 * GB)
                dve.tensor_scalar(present[:, :], rank[:, :], row_start[:, ROWS:ROWS + 1], None, ALU.is_lt)
                dve.tensor_copy(other[:, :], raw[:, :, 1])
                link(dve.tensor_scalar(second[:, :], raw[:, :, 0], float(D), None, ALU.is_ge))
                link(dve.tensor_scalar(active[:, :], second[:, :], second_mask[:, 0:1], first_mask[:, 0:1],
                                       ALU.mult, ALU.add))
                link(dve.tensor_tensor(active[:, :], active[:, :], present[:, :], ALU.mult))
                link(dve.tensor_tensor(coef[:, :, :], raw[:, :, 2:4],
                                       active[:, :].unsqueeze(2).to_broadcast([P, GB, 2]), ALU.mult))
                dve.scalar_tensor_tensor(target[:, :], second[:, :], float(-D), raw[:, :, 0],
                                         ALU.mult, ALU.add).then_inc(decoded, 1)
                dve.wait_ge(decoded, i + 1)
                link(dve.tensor_scalar(rank[:, :], rank[:, :], float(GROUP_RANKS), None, ALU.add))
                find_index()
                dve.wait_ge(rt_done, i + 1)
                for b in range(GB):
                    dve.tensor_scalar(vt_other[:, b, :], iota_row[:, :], other[:, b:b + 1],
                                      coef[:, b, 1:2], ALU.is_equal, ALU.mult)
                    last = dve.tensor_scalar(vt[:, b, :], iota_row[:, :], target[:, b:b + 1],
                                             coef[:, b, 0:1], ALU.is_equal, ALU.mult)
                link(last)
                dve.tensor_tensor(vt[:, :, :], vt[:, :, :], vt_other[:, :, :], ALU.add).then_inc(vt_ready, 1)
                dve.wait_ge(targets_done, i + 1)
                for b in range(GB):
                    dve.tensor_scalar(lower[:, b, :], target_ps[:, b, :], target[:, b:b + 1],
                                      coef[:, b, 0:1], ALU.is_equal, ALU.mult)
                    dve.tensor_scalar(lower_b[:, b, :], target_ps[:, b, :], other[:, b:b + 1],
                                      coef[:, b, 1:2], ALU.is_equal, ALU.mult)
                    last = dve.scalar_tensor_tensor(lower_mask[:, b, :], neg_sub[:, :], second[:, b:b + 1],
                                                    strict[:, :], ALU.mult, ALU.add)
                link(last)
                link(dve.tensor_tensor(lower[:, :, :], lower[:, :, :], lower_b[:, :, :], ALU.add))
                dve.tensor_tensor(lower[:, :, :], lower[:, :, :], lower_mask[:, :, :],
                                  ALU.mult).then_inc(lower_ready, 1)
                dve.wait_ge(lower_ready, i + 1)
                link(dve.tensor_tensor(t_sb[:, :, :], lower[:, :, :],
                                       level_mask[:, 0, :].unsqueeze(1).to_broadcast([P, GB, P]), ALU.mult))
                dve.tensor_tensor(t_sb[:, :, :], t_sb[:, :, :],
                                  ident[:, :].unsqueeze(1).to_broadcast([P, GB, P]),
                                  ALU.add).then_inc(t0_ready, 1)
                find_term(i + 1)
                for level in range(LEVELS):
                    dve.wait_ge(s_done, i * LEVELS + (level + 1))
                    dve.tensor_copy(s_sb[:, :, :], s_ps[:, :, :]).then_inc(s_copied, 1)
                    if 1 <= level <= APPLY:
                        dve.wait_ge(m_done, i * GB + level)
                        dve.tensor_copy(m_sb[:, :, :], m_ps[:, :, :]).then_inc(m_copied, 1)
                for b in range(GB):
                    last = dve.tensor_scalar(u_sb[:, b, :], iota_row[:, :], target[:, b:b + 1], None,
                                             ALU.is_equal)
                last.then_inc(u_ready, 1)
                assert c.n == c.per, c.n
            for b in range(GB):
                dve.wait_ge(m_done, n * GB + (b + 1))
                dve.tensor_copy(m_sb[:, :, :], m_ps[:, :, :]).then_inc(m_copied, 1)
            dve.wait_ge(mt_done, 1)
            dve.tensor_copy(mat_t[:, :, :], w_ps[:, :, :])

        @block.scalar
        def _(act):
            n = groups(act)
            with act.Fori(0, n) as i:
                act.wait_ge(decoded, i + 1)
                act.activation(target_bc[:, :, :], target[:, :].unsqueeze(2).to_broadcast([P, GB, P]),
                               ACT.Copy).then_inc(target_bc_ready, 1)
                for level in range(1, LEVELS):
                    act.wait_ge(y_done, i * UP + level)
                    act.activation(y_sb[:, :, :], y_ps[:, :, :], ACT.Copy).then_inc(y_copied, 1)
                    if level <= APPLY:
                        act.wait_ge(w_done, i * GB + level)
                        act.activation(w_sb[:, :], w_ps[:, level % 2, :], ACT.Copy).then_inc(w_copied, 1)
                    if level < UP:
                        act.wait_ge(t_done, i * (UP - 1) + level)
                        act.activation(t_sb[:, :, :], t_ps[:, :, :], ACT.Copy).then_inc(t_copied, 1)
                act.wait_ge(rt_done, i + 2)
                for h in range(K2):
                    last = act.activation(rt_sb[:, h, :, :], rt_ps[h][:, :, :], ACT.Copy)
                last.then_inc(rt_copied, 1)
            for b in range(GB):
                act.wait_ge(w_done, n * GB + (b + 1))
                act.activation(w_sb[:, :], w_ps[:, (b + 1) % 2, :], ACT.Copy).then_inc(w_copied, 1)

        @block.tensor
        def _(pe):
            def apply_read(turn, b):
                if b > 0:
                    pe.wait_ge(m_copied, turn * GB + b)
                for h in range(K2):
                    last = pe.matmul(w_ps[:, (b + 1) % 2, :], rt_sb[:, h, b, :], m_sb[:, h, :],
                                     start=(h == 0), stop=(h == K2 - 1))
                last.then_inc(w_done, 1)

            def apply_write(turn, b):
                pe.wait_ge(w_copied, turn * GB + (b + 1))
                for h in range(K2):
                    last = pe.matmul(m_ps[:, h, :], u_sb[:, b, h * P:(h + 1) * P], w_sb[:, :],
                                     start=False, stop=True, skip_group_check=True)
                last.then_inc(m_done, 1)

            n = groups(pe)
            pe.wait_ge(start_ready, 1)
            pe.matmul(m_ps[:, :, :], ident[:, :], m_sb[:, :, :], start=True, stop=True).then_inc(rt_done, 1)
            with pe.Fori(0, n) as i:
                pe.wait_ge(target_bc_ready, i + 1)
                for b in range(GB):
                    last = pe.matmul(target_ps[:, b, :], target_bc[:, b, :], ident_bf[:, :],
                                     start=True, stop=True)
                last.then_inc(targets_done, 1)
                pe.wait_ge(t0_ready, i + 1)
                for b in range(GB):
                    last = pe.matmul(s_ps[:, b, :], t_sb[:, b, :], ident[:, :], start=(b == 0), stop=True,
                                     skip_group_check=True)
                last.then_inc(s_done, 1)
                for b in range(GB):
                    pe.matmul(t_ps[:, b, :], ident[:, :], t_sb[:, b, :], start=(b == 0), stop=True,
                              skip_group_check=True)
                for level in range(1, LEVELS):
                    pe.wait_ge(masked, i * UP + level)
                    pe.wait_ge(s_copied, i * LEVELS + level)
                    for b in range(GB):
                        last = pe.matmul(y_ps[:, b, :], lower_level[:, level, b, :], s_sb[:, b, :],
                                         start=True, stop=True)
                    last.then_inc(y_done, 1)
                    if level <= APPLY:
                        apply_read(i, level - 1)
                    pe.wait_ge(y_copied, i * UP + level)
                    if level > 1:
                        pe.wait_ge(t_copied, i * (UP - 1) + (level - 1))
                    for b in range(GB):
                        last = pe.matmul(s_ps[:, b, :], t_sb[:, b, :], y_sb[:, b, :], start=False, stop=True,
                                         skip_group_check=True)
                    last.then_inc(s_done, 1)
                    if level < UP:
                        for b in range(GB):
                            last = pe.matmul(t_ps[:, b, :], y_sb[:, b, :], t_sb[:, b, :], start=False,
                                             stop=True, skip_group_check=True)
                        last.then_inc(t_done, 1)
                    if level <= APPLY:
                        apply_write(i, level - 1)
                pe.wait_ge(s_copied, i * LEVELS + LEVELS)
                pe.wait_ge(vt_ready, i + 1)
                for h in range(K2):
                    for b in range(GB):
                        last = pe.matmul(rt_ps[h][:, b, :], vt[:, b, h * P:(h + 1) * P], s_sb[:, b, :],
                                         start=True, stop=True)
                last.then_inc(rt_done, 1)
                pe.wait_ge(rt_copied, i + 1)
                pe.wait_ge(u_ready, i + 1)
                pe.wait_ge(m_copied, i * GB + GB)
            for b in range(GB):
                apply_read(n, b)
                apply_write(n, b)
            pe.wait_ge(m_copied, n * GB + GB)
            for h in range(K2):
                for g in range(K2):
                    last = pe.transpose(w_ps[:, g, h * P:(h + 1) * P], m_sb[:, h, g * P:(g + 1) * P],
                                        ident[:, :])
            last.then_inc(mt_done, 1)


def ffn(nc, v):
    N, D, INNER, G, H = v["N"], v["D"], v["INNER"], v["G"], v["H"]
    K2, PAIRS, TP, NT = v["K2"], v["PAIRS"], v["TP"], v["NT"]
    x_sb, iota_row, pcol, ident, mat_t = v["x_sb"], v["iota_row"], v["pcol"], v["ident"], v["mat_t"]
    with ExitStack() as ctx:
        def keep(name, shape, dt=F32):
            return ctx.enter_context(nc.sbuf_tensor(name, shape, dt))

        v = dict(v)
        v["wt_sb"] = keep("wt_sb", [P, NT, PAIRS, TP])
        v["wxs"] = keep("wxs", [P, K2, INNER])
        v["bias_row"] = keep("bias_row", [1, INNER])
        v["bias_bc"] = keep("bias_bc", [P, INNER])
        v["wfx_sb"] = keep("wfx_sb", [P, K2, INNER])
        v["bfx_bc"] = keep("bfx_bc", [P, INNER])
        v["wout_sb"] = keep("wout_sb", [P, PAIRS, D])
        v["bout_bc"] = keep("bout_bc", [P, D])
        v["pair_w"] = keep("pair_w", [P, 3, P])
        v["z_sb"] = keep("z_sb", [P, PAIRS, D + 1])
        v["q_sb"] = keep("q_sb", [P, PAIRS, D])
        v["mean"] = keep("mean", [TP, NT])
        v["rstd"] = keep("rstd", [TP, NT])
        v["eps_col"] = keep("eps_col", [P, 1])
        v["ones_row"] = keep("ones_row", [1, P])
        weights_phase(nc, v)
        rotate_phase(nc, v)
        tokens_phase(nc, v)
        slices_phase(nc, v)
        output_phase(nc, v)


def weights_phase(nc, v):
    D, INNER, G, H, K2, PAIRS, TP, NT = (v[k] for k in ("D", "INNER", "G", "H", "K2", "PAIRS", "TP", "NT"))
    ident, x_sb = v["ident"], v["x_sb"]
    wxs, bias_row, bias_bc = v["wxs"], v["bias_row"], v["bias_bc"]
    with ExitStack() as ctx:
        def sb(name, shape, dt=F32):
            return ctx.enter_context(nc.sbuf_tensor(name, shape, dt))

        def sem(name):
            return ctx.enter_context(nc.semaphore(name))

        wx_sb = sb("wx_sb", [P, K2, INNER])
        wxt_sb = sb("wxt_sb", [P, PAIRS, D])
        pair_slice = sb("pair_slice", [P, P])
        bx_col = sb("bx_col", [P, PAIRS])
        bs_row = sb("bs_row", [1, G])
        temp_row = sb("temp_row", [1, H])
        temp_inv = sb("temp_inv", [1, INNER])
        temp_inv_bc = sb("temp_inv_bc", [P, INNER])
        turn_ps = ctx.enter_context(nc.psum_tensor("turn_ps", [P, 2, 2, D], F32))
        wxs_ps = [ctx.enter_context(nc.psum_tensor(f"wxs_ps{k}", [P, INNER], F32)) for k in range(K2)]
        brow_ps = ctx.enter_context(nc.psum_tensor("brow_ps", [1, INNER], F32))
        tbc_ps = ctx.enter_context(nc.psum_tensor("tbc_ps", [P, INNER], F32))
        bbc_ps = ctx.enter_context(nc.psum_tensor("bbc_ps", [P, INNER], F32))
        loaded, zeroed, chain = sem("loaded"), sem("zeroed"), sem("dve_chain_w")
        turned, turned_copied, temp_ready, temp_bc = (sem("turned"), sem("turned_copied"), sem("temp_ready"),
                                                      sem("temp_bc"))
        products, bias_ready, bias_spread = sem("products"), sem("bias_ready"), sem("bias_spread")
        block = ctx.enter_context(nc.Block())
        pair_w = v["pair_w"]

        def row(a):
            return a.rearrange("(a n) -> a n", a=1)

        @block.sync
        def _(sp):
            n = 0
            loads = [(wx_sb[:, :, :], v["w_x"].rearrange("(k p) n -> p k n", p=P)),
                     (v["wfx_sb"][:, :, :], v["w_fx"].rearrange("(k p) n -> p k n", p=P)),
                     (v["wout_sb"][:, :, :], v["w_out"].rearrange("(k p) n -> p k n", p=P)),
                     (bx_col[:, :], v["b_x"].rearrange("(k p) -> p k", p=P)),
                     (bs_row[:, :], row(v["b_slice"])),
                     (temp_row[:, :], v["temperature"].rearrange("a h b c -> a (h b c)")),
                     (v["bfx_bc"][:, :], row(v["b_fx"]).to_broadcast([P, INNER])),
                     (v["bout_bc"][:, :], row(v["b_out"]).to_broadcast([P, D]))]
            for to, of in loads:
                sp.dma_start(to, of, allow_slow_non_contiguous=True).then_inc(loaded, 16)
            sp.wait_ge(zeroed, 1)
            for half in range(2):
                at = slice(half * G, (half + 1) * G)
                sp.dma_start(pair_slice[at, at], v["w_slice"]).then_inc(loaded, 16)
                for m, w in enumerate(("w_q", "w_k", "w_v")):
                    sp.dma_start(pair_w[at, m, at], v[w]).then_inc(loaded, 16)
            sp.wait_ge(loaded, 16 * 16)

        @block.gpsimd
        def _(pool):
            pool.memset(pair_w[:, :, :], 0.0)
            pool.memset(v["eps_col"][:, :], EPS)
            pool.memset(v["ones_row"][:, :], 1.0)
            pool.memset(pair_slice[:, :], 0.0).then_inc(zeroed, 1)

        @block.vector
        def _(dve):
            link = Chain(dve, chain).link
            dve.wait_ge(loaded, 16 * 16)
            link(dve.tensor_scalar(temp_row[:, :], temp_row[:, :], 0.1, 5.0, ALU.max, ALU.min))
            link(dve.reciprocal(temp_row[:, :], temp_row[:, :]))
            dve.tensor_copy(temp_inv[:, :].rearrange("a (h g) -> a h g", g=G),
                            temp_row[:, :].unsqueeze(2).to_broadcast([1, H, G])).then_inc(temp_ready, 1)
            for k in range(K2):
                dve.wait_ge(turned, k + 1)
                for half in range(2):
                    last = dve.tensor_copy(wxt_sb[:, 2 * half:2 * half + 2, k * P:(k + 1) * P],
                                           turn_ps[:, k, :, half * P:(half + 1) * P])
                last.then_inc(turned_copied, 1)
            dve.wait_ge(temp_bc, 1)
            link(dve.tensor_copy(temp_inv_bc[:, :], tbc_ps[:, :]))
            dve.wait_ge(products, 1)
            for k in range(K2):
                dve.tensor_tensor(wxs[:, k, :], wxs_ps[k][:, :], temp_inv_bc[:, :], ALU.mult)
            link(dve.tensor_tensor(bias_row[:, :].rearrange("a (h g) -> a h g", g=G),
                                   brow_ps[:, :].rearrange("a (h g) -> a h g", g=G),
                                   bs_row[:, :].unsqueeze(1).to_broadcast([1, H, G]), ALU.add))
            dve.tensor_tensor(bias_row[:, :], bias_row[:, :], temp_inv[:, :], ALU.mult).then_inc(bias_ready, 1)
            dve.wait_ge(bias_spread, 1)
            dve.tensor_copy(bias_bc[:, :], bbc_ps[:, :])

        @block.tensor
        def _(pe):
            pe.wait_ge(loaded, 16 * 16)
            for k in range(K2):
                for pair in range(PAIRS):
                    last = pe.transpose(turn_ps[:, k, pair % 2, (pair // 2) * P:(pair // 2 + 1) * P],
                                        wx_sb[:, k, pair * P:(pair + 1) * P], ident[:, :])
                last.then_inc(turned, 1)
            pe.wait_ge(temp_ready, 1)
            pe.matmul(tbc_ps[:, :], v["ones_row"][:, :], temp_inv[:, :], start=True, stop=True).then_inc(temp_bc, 1)
            pe.wait_ge(turned_copied, K2)
            for pair in range(PAIRS):
                at = slice(pair * P, (pair + 1) * P)
                for k in range(K2):
                    pe.matmul(wxs_ps[k][:, at], wxt_sb[:, pair, k * P:(k + 1) * P], pair_slice[:, :],
                              start=True, stop=True)
                last = pe.matmul(brow_ps[:, at], bx_col[:, pair:pair + 1], pair_slice[:, :], start=True, stop=True)
            last.then_inc(products, 1)
            pe.wait_ge(bias_ready, 1)
            pe.matmul(bbc_ps[:, :], v["ones_row"][:, :], bias_row[:, :], start=True, stop=True).then_inc(bias_spread, 1)


def rotate_phase(nc, v):
    D, K2, TP, NT = (v[k] for k in ("D", "K2", "TP", "NT"))
    x_sb, ident, mat_t, eps_col = v["x_sb"], v["ident"], v["mat_t"], v["eps_col"]
    mean, rstd, bout_bc = v["mean"], v["rstd"], v["bout_bc"]
    with ExitStack() as ctx:
        def sb(name, shape, dt=F32):
            return ctx.enter_context(nc.sbuf_tensor(name, shape, dt))

        def sem(name):
            return ctx.enter_context(nc.semaphore(name))

        stats = sb("stats1", [TP, 2, 6])
        both = sb("both1", [TP, 2, 2])
        mean1, rstd1 = sb("mean1", [TP, NT]), sb("rstd1", [TP, NT])
        normed = sb("normed1", [TP, 2, D])
        normed_t = sb("normed_t1", [P, 2, K2, TP])
        turn_ps = [ctx.enter_context(nc.psum_tensor(f"turn1_ps{j}", [P, 512], F32)) for j in range(2)]
        y_ps = [ctx.enter_context(nc.psum_tensor(f"rotated_ps{j}", [TP, D], F32)) for j in range(2)]
        chain, stats_done, rooted = sem("dve_chain_r"), sem("stats_done"), sem("rooted")
        normed_ready, turned, turned_copied, rotated = (sem("normed_ready"), sem("turned_r"),
                                                        sem("turned_copied_r"), sem("rotated"))
        stats2_done, rooted2 = sem("stats2_done"), sem("rooted2")
        started = sem("started")
        block = ctx.enter_context(nc.Block())

        @block.vector
        def _(dve):
            c = Chain(dve, chain)
            link = c.link

            def row_numbers(j, source):
                dve.sem_inc(started, 1)
                link(dve.bn_stats(stats[:, j, :], source))
                dve.sem_inc(started, 1)
                link(dve.bn_aggr(both[:, j, :], stats[:, j, :]))

            with dve.Fori(0, NT // 2) as turn:
                t = turn * 2
                c.loop(turn, 5)
                for j in range(2):
                    row_numbers(j, x_sb[:, t + j, :])
                dve.tensor_copy(mean1[:, bass.ds(t, 2)], both[:, :, 0])
                link(dve.tensor_copy(rstd1[:, bass.ds(t, 2)], both[:, :, 1]))
                assert c.n == 5
            c.close(NT // 2)
            link(dve.tensor_scalar(rstd1[:, :], rstd1[:, :], EPS, None, ALU.add))
            dve.tensor_copy(mean1[:, :], mean1[:, :]).then_inc(stats_done, 1)
            dve.wait_ge(rooted, 1)
            link(dve.reciprocal(rstd1[:, :], rstd1[:, :]))
            with dve.Fori(0, NT // 2) as turn:
                t = turn * 2
                c.loop(turn, 7)
                for j in range(2):
                    dve.tensor_scalar(normed[:, j, :], x_sb[:, t + j, :], mean1[:, bass.ds(t + j, 1)],
                                      rstd1[:, bass.ds(t + j, 1)], ALU.subtract,
                                      ALU.mult).then_inc(normed_ready, 1)
                for j in range(2):
                    dve.wait_ge(rotated, t + (j + 1))
                    link(dve.tensor_tensor(x_sb[:, t + j, :], x_sb[:, t + j, :], y_ps[j][:, :], ALU.add))
                    row_numbers(j, x_sb[:, t + j, :])
                dve.tensor_copy(mean[:, bass.ds(t, 2)], both[:, :, 0])
                link(dve.tensor_copy(rstd[:, bass.ds(t, 2)], both[:, :, 1]))
                assert c.n == 7
            c.close(NT // 2)
            link(dve.tensor_scalar(rstd[:, :], rstd[:, :], EPS, None, ALU.add))
            dve.tensor_copy(mean[:, :], mean[:, :]).then_inc(stats2_done, 1)
            dve.wait_ge(rooted2, 1)
            dve.reciprocal(rstd[:, :], rstd[:, :])

        @block.scalar
        def _(act):
            act.wait_ge(stats_done, 1)
            act.activation(rstd1[:, :], rstd1[:, :], ACT.Sqrt).then_inc(rooted, 1)
            with act.Fori(0, NT // 2) as turn:
                t = turn * 2
                for j in range(2):
                    act.wait_ge(turned, t + (j + 1))
                    act.activation(normed_t[:, j, :, :].rearrange("p k n -> p (k n)"), turn_ps[j][:, 0:K2 * TP],
                                   ACT.Copy).then_inc(turned_copied, 1)
            act.wait_ge(stats2_done, 1)
            act.activation(rstd[:, :], rstd[:, :], ACT.Sqrt).then_inc(rooted2, 1)

        @block.tensor
        def _(pe):
            with pe.Fori(0, NT // 2) as turn:
                t = turn * 2
                for j in range(2):
                    pe.wait_ge(normed_ready, t + (j + 1))
                    for k in range(K2):
                        last = pe.transpose(turn_ps[j][:, k * TP:(k + 1) * TP], normed[:, j, k * P:(k + 1) * P],
                                            ident[0:TP, 0:TP])
                    last.then_inc(turned, 1)
                for j in range(2):
                    pe.wait_ge(turned_copied, t + (j + 1))
                    for k in range(K2):
                        last = pe.matmul(y_ps[j][:, :], normed_t[:, j, k, :], mat_t[:, k, :], start=(k == 0),
                                         stop=(k == K2 - 1))
                    last.then_inc(rotated, 1)


def tokens_phase(nc, v):
    D, INNER, G, H, K2, PAIRS, TP, NT = (v[k] for k in ("D", "INNER", "G", "H", "K2", "PAIRS", "TP", "NT"))
    x_sb, ident, mean, rstd, bout_bc = v["x_sb"], v["ident"], v["mean"], v["rstd"], v["bout_bc"]
    wxs, bias_bc, wt_sb, z_sb = v["wxs"], v["bias_bc"], v["wt_sb"], v["z_sb"]
    with ExitStack() as ctx:
        def sb(name, shape, dt=F32):
            return ctx.enter_context(nc.sbuf_tensor(name, shape, dt))

        def sem(name):
            return ctx.enter_context(nc.semaphore(name))

        normed = sb("normed2", [TP, 2, D + 1])
        normed_t = sb("normed_t2", [P, 2, K2, TP])
        logits = sb("logits", [TP, 2, INNER])
        weights = sb("weights", [TP, 2, INNER])
        top = sb("top", [TP, 2, H])
        total = sb("total", [TP, 2, H])
        zeros = sb("zeros", [1, D + 1])
        xt_ps = ctx.enter_context(nc.psum_tensor("xt_ps", [P, 512], F32))
        wt_ps = ctx.enter_context(nc.psum_tensor("wt_ps", [P, 512], F32))
        logit_ps = [ctx.enter_context(nc.psum_tensor(f"logit_ps{j}", [TP, INNER], F32)) for j in range(2)]
        z_ps = [ctx.enter_context(nc.psum_tensor(f"z_ps{k}", [P, 512], F32)) for k in range(PAIRS)]
        chain, zeroed = sem("dve_chain_t"), sem("zeroed_t")
        normed_ready, turned, turned_copied = sem("normed2_ready"), sem("turned_t"), sem("turned_copied_t")
        scored, shifted, exps, weights_ready = sem("scored"), sem("shifted"), sem("exps"), sem("weights_ready")
        summed, weights_turned, weights_kept = sem("summed"), sem("weights_turned"), sem("weights_kept")
        block = ctx.enter_context(nc.Block())

        def heads(a):
            return a.rearrange("p (h g) -> p h g", g=G)

        @block.vector
        def _(dve):
            c = Chain(dve, chain)
            link = c.link
            dve.memset(zeros[:, :], 0.0)
            dve.memset(normed[:, :, D:D + 1], 1.0).then_inc(zeroed, 1)
            with dve.Fori(0, NT // 2) as turn:
                t = turn * 2
                c.loop(turn, 8)
                for j in range(2):
                    dve.wait_ge(summed, t + (j + 1))
                    dve.tensor_scalar(normed[:, j, 0:D], x_sb[:, t + j, :], mean[:, bass.ds(t + j, 1)],
                                      rstd[:, bass.ds(t + j, 1)], ALU.subtract,
                                      ALU.mult).then_inc(normed_ready, 1)
                for j in range(2):
                    dve.wait_ge(scored, t + (j + 1))
                    link(dve.tensor_tensor(logits[:, j, :], logit_ps[j][:, :], bias_bc[0:TP, :], ALU.add))
                    link(dve.tensor_reduce(top[:, j, :], heads(logits[:, j, :]), AX.X, ALU.max))
                    dve.tensor_tensor(heads(logits[:, j, :]), heads(logits[:, j, :]),
                                      top[:, j, :].unsqueeze(2).to_broadcast([TP, H, G]),
                                      ALU.subtract).then_inc(shifted, 1)
                for j in range(2):
                    dve.wait_ge(exps, t + (j + 1))
                    link(dve.tensor_reduce(total[:, j, :], heads(logits[:, j, :]), AX.X, ALU.add))
                    link(dve.reciprocal(total[:, j, :], total[:, j, :]))
                    dve.tensor_tensor(heads(weights[:, j, :]), heads(logits[:, j, :]),
                                      total[:, j, :].unsqueeze(2).to_broadcast([TP, H, G]),
                                      ALU.mult).then_inc(weights_ready, 1)
                assert c.n == 8
            dve.wait_ge(summed, NT + 2)
            for k in range(PAIRS):
                dve.tensor_copy(z_sb[:, k, :], z_ps[k][:, 0:D + 1])

        @block.scalar
        def _(act):
            with act.Fori(0, NT // 2) as turn:
                t = turn * 2
                for j in range(2):
                    act.wait_ge(turned, t + (j + 1))
                    act.activation(normed_t[:, j, :, :].rearrange("p k n -> p (k n)"), xt_ps[:, 0:K2 * TP],
                                   ACT.Copy).then_inc(turned_copied, 1)
                for j in range(2):
                    act.wait_ge(shifted, t + (j + 1))
                    act.activation(logits[:, j, :], logits[:, j, :], ACT.Exp).then_inc(exps, 1)
                for j in range(2):
                    act.wait_ge(weights_turned, t + (j + 1))
                    act.activation(wt_sb[:, t + j, :, :].rearrange("p k n -> p (k n)"), wt_ps[:, 0:PAIRS * TP],
                                   ACT.Copy).then_inc(weights_kept, 1)

        @block.tensor
        def _(pe):
            pe.wait_ge(zeroed, 1)
            for k in range(PAIRS):
                last = pe.matmul(z_ps[k][:, 0:D + 1], zeros[:, 0:P], zeros[:, :], start=True, stop=True)
            last.then_inc(summed, 2)
            with pe.Fori(0, NT // 2) as turn:
                t = turn * 2
                for j in range(2):
                    pe.wait_ge(normed_ready, t + (j + 1))
                    if j == 1:
                        pe.wait_ge(turned_copied, t + 1)
                    for k in range(K2):
                        last = pe.transpose(xt_ps[:, k * TP:(k + 1) * TP], normed[:, j, k * P:(k + 1) * P],
                                            ident[0:TP, 0:TP])
                    last.then_inc(turned, 1)
                for j in range(2):
                    pe.wait_ge(turned_copied, t + (j + 1))
                    for k in range(K2):
                        last = pe.matmul(logit_ps[j][:, :], normed_t[:, j, k, :], wxs[:, k, :], start=(k == 0),
                                         stop=(k == K2 - 1))
                    last.then_inc(scored, 1)
                for j in range(2):
                    pe.wait_ge(weights_ready, t + (j + 1))
                    if j == 1:
                        pe.wait_ge(weights_kept, t + 1)
                    for k in range(PAIRS):
                        last = pe.transpose(wt_ps[:, k * TP:(k + 1) * TP], weights[:, j, k * P:(k + 1) * P],
                                            ident[0:TP, 0:TP])
                    last.then_inc(weights_turned, 1)
                    for k in range(PAIRS):
                        last = pe.matmul(z_ps[k][:, 0:D + 1], weights[:, j, k * P:(k + 1) * P], normed[:, j, :],
                                         start=False, stop=True, skip_group_check=True)
                    last.then_inc(summed, 1)
                pe.wait_ge(weights_kept, t + 2)


def slices_phase(nc, v):
    D, INNER, G, H, K2, PAIRS = (v[k] for k in ("D", "INNER", "G", "H", "K2", "PAIRS"))
    z_sb, wfx_sb, bfx_bc, wout_sb, q_sb = v["z_sb"], v["wfx_sb"], v["bfx_bc"], v["wout_sb"], v["q_sb"]
    pair_w, ident = v["pair_w"], v["ident"]
    SCALE = G ** -0.5
    with ExitStack() as ctx:
        def sb(name, shape, dt=F32):
            return ctx.enter_context(nc.sbuf_tensor(name, shape, dt))

        def sem(name):
            return ctx.enter_context(nc.semaphore(name))

        zt_sb = sb("zt_sb", [P, K2, PAIRS, P])
        token = sb("token", [P, PAIRS, P])
        norm_inv = sb("norm_inv", [P, PAIRS])
        token_t = sb("token_t", [P, PAIRS, P])
        query_t, key_t, value = sb("query_t", [P, PAIRS, P]), sb("key_t", [P, PAIRS, P]), sb("value", [P, PAIRS, P])
        score = sb("score", [P, PAIRS, G])
        top, total = sb("top_s", [P, PAIRS]), sb("total_s", [P, PAIRS])
        attn, attn_t = sb("attn", [P, PAIRS, P]), sb("attn_t", [P, PAIRS, P])
        mixed_t = sb("mixed_t", [P, PAIRS, P])
        ps = [ctx.enter_context(nc.psum_tensor(f"slice_ps{k}", [P, PAIRS, P], F32)) for k in range(8)]
        chain, pe_done, act_done, ready = sem("dve_chain_s"), sem("pe_done"), sem("act_done"), sem("ready")
        block = ctx.enter_context(nc.Block())
        HALVES = [slice(0, G), slice(G, 2 * G)]

        @block.vector
        def _(dve):
            link = Chain(dve, chain).link
            dve.memset(attn[:, :, :], 0.0)
            link(dve.memset(token[:, :, :], 0.0))
            link(dve.tensor_scalar(norm_inv[:, :], z_sb[:, :, D], 1e-5, None, ALU.add))
            link(dve.reciprocal(norm_inv[:, :], norm_inv[:, :]))
            dve.wait_ge(pe_done, 1)
            for k in range(K2):
                last = dve.tensor_copy(zt_sb[:, k, :, :], ps[k][:, :, :])
            last.then_inc(ready, 1)
            dve.wait_ge(pe_done, 2)
            for pair in range(PAIRS):
                for n, at in enumerate(HALVES):
                    cols = slice(pair * P + n * G, pair * P + (n + 1) * G)
                    last = dve.scalar_tensor_tensor(token[at, pair, at], bfx_bc[at, cols],
                                                    z_sb[at, pair, D:D + 1], ps[2][at, pair, at],
                                                    ALU.mult, ALU.add)
            link(last)
            dve.tensor_tensor(token[:, :, :], token[:, :, :],
                              norm_inv[:, :].unsqueeze(2).to_broadcast([P, PAIRS, P]),
                              ALU.mult).then_inc(ready, 1)
            dve.wait_ge(pe_done, 3)
            dve.tensor_copy(token_t[:, :, :], ps[3][:, :, :]).then_inc(ready, 1)
            dve.wait_ge(pe_done, 4)
            dve.tensor_copy(query_t[:, :, :], ps[4][:, :, :])
            dve.tensor_copy(key_t[:, :, :], ps[5][:, :, :])
            dve.tensor_copy(value[:, :, :], ps[6][:, :, :]).then_inc(ready, 1)
            dve.wait_ge(pe_done, 5)
            for at in HALVES:
                last = dve.tensor_scalar(score[at, :, :], ps[7][at, :, at], SCALE, None, ALU.mult)
            link(last)
            link(dve.tensor_reduce(top[:, :], score[:, :, :], AX.X, ALU.max))
            dve.tensor_tensor(score[:, :, :], score[:, :, :], top[:, :].unsqueeze(2).to_broadcast([P, PAIRS, G]),
                              ALU.subtract).then_inc(ready, 1)
            dve.wait_ge(act_done, 1)
            link(dve.tensor_reduce(total[:, :], score[:, :, :], AX.X, ALU.add))
            link(dve.reciprocal(total[:, :], total[:, :]))
            for at in HALVES:
                last = dve.tensor_tensor(attn[at, :, at], score[at, :, :],
                                         total[at, :].unsqueeze(2).to_broadcast([G, PAIRS, G]), ALU.mult)
            last.then_inc(ready, 1)
            dve.wait_ge(pe_done, 6)
            dve.tensor_copy(attn_t[:, :, :], ps[0][:, :, :]).then_inc(ready, 1)
            dve.wait_ge(pe_done, 7)
            dve.tensor_copy(mixed_t[:, :, :], ps[1][:, :, :]).then_inc(ready, 1)
            dve.wait_ge(pe_done, 8)
            for pair in range(PAIRS):
                dve.tensor_copy(q_sb[:, pair, :],
                                ps[2 + pair // 2][:, :, :].rearrange("p a b -> p (a b)")
                                [:, (pair % 2) * D:(pair % 2 + 1) * D])

        @block.scalar
        def _(act):
            act.wait_ge(ready, 5)
            act.activation(score[:, :, :], score[:, :, :], ACT.Exp).then_inc(act_done, 1)

        @block.tensor
        def _(pe):
            for k in range(K2):
                for pair in range(PAIRS):
                    last = pe.transpose(ps[k][:, pair, :], z_sb[:, pair, k * P:(k + 1) * P], ident[:, :])
            last.then_inc(pe_done, 1)
            pe.wait_ge(ready, 1)
            for pair in range(PAIRS):
                for k in range(K2):
                    last = pe.matmul(ps[2][:, pair, :], zt_sb[:, k, pair, :], wfx_sb[:, k, pair * P:(pair + 1) * P],
                                     start=(k == 0), stop=(k == K2 - 1))
            last.then_inc(pe_done, 1)
            pe.wait_ge(ready, 2)
            for pair in range(PAIRS):
                last = pe.transpose(ps[3][:, pair, :], token[:, pair, :], ident[:, :])
            last.then_inc(pe_done, 1)
            pe.wait_ge(ready, 3)
            for pair in range(PAIRS):
                pe.matmul(ps[4][:, pair, :], pair_w[:, 0, :], token_t[:, pair, :], start=True, stop=True)
                pe.matmul(ps[5][:, pair, :], pair_w[:, 1, :], token_t[:, pair, :], start=True, stop=True)
                last = pe.matmul(ps[6][:, pair, :], token_t[:, pair, :], pair_w[:, 2, :], start=True, stop=True)
            last.then_inc(pe_done, 1)
            pe.wait_ge(ready, 4)
            for pair in range(PAIRS):
                last = pe.matmul(ps[7][:, pair, :], query_t[:, pair, :], key_t[:, pair, :], start=True, stop=True)
            last.then_inc(pe_done, 1)
            pe.wait_ge(ready, 6)
            for pair in range(PAIRS):
                last = pe.transpose(ps[0][:, pair, :], attn[:, pair, :], ident[:, :])
            last.then_inc(pe_done, 1)
            pe.wait_ge(ready, 7)
            for pair in range(PAIRS):
                last = pe.matmul(ps[1][:, pair, :], value[:, pair, :], attn_t[:, pair, :], start=True, stop=True)
            last.then_inc(pe_done, 1)
            pe.wait_ge(ready, 8)
            for pair in range(PAIRS):
                out = ps[2 + pair // 2][:, :, :].rearrange("p a b -> p (a b)")
                last = pe.matmul(out[:, (pair % 2) * D:(pair % 2 + 1) * D], mixed_t[:, pair, :],
                                 wout_sb[:, pair, :], start=True, stop=True)
            last.then_inc(pe_done, 1)


def output_phase(nc, v):
    D, K2, PAIRS, TP, NT = (v[k] for k in ("D", "K2", "PAIRS", "TP", "NT"))
    x_sb, wt_sb, q_sb, bout_bc, out = v["x_sb"], v["wt_sb"], v["q_sb"], v["bout_bc"], v["out"]
    with ExitStack() as ctx:
        def sb(name, shape, dt=F32):
            return ctx.enter_context(nc.sbuf_tensor(name, shape, dt))

        def sem(name):
            return ctx.enter_context(nc.semaphore(name))

        here = sb("here", [P, 2, PAIRS, TP])
        done = sb("done", [TP, 2, D])
        sum_ps = [ctx.enter_context(nc.psum_tensor(f"sum_ps{j}", [TP, D], F32)) for j in range(2)]
        here_ready, mixed, biased, done_ready = sem("here_ready"), sem("mixed"), sem("biased"), sem("done_ready")
        stored = [sem(f"out_stored{j}") for j in range(2)]
        block = ctx.enter_context(nc.Block())

        @block.scalar
        def _(act):
            with act.Fori(0, NT // 2) as turn:
                t = turn * 2
                for j in range(2):
                    act.wait_ge(mixed, t + (j + 1))
                    act.activation(here[:, j, :, :], wt_sb[:, t + j, :, :], ACT.Copy).then_inc(here_ready, 1)

        @block.gpsimd
        def _(pool):
            with pool.Fori(0, NT // 2) as turn:
                t = turn * 2
                for j in range(2):
                    pool.tensor_tensor(x_sb[:, t + j, :], x_sb[:, t + j, :], bout_bc[0:TP, :],
                                       ALU.add).then_inc(biased, 1)

        @block.tensor
        def _(pe):
            pe.nop().then_inc(mixed, 2)
            with pe.Fori(0, NT // 2) as turn:
                t = turn * 2
                for j in range(2):
                    pe.wait_ge(here_ready, t + (j + 1))
                    pe.wait_ge(done_ready, t + (j + 1))
                    for k in range(PAIRS):
                        last = pe.matmul(sum_ps[j][:, :], here[:, j, k, :], q_sb[:, k, :], start=(k == 0),
                                         stop=(k == PAIRS - 1))
                    last.then_inc(mixed, 1)

        @block.vector
        def _(dve):
            dve.nop().then_inc(done_ready, 2)
            with dve.Fori(0, NT // 2) as turn:
                t = turn * 2
                for j in range(2):
                    dve.wait_ge(mixed, t + (j + 3))
                    dve.wait_ge(biased, t + (j + 1))
                    dve.wait_ge(stored[j], t * 8 + 16)
                    dve.tensor_tensor(done[:, j, :], sum_ps[j][:, :], x_sb[:, t + j, :],
                                      ALU.add).then_inc(done_ready, 1)

        @block.sync
        def _(sp):
            for j in range(2):
                sp.nop().then_inc(stored[j], 16)
            with sp.Fori(0, NT // 2) as turn:
                t = turn * 2
                for j in range(2):
                    sp.wait_ge(done_ready, t + (j + 3))
                    sp.dma_start(out[bass.ds(t * TP + j * TP, TP), :], done[:, j, :]).then_inc(stored[j], 16)
            for j in range(2):
                sp.wait_ge(stored[j], 16 * (NT // 2) + 16)


_INS = ["x", "src", "dst", "edge_weight", "L0_ffn_W_fx", "L0_ffn_b_fx", "L0_ffn_W_x", "L0_ffn_b_x",
        "L0_ffn_W_slice", "L0_ffn_b_slice", "L0_ffn_W_q", "L0_ffn_W_k", "L0_ffn_W_v", "L0_ffn_W_out",
        "L0_ffn_b_out", "L0_ffn_temperature"]


def kernel(**inputs):
    import numpy as np
    import concourse.bacc as bacc
    from concourse.bass_utils import run_bass_kernel_spmd

    nc = bacc.Bacc("TRN2", target_bir_lowering=False, num_devices=1)
    arrays, args = {}, []
    for name in _INS:
        a = np.ascontiguousarray(inputs[name])
        arrays["in_" + name] = a
        args.append(nc.dram_tensor("in_" + name, a.shape, mybir.dt.from_np(a.dtype), kind="ExternalInput").ap())
    out = nc.dram_tensor("out_x", inputs["x"].shape, F32, kind="ExternalOutput").ap()
    build(nc, *args, out)
    r = run_bass_kernel_spmd(nc, [arrays], core_ids=[0])
    return r.results[0]["out_x"]
```

```python
from contextlib import ExitStack

import concourse.bass as bass
from concourse import mybir

F32 = mybir.dt.float32
I32 = mybir.dt.int32
BF16 = mybir.dt.bfloat16
ALU = mybir.AluOpType
ACT = mybir.ActivationFunctionType
AX = mybir.AxisListType

P = 128
ROUND = 1.5 * 2.0 ** 23
TWO_PI = 6.283185307179586
PI_LOW = 3.1415925
TWO_PI_A, TWO_PI_B = 6.28125, 0.0019350051879882812
TWO_PI_C = TWO_PI - TWO_PI_A - TWO_PI_B
EPS = 1e-5


class Chain:

    def __init__(self, engine, sem):
        self.engine, self.sem, self.n, self.turn, self.per = engine, sem, 0, None, 0

    def loop(self, turn, per):
        self.base, self.turn, self.per, self.n = self.n, turn, per, 0

    def link(self, instruction):
        self.n += 1
        instruction.then_inc(self.sem, 1)
        at = self.n if self.turn is None else self.turn * self.per + (self.base + self.n)
        self.engine.wait_ge(self.sem, at)

    def close(self, turns):
        self.n, self.turn = self.base + self.per * turns, None


def divisor(n):
    return max(k for k in range(1, P + 1) if n % k == 0)


def build(nc, x, src, dst, theta, w_fx, b_fx, w_x, b_x, w_slice, b_slice, w_q, w_k, w_v, w_out, b_out,
          temperature, out, debug=None):
    N, D = x.shape
    EDGES = src.shape[0]
    INNER = w_fx.shape[1]
    G = w_slice.shape[0]
    H = INNER // G
    K2 = D // P
    PAIRS = INNER // P
    ROWS = divisor(EDGES)
    STEPS = EDGES // ROWS
    TERMS = 2 * STEPS
    TABLE = ROWS * TERMS
    TP = divisor(N)
    NT = N // TP
    GB = 4
    OVERLAP = P - 1
    LEVELS = 7
    GROUP_RANKS = GB * OVERLAP
    MAX_GROUPS = (TABLE - 1) // GROUP_RANKS + 1
    SHIFTS = (TERMS - 1).bit_length()

    with ExitStack() as whole:
        def keep(name, shape, dt=F32):
            return whole.enter_context(nc.sbuf_tensor(name, shape, dt))

        x_sb = keep("x_sb", [TP, NT, D])
        iota_row = keep("iota_row", [P, D])
        pcol = keep("pcol", [P, 1])
        ident = keep("ident", [P, P])
        mat_t = keep("mat_t", [P, K2, D])
        wxs = keep("wxs", [P, K2, INNER])
        bias_bc = keep("bias_bc", [P, INNER])
        wfx_sb = keep("wfx_sb", [P, K2, INNER])
        bfx_bc = keep("bfx_bc", [P, INNER])
        wout_sb = keep("wout_sb", [P, PAIRS, D])
        bout_bc = keep("bout_bc", [P, D])
        pair_w = keep("pair_w", [P, 3, P])
        ones_row = keep("ones_row", [1, P])
        scale1 = keep("scale1", [TP, NT])
        shift1 = keep("shift1", [TP, NT])
        minus_half = keep("minus_half", [TP, NT])

        d_table = nc.dram_tensor("d_table", [TABLE, 1], I32, kind="Internal")
        term_table = nc.dram_tensor("term_table", [TABLE, 4], F32, kind="Internal")

        with ExitStack() as rot:
            def keep2(name, shape, dt=F32):
                return rot.enter_context(nc.sbuf_tensor(name, shape, dt))

            ident_bf = keep2("ident_bf", [P, P], BF16)
            strict = keep2("strict", [P, P])
            neg_sub = keep2("neg_sub", [P, P])
            level_mask = keep2("level_mask", [P, LEVELS, P])
            first_mask = keep2("first_mask", [P, 1])
            second_mask = keep2("second_mask", [P, 1])
            rank = keep2("rank", [P, GB])
            row_start = keep2("row_start", [P, ROWS + 1])
            row_gap = keep2("row_gap", [P, ROWS + 1])
            groups_i = keep2("groups_i", [1, 1], I32)

            edges_phase(nc, locals())
            rotations_phase(nc, locals())
        with ExitStack() as after:
            def keep3(name, shape, dt=F32):
                return after.enter_context(nc.sbuf_tensor(name, shape, dt))

            wt_sb = keep3("wt_sb", [P, NT, PAIRS, TP])
            z_sb = keep3("z_sb", [P, PAIRS, D])
            norm_sb = keep3("norm_sb", [P, PAIRS])
            tokens_phase(nc, locals())
            q_sb = keep3("q_sb", [P, PAIRS, D])
            slices_phase(nc, locals())
            output_phase(nc, locals())


def edges_phase(nc, v):
    P_, ROWS, STEPS, TERMS, TABLE = P, v["ROWS"], v["STEPS"], v["TERMS"], v["TABLE"]
    D, LEVELS, SHIFTS = v["D"], v["LEVELS"], v["SHIFTS"]
    GB, OVERLAP, TP, NT = v["GB"], v["OVERLAP"], v["TP"], v["NT"]
    x, src, dst, theta = v["x"], v["src"], v["dst"], v["theta"]
    x_sb, iota_row, pcol, ident = v["x_sb"], v["iota_row"], v["pcol"], v["ident"]
    ident_bf, strict, neg_sub, level_mask = v["ident_bf"], v["strict"], v["neg_sub"], v["level_mask"]
    first_mask, second_mask, rank = v["first_mask"], v["second_mask"], v["rank"]
    row_start, row_gap, groups_i = v["row_start"], v["row_gap"], v["groups_i"]
    d_table, term_table = v["d_table"], v["term_table"]
    INNER, G, H, K2, PAIRS = v["INNER"], v["G"], v["H"], v["K2"], v["PAIRS"]
    wxs, bias_bc, pair_w, ones_row = v["wxs"], v["bias_bc"], v["pair_w"], v["ones_row"]
    scale1, shift1, minus_half = v["scale1"], v["shift1"], v["minus_half"]

    with ExitStack() as ctx:
        def sb(name, shape, dt=F32):
            return ctx.enter_context(nc.sbuf_tensor(name, shape, dt))

        def sem(name):
            return ctx.enter_context(nc.semaphore(name))

        src_i = sb("src_i", [ROWS, STEPS], I32)
        dst_i = sb("dst_i", [ROWS, STEPS], I32)
        th = sb("th", [ROWS, STEPS])
        src_f = sb("src_f", [ROWS, STEPS])
        dst_f = sb("dst_f", [ROWS, STEPS])
        turns = sb("turns", [ROWS, STEPS])
        sine = sb("sine", [ROWS, STEPS])
        half_sine = sb("half_sine", [ROWS, STEPS])
        valid = sb("valid", [ROWS, STEPS, 2])
        record = sb("record", [ROWS, STEPS, 2, 4])
        count = sb("count", [ROWS, TERMS])
        place = sb("place", [ROWS, TERMS])
        shift_d = sb("shift_d", [ROWS, TERMS], I32)
        moved = sb("moved", [ROWS, TERMS], I32)
        row_i = sb("row_i", [P, P], I32)
        col_i = sb("col_i", [P, P], I32)
        pcol_i = sb("pcol_i", [P, 1], I32)
        at_least = sb("at_least", [P, LEVELS, P])
        is_last = sb("is_last", [P, 1])
        is_first = sb("is_first", [P, 1])
        before = sb("before", [P, ROWS + 1])
        follows = sb("follows", [P, ROWS + 1])
        total_bc = sb("total_bc", [ROWS, P])
        groups_f = sb("groups_f", [1, 1])
        offsets_ps = ctx.enter_context(nc.psum_tensor("offsets_ps", [P, 512], F32))
        counts_ps = ctx.enter_context(nc.psum_tensor("counts_ps", [P, 512], F32))

        indices_loaded, angles_loaded, x_loaded = sem("indices_loaded"), sem("angles_loaded"), sem("x_loaded")
        iotas, dve_chain, reduced, sines = sem("iotas"), sem("dve_chain_1"), sem("reduced"), sem("sines")
        totals_ready, offsets_ready = sem("totals_ready"), sem("offsets_ready")
        shifts_ready, records_ready, stored = sem("shifts_ready"), sem("records_ready"), sem("stored")

        wx_sb = sb("wx_sb", [P, K2, INNER])
        wxt_sb = sb("wxt_sb", [P, PAIRS, D])
        pair_slice = sb("pair_slice", [P, P])
        bx_col = sb("bx_col", [P, PAIRS])
        bs_row = sb("bs_row", [1, G])
        temp_row = sb("temp_row", [1, H])
        temp_inv = sb("temp_inv", [1, INNER])
        temp_inv_bc = sb("temp_inv_bc", [P, INNER])
        bias_row = sb("bias_row", [1, INNER])
        squares = sb("squares", [TP, D])
        neg_mean = sb("neg_mean", [TP, NT])
        turn_ps = ctx.enter_context(nc.psum_tensor("turn_ps", [P, 2, 2, D], F32))
        wxs_ps = [ctx.enter_context(nc.psum_tensor(f"wxs_ps{k}", [P, INNER], F32)) for k in range(K2)]
        brow_ps = ctx.enter_context(nc.psum_tensor("brow_ps", [1, INNER], F32))
        spread_ps = ctx.enter_context(nc.psum_tensor("spread_ps", [P, INNER], F32))
        loaded, zeroed, ident_ready = sem("loaded"), sem("zeroed"), sem("ident_ready")
        turned, turned_copied, temp_ready, temp_bc = (sem("turned"), sem("turned_copied"), sem("temp_ready"),
                                                      sem("temp_bc"))
        temp_bc_copied, products = sem("temp_bc_copied"), sem("products")
        bias_ready, bias_spread = sem("bias_ready"), sem("bias_spread")
        act_chain, pool_chain = sem("act_chain_1"), sem("pool_chain_1")
        sums_ready, mean_ready, squares_ready = sem("sums_ready"), sem("mean_ready"), sem("squares_ready")
        LOADS = 16
        block = ctx.enter_context(nc.Block())

        def row(a):
            return a.rearrange("(a n) -> a n", a=1)

        @block.sync
        def _(sp):
            sp.dma_start(src_i[:, :], src.rearrange("(p f) -> p f", p=ROWS)).then_inc(indices_loaded, 16)
            sp.dma_start(dst_i[:, :], dst.rearrange("(p f) -> p f", p=ROWS)).then_inc(indices_loaded, 16)
            sp.dma_start(th[:, :], theta.rearrange("(p f) -> p f", p=ROWS)).then_inc(angles_loaded, 16)
            loads = [(wx_sb[:, :, :], v["w_x"].rearrange("(k p) n -> p k n", p=P)),
                     (v["wfx_sb"][:, :, :], v["w_fx"].rearrange("(k p) n -> p k n", p=P)),
                     (v["wout_sb"][:, :, :], v["w_out"].rearrange("(k p) n -> p k n", p=P)),
                     (bx_col[:, :], v["b_x"].rearrange("(k p) -> p k", p=P)),
                     (bs_row[:, :], row(v["b_slice"])),
                     (temp_row[:, :], v["temperature"].rearrange("a h b c -> a (h b c)")),
                     (v["bfx_bc"][:, :], row(v["b_fx"]).to_broadcast([P, INNER])),
                     (v["bout_bc"][:, :], row(v["b_out"]).to_broadcast([P, D]))]
            for to, of in loads:
                sp.dma_start(to, of, allow_slow_non_contiguous=True).then_inc(loaded, 16)
            sp.wait_ge(zeroed, 1)
            for half in range(2):
                at = slice(half * G, (half + 1) * G)
                sp.dma_start(pair_slice[at, at], v["w_slice"]).then_inc(loaded, 16)
                for m, w in enumerate(("w_q", "w_k", "w_v")):
                    sp.dma_start(pair_w[at, m, at], v[w]).then_inc(loaded, 16)
            sp.dma_start(x_sb[:, :, :], x.rearrange("(t p) d -> p t d", p=TP)).then_inc(x_loaded, 16)
            sp.wait_ge(records_ready, 1)
            sp.dma_start(term_table.rearrange("(p f) c -> p (f c)", p=ROWS),
                         record[:, :, :, :].rearrange("p s t c -> p (s t c)")).then_inc(stored, 16)
            sp.wait_ge(shifts_ready, 1)
            sp.dma_start(d_table.rearrange("(p f) c -> p (f c)", p=ROWS), shift_d[:, :]).then_inc(stored, 16)
            sp.wait_ge(stored, 32)
            sp.wait_ge(x_loaded, 16)

        @block.gpsimd
        def _(pool):
            link = Chain(pool, pool_chain).link
            pool.memset(pair_w[:, :, :], 0.0)
            pool.memset(ones_row[:, :], 1.0)
            pool.memset(minus_half[:, :], -0.5)
            link(pool.memset(pair_slice[:, :], 0.0))
            pool.sem_inc(zeroed, 1)
            pool.iota(row_i[:, :], [[1, P]], base=0, channel_multiplier=0).then_inc(iotas, 1)
            pool.iota(col_i[:, :], [[0, P]], base=0, channel_multiplier=1).then_inc(iotas, 1)
            pool.iota(pcol_i[:, :], [[1, 1]], base=0, channel_multiplier=1).then_inc(iotas, 1)
            pool.iota(iota_row[:, :], [[1, D]], base=0, channel_multiplier=0,
                      allow_small_or_imprecise_dtypes=True).then_inc(iotas, 1)
            pool.iota(rank[:, :], [[OVERLAP, GB]], base=0, channel_multiplier=1,
                      allow_small_or_imprecise_dtypes=True).then_inc(iotas, 1)
            pool.iota(place[:, :], [[1, TERMS]], base=1, channel_multiplier=0,
                      allow_small_or_imprecise_dtypes=True).then_inc(iotas, 1)
            pool.wait_ge(sums_ready, 1)
            link(pool.tensor_scalar(neg_mean[:, :], neg_mean[:, :], -1.0 / D, None, ALU.mult))
            pool.sem_inc(mean_ready, 1)
            pool.wait_ge(squares_ready, 1)
            link(pool.tensor_scalar(scale1[:, :], scale1[:, :], 1.0 / D, EPS, ALU.mult, ALU.add))
            link(pool.tensor_tensor(scale1[:, :], scale1[:, :], minus_half[:, :], ALU.pow))
            link(pool.tensor_tensor(shift1[:, :], scale1[:, :], neg_mean[:, :], ALU.mult))

        @block.vector
        def _(dve):
            link = Chain(dve, dve_chain).link
            dve.wait_ge(iotas, 6)
            link(dve.tensor_copy(pcol[:, :], pcol_i[:, :]))
            link(dve.tensor_scalar(ident[:, :], iota_row[:, 0:P], pcol[:, 0:1], None, ALU.is_equal))
            dve.tensor_copy(ident_bf[:, :], ident[:, :]).then_inc(ident_ready, 1)
            dve.tensor_scalar(is_last[:, :], pcol[:, :], float(P - 1), None, ALU.is_equal)
            dve.tensor_scalar(is_first[:, :], pcol[:, :], 0.0, None, ALU.is_equal)
            dve.tensor_scalar(first_mask[:, :], pcol[:, :], float(P - 1), None, ALU.is_lt)
            dve.tensor_scalar(before[:, :], iota_row[:, 0:ROWS + 1], pcol[:, 0:1], None, ALU.is_gt)
            link(dve.tensor_scalar(strict[:, :], iota_row[:, 0:P], pcol[:, 0:1], None, ALU.is_lt))
            dve.tensor_tensor(second_mask[:, :], is_last[:, :], is_first[:, :], ALU.subtract)
            dve.tensor_scalar(follows[:, :], iota_row[:, 0:ROWS + 1], 1.0, pcol[:, 0:1], ALU.subtract,
                              ALU.is_equal)
            link(dve.tensor_scalar(neg_sub[:, :], iota_row[:, 0:P], 1.0, pcol[:, 0:1], ALU.add, ALU.is_equal))
            link(dve.tensor_scalar(neg_sub[:, :], neg_sub[:, :], -1.0, None, ALU.mult))
            link(dve.tensor_tensor(row_i[:, :], row_i[:, :], col_i[:, :], ALU.bitwise_xor))
            for level in range(LEVELS):
                last = dve.scalar_tensor_tensor(at_least[:, level, :], row_i[:, :], float(2 ** level),
                                                strict[:, :], ALU.is_ge, ALU.mult)
            link(last)
            dve.tensor_tensor(level_mask[:, 0:LEVELS - 1, :], at_least[:, 0:LEVELS - 1, :],
                              at_least[:, 1:LEVELS, :], ALU.subtract)
            dve.tensor_copy(level_mask[:, LEVELS - 1, :], at_least[:, LEVELS - 1, :])


            dve.wait_ge(loaded, 16 * LOADS)
            link(dve.tensor_scalar(temp_row[:, :], temp_row[:, :], 0.1, 5.0, ALU.max, ALU.min))
            link(dve.reciprocal(temp_row[:, :], temp_row[:, :]))
            dve.tensor_copy(temp_inv[:, :].rearrange("a (h g) -> a h g", g=G),
                            temp_row[:, :].unsqueeze(2).to_broadcast([1, H, G])).then_inc(temp_ready, 1)

            dve.wait_ge(indices_loaded, 32)
            dve.tensor_copy(src_f[:, :], src_i[:, :])
            link(dve.tensor_copy(dst_f[:, :], dst_i[:, :]))
            dve.tensor_tensor(turns[:, :], src_f[:, :], dst_f[:, :], ALU.not_equal)
            link(dve.tensor_scalar(valid[:, :, 1], dst_f[:, :], float(D), None, ALU.is_lt))
            link(dve.scalar_tensor_tensor(valid[:, :, 0], src_f[:, :], float(D), turns[:, :],
                                          ALU.is_lt, ALU.mult))
            flat_valid = valid[:, :, :].rearrange("p s t -> p (s t)")
            link(dve.tensor_tensor_scan(count[:, :], flat_valid, flat_valid, 0.0, ALU.add, ALU.max))
            link(dve.tensor_copy(total_bc[:, :], count[:, TERMS - 1:TERMS].to_broadcast([ROWS, P])))
            dve.tensor_copy(follows[:, :], follows[:, :]).then_inc(totals_ready, 1)
            link(dve.tensor_tensor(count[:, :], place[:, :], count[:, :], ALU.subtract))
            link(dve.tensor_tensor(shift_d[:, :], count[:, :], flat_valid, ALU.mult))

            dve.wait_ge(angles_loaded, 16)
            link(dve.tensor_scalar(turns[:, :], th[:, :], 1.0 / TWO_PI, ROUND, ALU.mult, ALU.add))
            link(dve.tensor_scalar(turns[:, :], turns[:, :], ROUND, None, ALU.subtract))
            for part in (TWO_PI_A, TWO_PI_B, TWO_PI_C):
                link(dve.scalar_tensor_tensor(th[:, :], turns[:, :], -part, th[:, :], ALU.mult, ALU.add))
            dve.tensor_scalar(th[:, :], th[:, :], PI_LOW, -PI_LOW, ALU.min, ALU.max).then_inc(reduced, 1)

            link(dve.tensor_scalar(src_f[:, :], src_f[:, :], float(D - 1), None, ALU.min))
            link(dve.tensor_scalar(dst_f[:, :], dst_f[:, :], float(D - 1), None, ALU.min))
            dve.tensor_copy(record[:, :, 0, 0], src_f[:, :])
            dve.tensor_copy(record[:, :, 0, 1], dst_f[:, :])
            dve.tensor_copy(record[:, :, 1, 1], src_f[:, :])
            link(dve.scalar_tensor_tensor(record[:, :, 1, 0], valid[:, :, 0], float(D), dst_f[:, :],
                                          ALU.mult, ALU.add))

            dve.wait_ge(products, 1)
            dve.wait_ge(temp_bc_copied, 1)
            for k in range(K2):
                dve.tensor_tensor(wxs[:, k, :], wxs_ps[k][:, :], temp_inv_bc[:, :], ALU.mult)
            link(dve.tensor_tensor(bias_row[:, :].rearrange("a (h g) -> a h g", g=G),
                                   brow_ps[:, :].rearrange("a (h g) -> a h g", g=G),
                                   bs_row[:, :].unsqueeze(1).to_broadcast([1, H, G]), ALU.add))
            dve.tensor_tensor(bias_row[:, :], bias_row[:, :], temp_inv[:, :], ALU.mult).then_inc(bias_ready, 1)

            def shift(level):
                by = 2 ** level
                link(dve.tensor_scalar(moved[:, :], shift_d[:, :], by, None, ALU.bitwise_and))
                link(dve.scalar_tensor_tensor(moved[:, :], moved[:, :], 0.0, shift_d[:, :],
                                              ALU.is_gt, ALU.mult))
                link(dve.tensor_tensor(shift_d[:, :], shift_d[:, :], moved[:, :], ALU.subtract))
                return dve.tensor_tensor(shift_d[:, 0:TERMS - by], shift_d[:, 0:TERMS - by],
                                         moved[:, by:TERMS], ALU.max)

            link(shift(0))
            dve.wait_ge(sines, 2)
            dve.tensor_scalar(record[:, :, 0, 3], sine[:, :], -1.0, None, ALU.mult)
            dve.tensor_copy(record[:, :, 1, 3], sine[:, :])
            link(dve.tensor_scalar(turns[:, :], half_sine[:, :], -2.0, None, ALU.mult))
            link(dve.tensor_tensor(record[:, :, 0, 2], turns[:, :], half_sine[:, :], ALU.mult))
            dve.tensor_copy(record[:, :, 1, 2], record[:, :, 0, 2]).then_inc(records_ready, 1)
            for level in range(1, SHIFTS):
                step = shift(level)
                if level < SHIFTS - 1:
                    link(step)
            step.then_inc(shifts_ready, 1)

            dve.wait_ge(bias_spread, 1)
            dve.tensor_copy(bias_bc[:, :], spread_ps[:, :])
            dve.wait_ge(offsets_ready, 1)
            dve.tensor_copy(row_start[:, :], offsets_ps[:, 0:ROWS + 1])
            dve.tensor_scalar(row_gap[:, :], counts_ps[:, 0:ROWS + 1], -1.0, float(TERMS), ALU.mult, ALU.add)
            link(dve.tensor_scalar(groups_f[:, :], offsets_ps[0:1, ROWS:ROWS + 1], 1.0, 0.5,
                                   ALU.max, ALU.subtract))
            link(dve.tensor_scalar(groups_f[:, :], groups_f[:, :], 1.0 / (GB * OVERLAP), 0.5,
                                   ALU.mult, ALU.subtract))
            link(dve.tensor_scalar(groups_f[:, :], groups_f[:, :], ROUND, None, ALU.add))
            link(dve.tensor_scalar(groups_i[:, :], groups_f[:, :], ROUND, 1.0, ALU.subtract, ALU.add))

        @block.scalar
        def _(act):
            act.wait_ge(turned, K2)
            act.activation(wxt_sb[:, :, :], turn_ps[:, :, :, :].rearrange("p a b d -> p (a b) d"), ACT.Copy).then_inc(turned_copied, 1)
            act.wait_ge(temp_bc, 1)
            act.activation(temp_inv_bc[:, :], spread_ps[:, :], ACT.Copy).then_inc(temp_bc_copied, 1)
            c = Chain(act, act_chain)
            act.wait_ge(reduced, 1)
            act.activation(sine[:, :], th[:, :], ACT.Sin).then_inc(sines, 1)
            act.activation(half_sine[:, :], th[:, :], ACT.Sin, scale=0.5).then_inc(sines, 1)
            act.wait_ge(x_loaded, 16)
            with act.Fori(0, NT) as t:
                c.loop(t, 1)
                c.link(act.activation(squares[:, :], x_sb[:, t, :], ACT.Copy,
                                      accum_out=neg_mean[:, bass.ds(t, 1)]))
            c.close(NT)
            act.sem_inc(sums_ready, 1)
            act.wait_ge(mean_ready, 1)
            with act.Fori(0, NT) as t:
                c.loop(t, 1)
                c.link(act.activation(squares[:, :], x_sb[:, t, :], ACT.Square, bias=neg_mean[:, bass.ds(t, 1)],
                                      accum_out=scale1[:, bass.ds(t, 1)]))
            act.sem_inc(squares_ready, 1)

        @block.tensor
        def _(pe):
            pe.wait_ge(ident_ready, 1)
            pe.wait_ge(loaded, 16 * LOADS)
            for k in range(K2):
                for pair in range(PAIRS):
                    last = pe.transpose(turn_ps[:, pair // 2, pair % 2, k * P:(k + 1) * P],
                                        wx_sb[:, k, pair * P:(pair + 1) * P], ident[:, :])
                last.then_inc(turned, 1)
            pe.wait_ge(temp_ready, 1)
            pe.matmul(spread_ps[:, :], ones_row[:, :], temp_inv[:, :], start=True, stop=True).then_inc(temp_bc, 1)
            pe.wait_ge(turned_copied, 1)
            for pair in range(PAIRS):
                at = slice(pair * P, (pair + 1) * P)
                for k in range(K2):
                    pe.matmul(wxs_ps[k][:, at], wxt_sb[:, pair, k * P:(k + 1) * P], pair_slice[:, :],
                              start=True, stop=True)
                last = pe.matmul(brow_ps[:, at], bx_col[:, pair:pair + 1], pair_slice[:, :], start=True, stop=True)
            last.then_inc(products, 1)
            pe.wait_ge(totals_ready, 1)
            pe.matmul(offsets_ps[:, 0:ROWS + 1], total_bc[:, :], before[0:ROWS, :], start=True, stop=True)
            pe.matmul(counts_ps[:, 0:ROWS + 1], total_bc[:, :], follows[0:ROWS, :], start=True,
                      stop=True).then_inc(offsets_ready, 1)
            pe.wait_ge(bias_ready, 1)
            pe.wait_ge(temp_bc_copied, 1)
            pe.matmul(spread_ps[:, :], ones_row[:, :], bias_row[:, :], start=True, stop=True).then_inc(bias_spread, 1)


def rotations_phase(nc, v):
    D, GB, K2, ROWS, LEVELS = v["D"], v["GB"], v["K2"], v["ROWS"], v["LEVELS"]
    TABLE, MAX_GROUPS, GROUP_RANKS = v["TABLE"], v["MAX_GROUPS"], v["GROUP_RANKS"]
    iota_row, pcol, ident, mat_t = v["iota_row"], v["pcol"], v["ident"], v["mat_t"]
    ident_bf, strict, neg_sub, level_mask = v["ident_bf"], v["strict"], v["neg_sub"], v["level_mask"]
    first_mask, second_mask, rank = v["first_mask"], v["second_mask"], v["rank"]
    row_start, row_gap, groups_i = v["row_start"], v["row_gap"], v["groups_i"]
    d_table, term_table = v["d_table"], v["term_table"]
    UP = LEVELS - 1
    HALF = P // 2
    TARGET, OTHER, AT_TARGET, AT_OTHER = range(4)
    assert GB <= UP

    with ExitStack() as ctx:
        def sb(name, shape, dt=F32):
            return ctx.enter_context(nc.sbuf_tensor(name, shape, dt))

        def ps(name, shape):
            return ctx.enter_context(nc.psum_tensor(name, shape, F32))

        def sem(name):
            return ctx.enter_context(nc.semaphore(name))

        index_f = sb("index_f", [P, GB])
        index_i = sb("index_i", [P, GB], I32)
        gathered_d = sb("gathered_d", [P, GB], I32)
        term_i = sb("term_i", [P, GB], I32)
        raw = sb("raw", [P, GB, 4])
        look = sb("look", [P, GB, ROWS - 1])
        look_sum = sb("look_sum", [P, GB])
        second = sb("second", [P, GB])
        active = sb("active", [P, GB])
        present = sb("present", [P, GB])
        fresh = sb("fresh", [P, 4, GB])
        held = sb("held", [P, 4, GB])
        target_bc = sb("target_bc", [P, GB, P], BF16)
        vt = sb("vt", [P, GB, D])
        vt_other = sb("vt_other", [P, GB, D])
        lower = sb("lower", [P, GB, P])
        lower_other = sb("lower_other", [P, GB, P])
        lower_mask = sb("lower_mask", [P, GB, P])
        lower_level = sb("lower_level", [P, LEVELS, GB, P])
        t0_sb = sb("t0_sb", [P, GB, P])
        t_sb = sb("t_sb", [P, GB, P])
        s_sb = sb("s_sb", [P, GB, P])
        y_sb = sb("y_sb", [P, GB, HALF])
        rt_sb = sb("rt_sb", [P, K2, GB, P])
        u_sb = sb("u_sb", [P, GB, D])
        w_sb = sb("w_sb", [P, D])
        m_sb = sb("m_sb", [P, K2, D])

        target_ps = ps("target_ps", [P, GB, P])
        y_ps = ps("y_ps", [P, GB, P])
        s_ps = ps("s_ps", [P, GB * P])
        t_ps = ps("t_ps", [P, GB, P])
        rt_ps = [ps(f"rt_ps{h}", [P, GB, P]) for h in range(K2)]
        w_ps = ps("w_ps", [P, 2, D])
        m_ps = ps("m_ps", [P, K2, D])

        chain, gathers_begun = sem("dve_chain_2"), sem("gathers_begun")
        index_ready, d_gathered = sem("index_ready"), sem("d_gathered")
        term_ready, raw_gathered = sem("term_ready"), sem("raw_gathered")
        decoded, target_bc_ready, targets_done = sem("decoded"), sem("target_bc_ready"), sem("targets_done")
        vt_ready, lower_ready, masked = sem("vt_ready"), sem("lower_ready"), sem("masked")
        t0_ready, y_done, s_done, t_done = sem("t0_ready"), sem("y_done"), sem("s_done"), sem("t_done")
        y_copied, s_ready, t_copied = sem("y_copied"), sem("s_ready"), sem("t_copied")
        rt_done, rt_ready, u_ready = sem("rt_done"), sem("rt_ready"), sem("u_ready")
        w_done, w_copied, m_done, m_ready = sem("w_done"), sem("w_copied"), sem("m_done"), sem("m_ready")
        mt_done = sem("mt_done")
        block = ctx.enter_context(nc.Block())

        def groups(engine):
            return engine.value_load(groups_i[0:1, 0:1], min_val=1, max_val=MAX_GROUPS)

        def halves(a, level):
            return a.rearrange("p b (n two w) -> p (b n) two w", two=2, w=2 ** level)

        @block.gpsimd
        def _(pool):
            def gather_d(group):
                pool.wait_ge(index_ready, group + 1)
                pool.sem_inc(gathers_begun, 1)
                for b in range(GB):
                    pool.indirect_dma_start(
                        out=gathered_d[:, b:b + 1], out_offset=None, in_=d_table[:, :],
                        in_offset=bass.IndirectOffsetOnAxis(ap=index_i[:, b:b + 1], axis=0)
                    ).then_inc(d_gathered, 16)

            def gather_terms(group):
                pool.wait_ge(term_ready, group + 1)
                pool.sem_inc(gathers_begun, 1)
                for b in range(GB):
                    pool.indirect_dma_start(
                        out=raw[:, b, :], out_offset=None, in_=term_table[:, :],
                        in_offset=bass.IndirectOffsetOnAxis(ap=term_i[:, b:b + 1], axis=0)
                    ).then_inc(raw_gathered, 16)

            def mask(level):
                pool.tensor_tensor(lower_level[:, level, :, :], lower[:, :, :],
                                   level_mask[:, level, :].unsqueeze(1).to_broadcast([P, GB, P]),
                                   ALU.mult).then_inc(masked, 1)

            n = groups(pool)
            gather_d(0)
            gather_terms(0)
            gather_d(1)
            pool.wait_ge(lower_ready, 1)
            for level in range(1, LEVELS):
                mask(level)
            gather_terms(1)
            with pool.Fori(0, n) as i:
                gather_d(i + 2)
                pool.wait_ge(lower_ready, i + 2)
                for level in range(1, LEVELS):
                    pool.wait_ge(y_done, i * UP + level)
                    mask(level)
                    if level == 3:
                        gather_terms(i + 2)
            pool.wait_ge(raw_gathered, n * (16 * GB) + 2 * 16 * GB)

        @block.vector
        def _(dve):
            c = Chain(dve, chain)
            link = c.link

            def find_index():
                for b in range(GB):
                    last = dve.scalar_tensor_tensor(look[:, b, :], row_start[:, 1:ROWS], rank[:, b:b + 1],
                                                    row_gap[:, 1:ROWS], ALU.is_le, ALU.mult,
                                                    accum_out=look_sum[:, b:b + 1])
                link(last)
                link(dve.tensor_tensor(index_f[:, :], look_sum[:, :], rank[:, :], ALU.add))
                link(dve.tensor_scalar(index_f[:, :], index_f[:, :], float(TABLE - 1), None, ALU.min))
                dve.tensor_copy(index_i[:, :], index_f[:, :]).then_inc(index_ready, 1)

            def find_term(group):
                dve.wait_ge(d_gathered, group * (16 * GB) + 16 * GB)
                dve.tensor_tensor(term_i[:, :], index_f[:, :], gathered_d[:, :],
                                  ALU.add).then_inc(term_ready, 1)

            def decode(group):
                dve.wait_ge(raw_gathered, group * (16 * GB) + 16 * GB)
                dve.tensor_scalar(present[:, :], rank[:, :], row_start[:, ROWS:ROWS + 1], None, ALU.is_lt)
                dve.tensor_copy(fresh[:, OTHER, :], raw[:, :, 1])
                link(dve.tensor_scalar(second[:, :], raw[:, :, 0], float(D), None, ALU.is_ge))
                dve.scalar_tensor_tensor(fresh[:, TARGET, :], second[:, :], float(-D), raw[:, :, 0],
                                         ALU.mult, ALU.add)
                link(dve.tensor_scalar(active[:, :], second[:, :], second_mask[:, 0:1], first_mask[:, 0:1],
                                       ALU.mult, ALU.add))
                link(dve.tensor_tensor(active[:, :], active[:, :], present[:, :], ALU.mult))
                dve.tensor_tensor(fresh[:, AT_TARGET:AT_OTHER + 1, :].rearrange("p c b -> p b c"),
                                  raw[:, :, 2:4], active[:, :].unsqueeze(2).to_broadcast([P, GB, 2]),
                                  ALU.mult).then_inc(decoded, 1)
                dve.wait_ge(decoded, group + 1)

            def next_ranks():
                link(dve.tensor_scalar(rank[:, :], rank[:, :], float(GROUP_RANKS), None, ALU.add))

            def lower_entries(group):
                dve.wait_ge(targets_done, group + 1)
                for b in range(GB):
                    dve.tensor_scalar(lower[:, b, :], target_ps[:, b, :], fresh[:, TARGET, b:b + 1],
                                      fresh[:, AT_TARGET, b:b + 1], ALU.is_equal, ALU.mult)
                    last = dve.tensor_scalar(lower_other[:, b, :], target_ps[:, b, :],
                                             fresh[:, OTHER, b:b + 1], fresh[:, AT_OTHER, b:b + 1],
                                             ALU.is_equal, ALU.mult)
                link(last)

            def lower_masks(group):
                for b in range(GB):
                    dve.scalar_tensor_tensor(lower_mask[:, b, :], neg_sub[:, :], second[:, b:b + 1],
                                             strict[:, :], ALU.mult, ALU.add)
                link(dve.tensor_tensor(lower[:, :, :], lower[:, :, :], lower_other[:, :, :], ALU.add))
                dve.tensor_tensor(lower[:, :, :], lower[:, :, :], lower_mask[:, :, :],
                                  ALU.mult).then_inc(lower_ready, 1)
                dve.wait_ge(lower_ready, group + 1)

            def first_level():
                link(dve.tensor_tensor(t0_sb[:, :, :], lower[:, :, :],
                                       level_mask[:, 0, :].unsqueeze(1).to_broadcast([P, GB, P]), ALU.mult))
                dve.tensor_tensor(t0_sb[:, :, :], t0_sb[:, :, :],
                                  ident[:, :].unsqueeze(1).to_broadcast([P, GB, P]),
                                  ALU.add).then_inc(t0_ready, 1)

            def targets_rows():
                for b in range(GB):
                    last = dve.tensor_scalar(u_sb[:, b, :], iota_row[:, :], held[:, TARGET, b:b + 1], None,
                                             ALU.is_equal)
                last.then_inc(u_ready, 1)

            def vectors_rows(group):
                for b in range(GB):
                    last = dve.tensor_scalar(vt_other[:, b, :], iota_row[:, :], held[:, OTHER, b:b + 1],
                                             held[:, AT_OTHER, b:b + 1], ALU.is_equal, ALU.mult)
                link(last)
                dve.wait_ge(u_ready, group + 2)
                for b in range(GB):
                    last = dve.scalar_tensor_tensor(vt[:, b, :], u_sb[:, b, :], held[:, AT_TARGET, b:b + 1],
                                                    vt_other[:, b, :], ALU.mult, ALU.add)
                last.then_inc(vt_ready, 1)

            n = groups(dve)
            dve.memset(u_sb[:, :, :], 0.0).then_inc(u_ready, 1)
            dve.memset(rt_sb[:, :, :, :], 0.0).then_inc(rt_ready, 1)
            for h in range(K2):
                last = dve.tensor_scalar(m_sb[:, h, :], iota_row[:, :], float(-h * P), pcol[:, 0:1],
                                         ALU.add, ALU.is_equal)
            last.then_inc(m_ready, 1)
            find_index()
            find_term(0)
            decode(0)
            next_ranks()
            find_index()
            lower_entries(0)
            lower_masks(0)
            first_level()
            find_term(1)
            with dve.Fori(0, n) as i:
                c.loop(i, 12)
                dve.wait_ge(s_done, i * LEVELS + 1)
                dve.tensor_copy(s_sb[:, :, :].rearrange("p b k -> p (b k)"), s_ps[:, :]).then_inc(s_ready, 1)
                link(dve.tensor_copy(held[:, :, :], fresh[:, :, :]))
                decode(i + 1)
                next_ranks()
                find_index()
                for level in range(1, LEVELS):
                    dve.wait_ge(s_done, i * LEVELS + (level + 1))
                    right = halves(s_sb[:, :, :], level)[:, :, 1, :]
                    dve.tensor_tensor(right, right,
                                      s_ps[:, 0:GB * HALF].rearrange("p (n w) -> p n w", w=2 ** level),
                                      ALU.add).then_inc(s_ready, 1)
                    if level == 1:
                        dve.wait_ge(masked, i * UP + UP)
                        lower_entries(i + 1)
                    if level == 2:
                        lower_masks(i + 1)
                    if level == 3:
                        first_level()
                        find_term(i + 2)
                    if level == 4:
                        dve.wait_ge(m_done, i * GB + GB)
                        targets_rows()
                    if level == 5:
                        vectors_rows(i)
                assert c.n == c.per, c.n
            dve.wait_ge(mt_done, 1)
            dve.tensor_copy(mat_t[:, :, :], w_ps[:, :, :])

        @block.scalar
        def _(act):
            def spread_targets(group):
                act.wait_ge(decoded, group + 1)
                act.activation(target_bc[:, :, :], fresh[:, TARGET, :].unsqueeze(2).to_broadcast([P, GB, P]),
                               ACT.Copy).then_inc(target_bc_ready, 1)

            def copy_applied(turn, b):
                act.wait_ge(w_done, turn * GB + (b + 1))
                act.activation(w_sb[:, :], w_ps[:, b % 2, :], ACT.Copy).then_inc(w_copied, 1)
                act.wait_ge(m_done, turn * GB + (b + 1))
                act.activation(m_sb[:, :, :], m_ps[:, :, :], ACT.Copy).then_inc(m_ready, 1)

            n = groups(act)
            spread_targets(0)
            with act.Fori(0, n) as i:
                for level in range(1, LEVELS):
                    act.wait_ge(y_done, i * UP + level)
                    act.activation(y_sb[:, :, :], y_ps[:, :, 0:HALF], ACT.Copy).then_inc(y_copied, 1)
                    if level == 2:
                        act.wait_ge(t_done, i * (UP - 1) + 1)
                        act.activation(t_sb[:, :, :], t_ps[:, :, :], ACT.Copy).then_inc(t_copied, 1)
                    if level > 2:
                        act.wait_ge(t_done, i * (UP - 1) + (level - 1))
                        act.activation(halves(t_sb[:, :, :], level - 1)[:, :, 0, :],
                                       halves(t_ps[:, :, :], level - 1)[:, :, 0, :],
                                       ACT.Copy).then_inc(t_copied, 1)
                    if level == 1:
                        spread_targets(i + 1)
                    if level <= GB:
                        copy_applied(i, level - 1)
                act.wait_ge(rt_done, i + 1)
                for h in range(K2):
                    last = act.activation(rt_sb[:, h, :, :], rt_ps[h][:, :, :], ACT.Copy)
                last.then_inc(rt_ready, 1)
            for b in range(GB):
                copy_applied(n, b)

        @block.tensor
        def _(pe):
            def spread_targets(group):
                pe.wait_ge(target_bc_ready, group + 1)
                for b in range(GB):
                    last = pe.matmul(target_ps[:, b, :], target_bc[:, b, :], ident_bf[:, :],
                                     start=True, stop=True)
                last.then_inc(targets_done, 1)

            def apply_read(turn, b):
                if b == 0:
                    pe.wait_ge(rt_ready, turn + 1)
                pe.wait_ge(m_ready, turn * GB + (b + 1))
                for h in range(K2):
                    last = pe.matmul(w_ps[:, b % 2, :], rt_sb[:, h, b, :], m_sb[:, h, :],
                                     start=(h == 0), stop=(h == K2 - 1))
                last.then_inc(w_done, 1)

            def apply_write(turn, b):
                if b == 0:
                    pe.wait_ge(u_ready, turn + 1)
                pe.wait_ge(w_copied, turn * GB + (b + 1))
                for h in range(K2):
                    last = pe.matmul(m_ps[:, h, :], u_sb[:, b, h * P:(h + 1) * P], w_sb[:, :],
                                     start=False, stop=True, skip_group_check=True)
                last.then_inc(m_done, 1)

            n = groups(pe)
            pe.wait_ge(m_ready, 1)
            pe.matmul(m_ps[:, :, :], ident[:, :], m_sb[:, :, :], start=True, stop=True)
            spread_targets(0)
            with pe.Fori(0, n) as i:
                pe.wait_ge(t0_ready, i + 1)
                for b in range(GB):
                    last = pe.transpose(s_ps[:, b * P:(b + 1) * P], t0_sb[:, b, :], ident[:, :])
                last.then_inc(s_done, 1)
                for level in range(1, LEVELS):
                    pe.wait_ge(masked, i * UP + level)
                    pe.wait_ge(s_ready, i * LEVELS + level)
                    for b in range(GB):
                        last = pe.matmul(y_ps[:, b, 0:HALF], lower_level[:, level, b, :],
                                         halves(s_sb[:, b:b + 1, :], level)[:, :, 1, :],
                                         start=True, stop=True)
                    last.then_inc(y_done, 1)
                    if level > 1:
                        for b in range(GB):
                            last = pe.transpose(t_ps[:, b, :], s_sb[:, b, :], ident[:, :])
                        last.then_inc(t_done, 1)
                    if level == 2:
                        spread_targets(i + 1)
                    if level <= GB:
                        apply_read(i, level - 1)
                    pe.wait_ge(y_copied, i * UP + level)
                    if level > 1:
                        pe.wait_ge(t_copied, i * (UP - 1) + (level - 1))
                    t_now = t0_sb if level == 1 else t_sb
                    for b in range(GB):
                        last = pe.matmul(s_ps[:, b * HALF:(b + 1) * HALF], t_now[:, b, :], y_sb[:, b, :],
                                         start=True, stop=True)
                    last.then_inc(s_done, 1)
                    if level <= GB:
                        apply_write(i, level - 1)
                pe.wait_ge(s_ready, i * LEVELS + LEVELS)
                pe.wait_ge(vt_ready, i + 1)
                for h in range(K2):
                    for b in range(GB):
                        last = pe.matmul(rt_ps[h][:, b, :], vt[:, b, h * P:(h + 1) * P], s_sb[:, b, :],
                                         start=True, stop=True)
                last.then_inc(rt_done, 1)
            for b in range(GB):
                apply_read(n, b)
                apply_write(n, b)
            pe.wait_ge(m_ready, n * GB + (GB + 1))
            for h in range(K2):
                for g in range(K2):
                    last = pe.transpose(w_ps[:, g, h * P:(h + 1) * P], m_sb[:, h, g * P:(g + 1) * P],
                                        ident[:, :])
            last.then_inc(mt_done, 1)


def tokens_phase(nc, v):
    D, INNER, G, H, K2, PAIRS, TP, NT = (v[k] for k in ("D", "INNER", "G", "H", "K2", "PAIRS", "TP", "NT"))
    x_sb, ident, mat_t, minus_half = v["x_sb"], v["ident"], v["mat_t"], v["minus_half"]
    scale1, shift1 = v["scale1"], v["shift1"]
    wxs, bias_bc, wt_sb, z_sb, norm_sb = v["wxs"], v["bias_bc"], v["wt_sb"], v["z_sb"], v["norm_sb"]
    TURNS = NT // 2
    assert NT % 2 == 0 and PAIRS % 2 == 0 and TURNS > 5
    with ExitStack() as ctx:
        def sb(name, shape, dt=F32):
            return ctx.enter_context(nc.sbuf_tensor(name, shape, dt))

        def ps(name, shape):
            return ctx.enter_context(nc.psum_tensor(name, shape, F32))

        def sem(name):
            return ctx.enter_context(nc.semaphore(name))

        normed1 = sb("normed1", [TP, 2, D])
        normed1_t = sb("normed1_t", [P, 2, K2 * TP])
        stats = sb("stats", [TP, 2, 6])
        both = sb("both", [TP, 2, 2])
        mean2 = sb("mean2", [TP, NT])
        rstd2 = sb("rstd2", [TP, NT])
        normed2 = sb("normed2", [TP, 2, D])
        normed2_t = sb("normed2_t", [P, 2, K2 * TP])
        normed_z = sb("normed_z", [TP, 2, D])
        logits = sb("logits", [TP, 2, INNER])
        weights = sb("weights", [TP, 2, INNER])
        top = sb("top", [TP, 2, H])
        total = sb("total", [TP, 2, H])
        norm_part = sb("norm_part", [P, 2, PAIRS])
        zeros = sb("zeros", [1, 2 * D])
        turn_ps = ps("xt_ps", [P, 2, D])
        rotated_ps = ps("rotated_ps", [TP, 2, D])
        logit_ps = [ps(f"logit_ps{j}", [TP, INNER]) for j in range(2)]
        wt_ps = [ps(f"wt_ps{j}", [P, PAIRS * P]) for j in range(2)]
        z_ps = [ps(f"z_ps{k}", [P, 2, D]) for k in range(PAIRS // 2)]
        chain, zeroed, stats_begun = sem("dve_chain_t"), sem("zeroed_t"), sem("stats_begun")
        normed1_ready, turned1, copied1 = sem("normed1_ready"), sem("turned1"), sem("copied1")
        rotated, numbers_ready, rstd_ready = sem("rotated"), sem("numbers_ready"), sem("rstd_ready")
        normed2_ready, turned2, copied2 = sem("normed2_ready"), sem("turned2"), sem("copied2")
        normed_z_ready = sem("normed_z_ready")
        scored, top_ready, shifted, exps = sem("scored"), sem("top_ready"), sem("shifted"), sem("exps")
        total_ready, weights_ready = sem("total_ready"), sem("weights_ready")
        weights_turned, weights_kept = sem("weights_turned"), sem("weights_kept")
        weights_added, summed = sem("weights_added"), sem("summed")
        block = ctx.enter_context(nc.Block())

        def heads(a):
            return a.rearrange("p (h g) -> p h g", g=G)

        def inside(q):
            return not isinstance(q, int) or 0 <= q < TURNS

        def all_turns(engine, turn, chain_of=None, links=0):
            for r in range(-2, 2):
                turn(r)
            with engine.Fori(2, TURNS - 2) as r:
                if chain_of is not None:
                    chain_of.loop(r - 2, links)
                turn(r)
                if chain_of is not None:
                    assert chain_of.n == links, chain_of.n
            if chain_of is not None:
                chain_of.close(TURNS - 4)
            for r in range(TURNS - 2, TURNS + 2):
                turn(r)

        @block.gpsimd
        def _(pool):
            def inverse_deviation(q):
                pool.wait_ge(numbers_ready, q + 1)
                at = bass.ds(q * 2, 2)
                pool.tensor_tensor(rstd2[:, at], rstd2[:, at], minus_half[:, 0:2], ALU.pow).then_inc(rstd_ready, 1)

            def shift(q, j):
                pool.wait_ge(top_ready, q * 2 + (j + 1))
                pool.tensor_tensor(heads(logits[:, j, :]), heads(logits[:, j, :]),
                                   top[:, j, :].unsqueeze(2).to_broadcast([TP, H, G]),
                                   ALU.subtract).then_inc(shifted, 1)

            def divide(q, j):
                pool.wait_ge(total_ready, q * 2 + (j + 1))
                pool.wait_ge(summed, q * 2 + (j + 1))
                pool.tensor_tensor(heads(weights[:, j, :]), heads(logits[:, j, :]),
                                   total[:, j, :].unsqueeze(2).to_broadcast([TP, H, G]),
                                   ALU.mult).then_inc(weights_ready, 1)

            def turn(r):
                if inside(r - 1):
                    shift(r - 1, 0)
                    shift(r - 1, 1)
                if inside(r + 1):
                    inverse_deviation(r + 1)
                if inside(r - 1):
                    divide(r - 1, 0)
                    divide(r - 1, 1)

            all_turns(pool, turn)

        @block.vector
        def _(dve):
            c = Chain(dve, chain)
            link = c.link

            def rotation(q):
                dve.wait_ge(rotated, q + 1)
                for j in range(2):
                    last = dve.tensor_tensor(x_sb[:, q * 2 + j, :], x_sb[:, q * 2 + j, :], rotated_ps[:, j, :],
                                             ALU.add)
                link(last)
                dve.sem_inc(stats_begun, 1)
                for j in range(2):
                    last = dve.bn_stats(stats[:, j, :], x_sb[:, q * 2 + j, :])
                link(last)
                dve.sem_inc(stats_begun, 1)
                for j in range(2):
                    last = dve.bn_aggr(both[:, j, :], stats[:, j, :])
                link(last)
                at = bass.ds(q * 2, 2)
                dve.tensor_copy(mean2[:, at], both[:, :, 0])
                dve.tensor_scalar(rstd2[:, at], both[:, :, 1], EPS, None, ALU.add).then_inc(numbers_ready, 1)

            def normalise(q, to, ready):
                for j in range(2):
                    at = bass.ds(q * 2 + j, 1)
                    last = dve.tensor_scalar(to[:, j, :], x_sb[:, q * 2 + j, :], mean2[:, at], rstd2[:, at],
                                             ALU.subtract, ALU.mult)
                last.then_inc(ready, 1)

            def bias_and_top(q, j):
                dve.wait_ge(scored, q * 2 + (j + 1))
                if not (isinstance(q, int) and q == 0):
                    dve.wait_ge(weights_ready, q * 2 + (j - 1))
                link(dve.tensor_tensor(logits[:, j, :], logit_ps[j][:, :], bias_bc[0:TP, :], ALU.add))
                dve.tensor_reduce(top[:, j, :], heads(logits[:, j, :]), AX.X, ALU.max).then_inc(top_ready, 1)

            def totals(q, j):
                dve.wait_ge(exps, q * 2 + (j + 1))
                link(dve.tensor_reduce(total[:, j, :], heads(logits[:, j, :]), AX.X, ALU.add))
                dve.reciprocal(total[:, j, :], total[:, j, :]).then_inc(total_ready, 1)

            def norms(q, j):
                dve.wait_ge(weights_kept, q * 2 + (j + 1))
                link(dve.tensor_reduce(norm_part[:, j, :],
                                       wt_ps[j][:, 0:PAIRS * TP].rearrange("p (k n) -> p k n", n=TP), AX.X,
                                       ALU.add))
                dve.tensor_tensor(norm_sb[:, :], norm_sb[:, :], norm_part[:, j, :],
                                  ALU.add).then_inc(weights_added, 1)
                dve.wait_ge(weights_added, q * 2 + (j + 3))

            def turn(r):
                if inside(r):
                    dve.wait_ge(rstd_ready, r + 1)
                    if not (isinstance(r, int) and r == 0):
                        dve.wait_ge(turned2, r)
                    normalise(r, normed2, normed2_ready)
                if inside(r - 2):
                    dve.wait_ge(summed, (r - 2) * 2 + 2)
                    normalise(r - 2, normed_z, normed_z_ready)
                if inside(r - 1):
                    bias_and_top(r - 1, 0)
                    bias_and_top(r - 1, 1)
                    totals(r - 1, 0)
                    totals(r - 1, 1)
                if inside(r + 1):
                    rotation(r + 1)
                if inside(r - 2):
                    norms(r - 2, 0)
                    norms(r - 2, 1)

            dve.memset(norm_sb[:, :], 0.0)
            link(dve.memset(zeros[:, :], 0.0))
            dve.sem_inc(zeroed, 1)
            dve.sem_inc(weights_added, 2)
            all_turns(dve, turn, c, 9)
            dve.wait_ge(summed, NT + 2)
            for k in range(PAIRS // 2):
                dve.tensor_copy(z_sb[:, 2 * k:2 * k + 2, :], z_ps[k][:, :, :])

        @block.scalar
        def _(act):
            def normalise(q):
                if not (isinstance(q, int) and q == 0):
                    act.wait_ge(turned1, q)
                for j in range(2):
                    last = act.activation(normed1[:, j, :], x_sb[:, q * 2 + j, :], ACT.Identity,
                                          bias=shift1[:, bass.ds(q * 2 + j, 1)],
                                          scale=scale1[:, bass.ds(q * 2 + j, 1)])
                last.then_inc(normed1_ready, 1)

            def exponentials(q, j):
                act.wait_ge(shifted, q * 2 + (j + 1))
                act.activation(logits[:, j, :], logits[:, j, :], ACT.Exp).then_inc(exps, 1)

            def keep_weights(q, j):
                act.wait_ge(weights_turned, q * 2 + (j + 1))
                act.activation(wt_sb[:, q * 2 + j, :, :].rearrange("p k n -> p (k n)"),
                               wt_ps[j][:, 0:PAIRS * TP], ACT.Copy).then_inc(weights_kept, 1)

            def turn(r):
                if inside(r + 1):
                    act.wait_ge(turned1, r + 2)
                    act.activation(normed1_t[:, :, :], turn_ps[:, :, 0:K2 * TP], ACT.Copy).then_inc(copied1, 1)
                if inside(r + 2):
                    normalise(r + 2)
                if inside(r - 1):
                    exponentials(r - 1, 0)
                    exponentials(r - 1, 1)
                if inside(r):
                    act.wait_ge(turned2, r + 1)
                    act.activation(normed2_t[:, :, :], turn_ps[:, :, 0:K2 * TP], ACT.Copy).then_inc(copied2, 1)
                if inside(r - 2):
                    keep_weights(r - 2, 0)
                    keep_weights(r - 2, 1)

            all_turns(act, turn)

        @block.tensor
        def _(pe):
            def transposes(normed, done):
                for j in range(2):
                    for k in range(K2):
                        last = pe.transpose(turn_ps[:, j, k * TP:(k + 1) * TP], normed[:, j, k * P:(k + 1) * P],
                                            ident[0:TP, 0:TP])
                last.then_inc(done, 1)

            def rotate(q):
                pe.wait_ge(copied1, q + 1)
                if not (isinstance(q, int) and q == 0):
                    pe.wait_ge(numbers_ready, q)
                for j in range(2):
                    for k in range(K2):
                        last = pe.matmul(rotated_ps[:, j, :], normed1_t[:, j, k * TP:(k + 1) * TP],
                                         mat_t[:, k, :], start=(k == 0), stop=(k == K2 - 1))
                last.then_inc(rotated, 1)

            def score(q):
                pe.wait_ge(copied2, q + 1)
                if not (isinstance(q, int) and q == 0):
                    pe.wait_ge(top_ready, q * 2)
                for j in range(2):
                    for k in range(K2):
                        last = pe.matmul(logit_ps[j][:, :], normed2_t[:, j, k * TP:(k + 1) * TP], wxs[:, k, :],
                                         start=(k == 0), stop=(k == K2 - 1))
                    last.then_inc(scored, 1)

            def sum_up(q, j):
                pe.wait_ge(weights_ready, q * 2 + (j + 1))
                pe.wait_ge(weights_added, q * 2 + (j + 1))
                for k in range(PAIRS):
                    last = pe.transpose(wt_ps[j][:, k * TP:(k + 1) * TP], weights[:, j, k * P:(k + 1) * P],
                                        ident[0:TP, 0:TP])
                last.then_inc(weights_turned, 1)
                pe.wait_ge(normed_z_ready, q + 1)
                for k in range(PAIRS):
                    last = pe.matmul(z_ps[k // 2][:, k % 2, :], weights[:, j, k * P:(k + 1) * P],
                                     normed_z[:, j, :], start=False, stop=True, skip_group_check=True)
                last.then_inc(summed, 1)

            def turn(r):
                if inside(r + 1):
                    pe.wait_ge(normed1_ready, r + 2)
                    if not isinstance(r, int) or r > 0:
                        pe.wait_ge(copied2, r)
                    transposes(normed1, turned1)
                if inside(r - 1):
                    score(r - 1)
                if inside(r + 1):
                    rotate(r + 1)
                if inside(r):
                    pe.wait_ge(normed2_ready, r + 1)
                    transposes(normed2, turned2)
                if inside(r - 2):
                    sum_up(r - 2, 0)
                    sum_up(r - 2, 1)

            pe.wait_ge(zeroed, 1)
            for k in range(PAIRS // 2):
                last = pe.matmul(z_ps[k][:, :, :], zeros[:, 0:P], zeros[:, :], start=True, stop=True)
            last.then_inc(summed, 2)
            all_turns(pe, turn)


def slices_phase(nc, v):
    D, INNER, G, H, K2, PAIRS = (v[k] for k in ("D", "INNER", "G", "H", "K2", "PAIRS"))
    z_sb, wfx_sb, bfx_bc, wout_sb, q_sb = v["z_sb"], v["wfx_sb"], v["bfx_bc"], v["wout_sb"], v["q_sb"]
    pair_w, ident, norm_sb = v["pair_w"], v["ident"], v["norm_sb"]
    SCALE = G ** -0.5
    with ExitStack() as ctx:
        def sb(name, shape, dt=F32):
            return ctx.enter_context(nc.sbuf_tensor(name, shape, dt))

        def sem(name):
            return ctx.enter_context(nc.semaphore(name))

        zt_sb = sb("zt_sb", [P, K2, PAIRS, P])
        token = sb("token", [P, PAIRS, P])
        norm_inv = sb("norm_inv", [P, PAIRS])
        token_t = sb("token_t", [P, PAIRS, P])
        query_t, key_t, value = sb("query_t", [P, PAIRS, P]), sb("key_t", [P, PAIRS, P]), sb("value", [P, PAIRS, P])
        score = sb("score", [P, PAIRS, G])
        top, total = sb("top_s", [P, PAIRS]), sb("total_s", [P, PAIRS])
        attn, attn_t = sb("attn", [P, PAIRS, P]), sb("attn_t", [P, PAIRS, P])
        mixed_t = sb("mixed_t", [P, PAIRS, P])
        ps = [ctx.enter_context(nc.psum_tensor(f"slice_ps{k}", [P, PAIRS, P], F32)) for k in range(8)]
        chain, pe_done, act_done, ready = sem("dve_chain_s"), sem("pe_done"), sem("act_done"), sem("ready")
        block = ctx.enter_context(nc.Block())
        HALVES = [slice(0, G), slice(G, 2 * G)]

        @block.vector
        def _(dve):
            link = Chain(dve, chain).link
            dve.memset(attn[:, :, :], 0.0)
            link(dve.memset(token[:, :, :], 0.0))
            link(dve.tensor_scalar(norm_inv[:, :], norm_sb[:, :], 1e-5, None, ALU.add))
            link(dve.reciprocal(norm_inv[:, :], norm_inv[:, :]))
            dve.wait_ge(pe_done, 1)
            for k in range(K2):
                last = dve.tensor_copy(zt_sb[:, k, :, :], ps[k][:, :, :])
            last.then_inc(ready, 1)
            dve.wait_ge(pe_done, 2)
            for pair in range(PAIRS):
                for n, at in enumerate(HALVES):
                    cols = slice(pair * P + n * G, pair * P + (n + 1) * G)
                    last = dve.scalar_tensor_tensor(token[at, pair, at], bfx_bc[at, cols],
                                                    norm_sb[at, pair:pair + 1], ps[2][at, pair, at],
                                                    ALU.mult, ALU.add)
            link(last)
            dve.tensor_tensor(token[:, :, :], token[:, :, :],
                              norm_inv[:, :].unsqueeze(2).to_broadcast([P, PAIRS, P]),
                              ALU.mult).then_inc(ready, 1)
            dve.wait_ge(pe_done, 3)
            dve.tensor_copy(token_t[:, :, :], ps[3][:, :, :]).then_inc(ready, 1)
            dve.wait_ge(pe_done, 4)
            dve.tensor_copy(query_t[:, :, :], ps[4][:, :, :])
            dve.tensor_copy(key_t[:, :, :], ps[5][:, :, :])
            dve.tensor_copy(value[:, :, :], ps[6][:, :, :]).then_inc(ready, 1)
            dve.wait_ge(pe_done, 5)
            for at in HALVES:
                last = dve.tensor_scalar(score[at, :, :], ps[7][at, :, at], SCALE, None, ALU.mult)
            link(last)
            link(dve.tensor_reduce(top[:, :], score[:, :, :], AX.X, ALU.max))
            dve.tensor_tensor(score[:, :, :], score[:, :, :], top[:, :].unsqueeze(2).to_broadcast([P, PAIRS, G]),
                              ALU.subtract).then_inc(ready, 1)
            dve.wait_ge(act_done, 1)
            link(dve.tensor_reduce(total[:, :], score[:, :, :], AX.X, ALU.add))
            link(dve.reciprocal(total[:, :], total[:, :]))
            for at in HALVES:
                last = dve.tensor_tensor(attn[at, :, at], score[at, :, :],
                                         total[at, :].unsqueeze(2).to_broadcast([G, PAIRS, G]), ALU.mult)
            last.then_inc(ready, 1)
            dve.wait_ge(pe_done, 6)
            dve.tensor_copy(attn_t[:, :, :], ps[0][:, :, :]).then_inc(ready, 1)
            dve.wait_ge(pe_done, 7)
            dve.tensor_copy(mixed_t[:, :, :], ps[1][:, :, :]).then_inc(ready, 1)
            dve.wait_ge(pe_done, 8)
            for pair in range(PAIRS):
                dve.tensor_copy(q_sb[:, pair, :],
                                ps[2 + pair // 2][:, :, :].rearrange("p a b -> p (a b)")
                                [:, (pair % 2) * D:(pair % 2 + 1) * D])

        @block.scalar
        def _(act):
            act.wait_ge(ready, 5)
            act.activation(score[:, :, :], score[:, :, :], ACT.Exp).then_inc(act_done, 1)

        @block.tensor
        def _(pe):
            for k in range(K2):
                for pair in range(PAIRS):
                    last = pe.transpose(ps[k][:, pair, :], z_sb[:, pair, k * P:(k + 1) * P], ident[:, :])
            last.then_inc(pe_done, 1)
            pe.wait_ge(ready, 1)
            for pair in range(PAIRS):
                for k in range(K2):
                    last = pe.matmul(ps[2][:, pair, :], zt_sb[:, k, pair, :], wfx_sb[:, k, pair * P:(pair + 1) * P],
                                     start=(k == 0), stop=(k == K2 - 1))
            last.then_inc(pe_done, 1)
            pe.wait_ge(ready, 2)
            for pair in range(PAIRS):
                last = pe.transpose(ps[3][:, pair, :], token[:, pair, :], ident[:, :])
            last.then_inc(pe_done, 1)
            pe.wait_ge(ready, 3)
            for pair in range(PAIRS):
                pe.matmul(ps[4][:, pair, :], pair_w[:, 0, :], token_t[:, pair, :], start=True, stop=True)
                pe.matmul(ps[5][:, pair, :], pair_w[:, 1, :], token_t[:, pair, :], start=True, stop=True)
                last = pe.matmul(ps[6][:, pair, :], token_t[:, pair, :], pair_w[:, 2, :], start=True, stop=True)
            last.then_inc(pe_done, 1)
            pe.wait_ge(ready, 4)
            for pair in range(PAIRS):
                last = pe.matmul(ps[7][:, pair, :], query_t[:, pair, :], key_t[:, pair, :], start=True, stop=True)
            last.then_inc(pe_done, 1)
            pe.wait_ge(ready, 6)
            for pair in range(PAIRS):
                last = pe.transpose(ps[0][:, pair, :], attn[:, pair, :], ident[:, :])
            last.then_inc(pe_done, 1)
            pe.wait_ge(ready, 7)
            for pair in range(PAIRS):
                last = pe.matmul(ps[1][:, pair, :], value[:, pair, :], attn_t[:, pair, :], start=True, stop=True)
            last.then_inc(pe_done, 1)
            pe.wait_ge(ready, 8)
            for pair in range(PAIRS):
                out = ps[2 + pair // 2][:, :, :].rearrange("p a b -> p (a b)")
                last = pe.matmul(out[:, (pair % 2) * D:(pair % 2 + 1) * D], mixed_t[:, pair, :],
                                 wout_sb[:, pair, :], start=True, stop=True)
            last.then_inc(pe_done, 1)


def output_phase(nc, v):
    D, K2, PAIRS, TP, NT = (v[k] for k in ("D", "K2", "PAIRS", "TP", "NT"))
    x_sb, wt_sb, q_sb, bout_bc, out = v["x_sb"], v["wt_sb"], v["q_sb"], v["bout_bc"], v["out"]
    with ExitStack() as ctx:
        def sb(name, shape, dt=F32):
            return ctx.enter_context(nc.sbuf_tensor(name, shape, dt))

        def sem(name):
            return ctx.enter_context(nc.semaphore(name))

        here = sb("here", [P, 2, PAIRS, TP])
        done = sb("done", [TP, 2, D])
        sum_ps = [ctx.enter_context(nc.psum_tensor(f"sum_ps{j}", [TP, D], F32)) for j in range(2)]
        here_ready, mixed, biased, done_ready = sem("here_ready"), sem("mixed"), sem("biased"), sem("done_ready")
        stored = [sem(f"out_stored{j}") for j in range(2)]
        block = ctx.enter_context(nc.Block())

        @block.scalar
        def _(act):
            with act.Fori(0, NT // 2) as turn:
                t = turn * 2
                for j in range(2):
                    act.wait_ge(mixed, t + (j + 1))
                    act.activation(here[:, j, :, :], wt_sb[:, t + j, :, :], ACT.Copy).then_inc(here_ready, 1)

        @block.gpsimd
        def _(pool):
            with pool.Fori(0, NT // 2) as turn:
                t = turn * 2
                for j in range(2):
                    pool.tensor_tensor(x_sb[:, t + j, :], x_sb[:, t + j, :], bout_bc[0:TP, :],
                                       ALU.add).then_inc(biased, 1)

        @block.tensor
        def _(pe):
            pe.nop().then_inc(mixed, 2)
            with pe.Fori(0, NT // 2) as turn:
                t = turn * 2
                for j in range(2):
                    pe.wait_ge(here_ready, t + (j + 1))
                    pe.wait_ge(done_ready, t + (j + 1))
                    for k in range(PAIRS):
                        last = pe.matmul(sum_ps[j][:, :], here[:, j, k, :], q_sb[:, k, :], start=(k == 0),
                                         stop=(k == PAIRS - 1))
                    last.then_inc(mixed, 1)

        @block.vector
        def _(dve):
            dve.nop().then_inc(done_ready, 2)
            with dve.Fori(0, NT // 2) as turn:
                t = turn * 2
                for j in range(2):
                    dve.wait_ge(mixed, t + (j + 3))
                    dve.wait_ge(biased, t + (j + 1))
                    dve.wait_ge(stored[j], t * 8 + 16)
                    dve.tensor_tensor(done[:, j, :], sum_ps[j][:, :], x_sb[:, t + j, :],
                                      ALU.add).then_inc(done_ready, 1)

        @block.sync
        def _(sp):
            for j in range(2):
                sp.nop().then_inc(stored[j], 16)
            with sp.Fori(0, NT // 2) as turn:
                t = turn * 2
                for j in range(2):
                    sp.wait_ge(done_ready, t + (j + 3))
                    sp.dma_start(out[bass.ds(t * TP + j * TP, TP), :], done[:, j, :]).then_inc(stored[j], 16)
            for j in range(2):
                sp.wait_ge(stored[j], 16 * (NT // 2) + 16)


_INS = ["x", "src", "dst", "edge_weight", "L0_ffn_W_fx", "L0_ffn_b_fx", "L0_ffn_W_x", "L0_ffn_b_x",
        "L0_ffn_W_slice", "L0_ffn_b_slice", "L0_ffn_W_q", "L0_ffn_W_k", "L0_ffn_W_v", "L0_ffn_W_out",
        "L0_ffn_b_out", "L0_ffn_temperature"]


def kernel(**inputs):
    import numpy as np
    import concourse.bacc as bacc
    from concourse.bass_utils import run_bass_kernel_spmd

    nc = bacc.Bacc("TRN2", target_bir_lowering=False, num_devices=1)
    arrays, args = {}, []
    for name in _INS:
        a = np.ascontiguousarray(inputs[name])
        arrays["in_" + name] = a
        args.append(nc.dram_tensor("in_" + name, a.shape, mybir.dt.from_np(a.dtype), kind="ExternalInput").ap())
    out = nc.dram_tensor("out_x", inputs["x"].shape, F32, kind="ExternalOutput").ap()
    build(nc, *args, out)
    r = run_bass_kernel_spmd(nc, [arrays], core_ids=[0])
    return r.results[0]["out_x"]
```

```python
from contextlib import ExitStack

import concourse.bass as bass
from concourse import mybir

F32 = mybir.dt.float32
I32 = mybir.dt.int32
I16 = mybir.dt.int16
BF16 = mybir.dt.bfloat16
ALU = mybir.AluOpType
ACT = mybir.ActivationFunctionType
AX = mybir.AxisListType

P = 128
ROUND = 1.5 * 2.0 ** 23
TWO_PI = 6.283185307179586
PI_LOW = 3.1415925
TWO_PI_A, TWO_PI_B = 6.28125, 0.0019350051879882812
TWO_PI_C = TWO_PI - TWO_PI_A - TWO_PI_B
EPS = 1e-5


class Chain:

    def __init__(self, engine, sem):
        self.engine, self.sem, self.n, self.turn, self.per = engine, sem, 0, None, 0

    def loop(self, turn, per):
        self.base, self.turn, self.per, self.n = self.n, turn, per, 0

    def mark(self, instruction):
        self.n += 1
        instruction.then_inc(self.sem, 1)

    def settle(self):
        at = self.n if self.turn is None else self.turn * self.per + (self.base + self.n)
        self.engine.wait_ge(self.sem, at)

    def link(self, instruction):
        self.mark(instruction)
        self.settle()

    def close(self, turns):
        self.n, self.turn = self.base + self.per * turns, None


def divisor(n, limit=P):
    return max(k for k in range(1, limit + 1) if n % k == 0)


def build(nc, x, src, dst, theta, w_fx, b_fx, w_x, b_x, w_slice, b_slice, w_q, w_k, w_v, w_out, b_out,
          temperature, out):
    N, D = x.shape
    EDGES = src.shape[0]
    INNER = w_fx.shape[1]
    G = w_slice.shape[0]
    H = INNER // G
    K2 = D // P
    PAIRS = INNER // P
    ROWS = divisor(EDGES)
    STEPS = EDGES // ROWS
    TERMS = 2 * STEPS
    TABLE = ROWS * TERMS
    TP = divisor(N)
    NT = N // TP
    GB = 4
    OVERLAP = P - 1
    LEVELS = 7
    GROUP_RANKS = GB * OVERLAP
    MAX_GROUPS = (TABLE - 1) // GROUP_RANKS + 1
    SHIFTS = (TERMS - 1).bit_length()

    with ExitStack() as whole:
        def keep(name, shape, dt=F32):
            return whole.enter_context(nc.sbuf_tensor(name, shape, dt))

        x_sb = keep("x_sb", [TP, NT, D])
        iota_row = keep("iota_row", [P, D])
        pcol = keep("pcol", [P, 1])
        ident = keep("ident", [P, P])
        mat_t = keep("mat_t", [P, K2, D])
        wxs = keep("wxs", [P, K2, INNER])
        bias_bc = keep("bias_bc", [P, INNER])
        wfx_sb = keep("wfx_sb", [P, K2, INNER])
        bfx_bc = keep("bfx_bc", [P, INNER])
        wout_sb = keep("wout_sb", [P, PAIRS, D])
        bout_bc = keep("bout_bc", [P, D])
        pair_w = keep("pair_w", [P, 3, P])
        ones_row = keep("ones_row", [1, P])
        neg_mean = keep("neg_mean", [TP, NT])
        scale1 = keep("scale1", [TP, NT])
        shift1 = keep("shift1", [TP, NT])
        minus_half = keep("minus_half", [TP, NT])

        d_table = nc.dram_tensor("d_table", [TABLE, 1], I32, kind="Internal")
        term_table = nc.dram_tensor("term_table", [TABLE, 4], F32, kind="Internal")

        with ExitStack() as rot:
            def keep2(name, shape, dt=F32):
                return rot.enter_context(nc.sbuf_tensor(name, shape, dt))

            ident_bf = keep2("ident_bf", [P, P], BF16)
            strict = keep2("strict", [P, P])
            neg_sub = keep2("neg_sub", [P, P])
            same_square = keep2("same_square", [P, LEVELS - 1, P])
            first_mask = keep2("first_mask", [P, 1])
            second_mask = keep2("second_mask", [P, 1])
            rank = keep2("rank", [P, GB])
            row_start = keep2("row_start", [P, ROWS + 1])
            row_gap = keep2("row_gap", [P, ROWS + 1])
            groups_i = keep2("groups_i", [1, 1], I32)

            edges_phase(nc, locals())
            rotations_phase(nc, locals())
        with ExitStack() as after:
            def keep3(name, shape, dt=F32):
                return after.enter_context(nc.sbuf_tensor(name, shape, dt))

            wt_sb = keep3("wt_sb", [P, NT, PAIRS, TP])
            z_sb = keep3("z_sb", [P, PAIRS, D])
            norm_sb = keep3("norm_sb", [P, PAIRS])
            tokens_phase(nc, locals())
            q_sb = keep3("q_sb", [P, PAIRS, D])
            slices_phase(nc, locals())
            output_phase(nc, locals())


def edges_phase(nc, v):
    ROWS, STEPS, TERMS, TABLE = v["ROWS"], v["STEPS"], v["TERMS"], v["TABLE"]
    D, LEVELS, SHIFTS = v["D"], v["LEVELS"], v["SHIFTS"]
    GB, OVERLAP, TP, NT = v["GB"], v["OVERLAP"], v["TP"], v["NT"]
    x, src, dst, theta = v["x"], v["src"], v["dst"], v["theta"]
    x_sb, iota_row, pcol, ident = v["x_sb"], v["iota_row"], v["pcol"], v["ident"]
    ident_bf, strict, neg_sub, same_square = v["ident_bf"], v["strict"], v["neg_sub"], v["same_square"]
    first_mask, second_mask, rank = v["first_mask"], v["second_mask"], v["rank"]
    row_start, row_gap, groups_i = v["row_start"], v["row_gap"], v["groups_i"]
    d_table, term_table = v["d_table"], v["term_table"]
    INNER, G, H, K2, PAIRS = v["INNER"], v["G"], v["H"], v["K2"], v["PAIRS"]
    wxs, bias_bc, pair_w, ones_row = v["wxs"], v["bias_bc"], v["pair_w"], v["ones_row"]
    neg_mean, scale1, minus_half = v["neg_mean"], v["scale1"], v["minus_half"]

    TILES = divisor(NT, 10)
    OTHERS = NT // TILES // 5 * TILES
    FIRSTS = NT - OTHERS

    with ExitStack() as ctx:
        def sb(name, shape, dt=F32):
            return ctx.enter_context(nc.sbuf_tensor(name, shape, dt))

        def sem(name):
            return ctx.enter_context(nc.semaphore(name))

        src_i = sb("src_i", [ROWS, STEPS], I32)
        dst_i = sb("dst_i", [ROWS, STEPS], I32)
        th = sb("th", [ROWS, STEPS])
        src_f = sb("src_f", [ROWS, STEPS])
        dst_f = sb("dst_f", [ROWS, STEPS])
        turns = sb("turns", [ROWS, STEPS])
        sine = sb("sine", [ROWS, STEPS])
        half_sine = sb("half_sine", [ROWS, STEPS])
        valid = sb("valid", [ROWS, STEPS, 2])
        record = sb("record", [ROWS, STEPS, 2, 4])
        count = sb("count", [ROWS, TERMS])
        place = sb("place", [ROWS, TERMS])
        shift_d = sb("shift_d", [ROWS, TERMS], I16)
        moved = sb("moved", [ROWS, TERMS], I16)
        shift_done = sb("shift_done", [ROWS, TERMS], I32)
        row_i = sb("row_i", [P, P], I32)
        col_i = sb("col_i", [P, P], I32)
        pcol_i = sb("pcol_i", [P, 1], I32)
        is_last = sb("is_last", [P, 1])
        is_first = sb("is_first", [P, 1])
        before = sb("before", [P, ROWS + 1])
        follows = sb("follows", [P, ROWS + 1])
        total_bc = sb("total_bc", [ROWS, P])
        groups_f = sb("groups_f", [1, 1])
        offsets_ps = ctx.enter_context(nc.psum_tensor("offsets_ps", [P, 512], F32))
        counts_ps = ctx.enter_context(nc.psum_tensor("counts_ps", [P, 512], F32))

        indices_loaded, angles_loaded, x_loaded = sem("indices_loaded"), sem("angles_loaded"), sem("x_loaded")
        iotas, dve_chain, reduced, sines = sem("iotas"), sem("dve_chain_1"), sem("reduced"), sem("sines")
        totals_ready, offsets_ready = sem("totals_ready"), sem("offsets_ready")
        shifts_ready, records_ready, stored = sem("shifts_ready"), sem("records_ready"), sem("stored")

        wx_sb = sb("wx_sb", [P, K2, INNER])
        wxt_sb = sb("wxt_sb", [P, PAIRS, D])
        pair_slice = sb("pair_slice", [P, P])
        bx_col = sb("bx_col", [P, PAIRS])
        bs_row = sb("bs_row", [1, G])
        temp_row = sb("temp_row", [1, H])
        temp_inv = sb("temp_inv", [1, INNER])
        temp_inv_bc = sb("temp_inv_bc", [P, INNER])
        bias_row = sb("bias_row", [1, INNER])
        squares = sb("squares", [TP, TILES, D])
        stats = sb("stats_1", [TP, TILES, 6])
        both = sb("both_1", [TP, TILES, 2])
        turn_ps = ctx.enter_context(nc.psum_tensor("turn_ps", [P, 2, 2, D], F32))
        wxs_ps = [ctx.enter_context(nc.psum_tensor(f"wxs_ps{k}", [P, INNER], F32)) for k in range(K2)]
        brow_ps = ctx.enter_context(nc.psum_tensor("brow_ps", [1, INNER], F32))
        spread_ps = ctx.enter_context(nc.psum_tensor("spread_ps", [P, INNER], F32))
        loaded, zeroed, ident_ready = sem("loaded"), sem("zeroed"), sem("ident_ready")
        turned, turned_copied, temp_ready, temp_bc = (sem("turned"), sem("turned_copied"), sem("temp_ready"),
                                                      sem("temp_bc"))
        temp_bc_copied, products = sem("temp_bc_copied"), sem("products")
        bias_ready, bias_spread = sem("bias_ready"), sem("bias_spread")
        act_chain, pool_chain = sem("act_chain_1"), sem("pool_chain_1")
        sums_ready, mean_ready, stats_begun = sem("sums_ready"), sem("mean_ready"), sem("stats_begun_1")
        LOADS = 16
        assert TERMS < 2 ** 15 and NT % TILES == 0
        block = ctx.enter_context(nc.Block())

        def row(a):
            return a.rearrange("(a n) -> a n", a=1)

        @block.sync
        def _(sp):
            sp.dma_start(src_i[:, :], src.rearrange("(p f) -> p f", p=ROWS)).then_inc(indices_loaded, 16)
            sp.dma_start(dst_i[:, :], dst.rearrange("(p f) -> p f", p=ROWS)).then_inc(indices_loaded, 16)
            sp.dma_start(th[:, :], theta.rearrange("(p f) -> p f", p=ROWS)).then_inc(angles_loaded, 16)
            loads = [(wx_sb[:, :, :], v["w_x"].rearrange("(k p) n -> p k n", p=P)),
                     (v["wfx_sb"][:, :, :], v["w_fx"].rearrange("(k p) n -> p k n", p=P)),
                     (v["wout_sb"][:, :, :], v["w_out"].rearrange("(k p) n -> p k n", p=P)),
                     (bx_col[:, :], v["b_x"].rearrange("(k p) -> p k", p=P)),
                     (bs_row[:, :], row(v["b_slice"])),
                     (temp_row[:, :], v["temperature"].rearrange("a h b c -> a (h b c)")),
                     (v["bfx_bc"][:, :], row(v["b_fx"]).to_broadcast([P, INNER])),
                     (v["bout_bc"][:, :], row(v["b_out"]).to_broadcast([P, D]))]
            for to, of in loads:
                sp.dma_start(to, of, allow_slow_non_contiguous=True).then_inc(loaded, 16)
            sp.wait_ge(zeroed, 1)
            for half in range(2):
                at = slice(half * G, (half + 1) * G)
                sp.dma_start(pair_slice[at, at], v["w_slice"]).then_inc(loaded, 16)
                for m, w in enumerate(("w_q", "w_k", "w_v")):
                    sp.dma_start(pair_w[at, m, at], v[w]).then_inc(loaded, 16)
            sp.dma_start(x_sb[:, :, :], x.rearrange("(t p) d -> p t d", p=TP)).then_inc(x_loaded, 16)
            sp.wait_ge(records_ready, 1)
            sp.dma_start(term_table.rearrange("(p f) c -> p (f c)", p=ROWS),
                         record[:, :, :, :].rearrange("p s t c -> p (s t c)")).then_inc(stored, 16)
            sp.wait_ge(shifts_ready, 1)
            sp.dma_start(d_table.rearrange("(p f) c -> p (f c)", p=ROWS), shift_done[:, :]).then_inc(stored, 16)
            sp.wait_ge(stored, 32)
            sp.wait_ge(x_loaded, 16)

        @block.gpsimd
        def _(pool):
            link = Chain(pool, pool_chain).link
            pool.memset(pair_w[:, :, :], 0.0)
            pool.memset(ones_row[:, :], 1.0)
            pool.memset(minus_half[:, :], -0.5)
            link(pool.memset(pair_slice[:, :], 0.0))
            pool.sem_inc(zeroed, 1)
            pool.iota(row_i[:, :], [[1, P]], base=0, channel_multiplier=0).then_inc(iotas, 1)
            pool.iota(col_i[:, :], [[0, P]], base=0, channel_multiplier=1).then_inc(iotas, 1)
            pool.iota(pcol_i[:, :], [[1, 1]], base=0, channel_multiplier=1).then_inc(iotas, 1)
            pool.iota(iota_row[:, :], [[1, D]], base=0, channel_multiplier=0,
                      allow_small_or_imprecise_dtypes=True).then_inc(iotas, 1)
            pool.iota(rank[:, :], [[OVERLAP, GB]], base=0, channel_multiplier=1,
                      allow_small_or_imprecise_dtypes=True).then_inc(iotas, 1)
            pool.iota(place[:, :], [[1, TERMS]], base=1, channel_multiplier=0,
                      allow_small_or_imprecise_dtypes=True).then_inc(iotas, 1)
            pool.wait_ge(sums_ready, 1)
            link(pool.tensor_scalar(neg_mean[:, 0:FIRSTS], neg_mean[:, 0:FIRSTS], -1.0 / D, None,
                                    ALU.mult))
            pool.sem_inc(mean_ready, 1)

        @block.vector
        def _(dve):
            c = Chain(dve, dve_chain)
            link = c.link
            dve.wait_ge(iotas, 6)
            link(dve.tensor_copy(pcol[:, :], pcol_i[:, :]))
            link(dve.tensor_scalar(ident[:, :], iota_row[:, 0:P], pcol[:, 0:1], None, ALU.is_equal))
            dve.tensor_copy(ident_bf[:, :], ident[:, :]).then_inc(ident_ready, 1)
            dve.tensor_scalar(is_last[:, :], pcol[:, :], float(P - 1), None, ALU.is_equal)
            dve.tensor_scalar(is_first[:, :], pcol[:, :], 0.0, None, ALU.is_equal)
            dve.tensor_scalar(first_mask[:, :], pcol[:, :], float(P - 1), None, ALU.is_lt)
            dve.tensor_scalar(before[:, :], iota_row[:, 0:ROWS + 1], pcol[:, 0:1], None, ALU.is_gt)
            link(dve.tensor_scalar(strict[:, :], iota_row[:, 0:P], pcol[:, 0:1], None, ALU.is_lt))
            dve.tensor_tensor(second_mask[:, :], is_last[:, :], is_first[:, :], ALU.subtract)
            dve.tensor_scalar(follows[:, :], iota_row[:, 0:ROWS + 1], 1.0, pcol[:, 0:1], ALU.subtract,
                              ALU.is_equal)
            link(dve.tensor_scalar(neg_sub[:, :], iota_row[:, 0:P], 1.0, pcol[:, 0:1], ALU.add, ALU.is_equal))
            link(dve.tensor_scalar(neg_sub[:, :], neg_sub[:, :], -1.0, None, ALU.mult))
            link(dve.tensor_tensor(row_i[:, :], row_i[:, :], col_i[:, :], ALU.bitwise_xor))
            for level in range(1, LEVELS):
                dve.tensor_scalar(same_square[:, level - 1, :], row_i[:, :], float(2 ** level), None, ALU.is_lt)

            dve.wait_ge(indices_loaded, 32)
            dve.tensor_copy(src_f[:, :], src_i[:, :])
            link(dve.tensor_copy(dst_f[:, :], dst_i[:, :]))
            dve.tensor_tensor(turns[:, :], src_f[:, :], dst_f[:, :], ALU.not_equal)
            link(dve.tensor_scalar(valid[:, :, 1], dst_f[:, :], float(D), None, ALU.is_lt))
            link(dve.scalar_tensor_tensor(valid[:, :, 0], src_f[:, :], float(D), turns[:, :],
                                          ALU.is_lt, ALU.mult))
            flat_valid = valid[:, :, :].rearrange("p s t -> p (s t)")
            link(dve.tensor_tensor_scan(count[:, :], flat_valid, flat_valid, 0.0, ALU.add, ALU.max))
            link(dve.tensor_copy(total_bc[:, :], count[:, TERMS - 1:TERMS].to_broadcast([ROWS, P])))
            dve.tensor_copy(follows[:, :], follows[:, :]).then_inc(totals_ready, 1)
            link(dve.tensor_tensor(count[:, :], place[:, :], count[:, :], ALU.subtract))
            link(dve.tensor_tensor(shift_d[:, :], count[:, :], flat_valid, ALU.mult))

            dve.wait_ge(loaded, 16 * LOADS)
            link(dve.tensor_scalar(temp_row[:, :], temp_row[:, :], 0.1, 5.0, ALU.max, ALU.min))
            link(dve.reciprocal(temp_row[:, :], temp_row[:, :]))
            dve.tensor_copy(temp_inv[:, :].rearrange("a (h g) -> a h g", g=G),
                            temp_row[:, :].unsqueeze(2).to_broadcast([1, H, G])).then_inc(temp_ready, 1)

            dve.wait_ge(angles_loaded, 16)
            link(dve.tensor_scalar(turns[:, :], th[:, :], 1.0 / TWO_PI, ROUND, ALU.mult, ALU.add))
            link(dve.tensor_scalar(turns[:, :], turns[:, :], ROUND, None, ALU.subtract))
            for part in (TWO_PI_A, TWO_PI_B, TWO_PI_C):
                link(dve.scalar_tensor_tensor(th[:, :], turns[:, :], -part, th[:, :], ALU.mult, ALU.add))
            dve.tensor_scalar(th[:, :], th[:, :], PI_LOW, -PI_LOW, ALU.min, ALU.max).then_inc(reduced, 1)

            link(dve.tensor_scalar(src_f[:, :], src_f[:, :], float(D - 1), None, ALU.min))
            link(dve.tensor_scalar(dst_f[:, :], dst_f[:, :], float(D - 1), None, ALU.min))
            dve.tensor_copy(record[:, :, 0, 0], src_f[:, :])
            dve.tensor_copy(record[:, :, 0, 1], dst_f[:, :])
            dve.tensor_copy(record[:, :, 1, 1], src_f[:, :])
            link(dve.scalar_tensor_tensor(record[:, :, 1, 0], valid[:, :, 0], float(D), dst_f[:, :],
                                          ALU.mult, ALU.add))

            dve.wait_ge(products, 1)
            dve.wait_ge(temp_bc_copied, 1)
            for k in range(K2):
                dve.tensor_tensor(wxs[:, k, :], wxs_ps[k][:, :], temp_inv_bc[:, :], ALU.mult)
            link(dve.tensor_tensor(bias_row[:, :].rearrange("a (h g) -> a h g", g=G),
                                   brow_ps[:, :].rearrange("a (h g) -> a h g", g=G),
                                   bs_row[:, :].unsqueeze(1).to_broadcast([1, H, G]), ALU.add))
            dve.tensor_tensor(bias_row[:, :], bias_row[:, :], temp_inv[:, :], ALU.mult).then_inc(bias_ready, 1)

            def shift(level):
                by = 2 ** level
                link(dve.tensor_scalar(moved[:, :], shift_d[:, :], by, None, ALU.bitwise_and))
                link(dve.tensor_scalar(moved[:, :], moved[:, :], -1.0 / by, None, ALU.mult))
                link(dve.tensor_tensor(moved[:, :], moved[:, :], shift_d[:, :], ALU.bitwise_and))
                return dve.tensor_tensor(shift_d[:, 0:TERMS - by], shift_d[:, 0:TERMS - by],
                                         moved[:, by:TERMS], ALU.max)

            link(shift(0))
            dve.wait_ge(sines, 2)
            dve.tensor_scalar(record[:, :, 0, 3], sine[:, :], -1.0, None, ALU.mult)
            dve.tensor_copy(record[:, :, 1, 3], sine[:, :])
            link(dve.tensor_scalar(turns[:, :], half_sine[:, :], -2.0, None, ALU.mult))
            link(dve.tensor_tensor(record[:, :, 0, 2], turns[:, :], half_sine[:, :], ALU.mult))
            dve.tensor_copy(record[:, :, 1, 2], record[:, :, 0, 2]).then_inc(records_ready, 1)
            for level in range(1, SHIFTS):
                link(shift(level))
            dve.tensor_copy(shift_done[:, :], shift_d[:, :]).then_inc(shifts_ready, 1)

            dve.wait_ge(bias_spread, 1)
            dve.tensor_copy(bias_bc[:, :], spread_ps[:, :])
            dve.wait_ge(offsets_ready, 1)
            dve.tensor_copy(row_start[:, :], offsets_ps[:, 0:ROWS + 1])
            dve.tensor_scalar(row_gap[:, :], counts_ps[:, 0:ROWS + 1], -1.0, float(TERMS), ALU.mult, ALU.add)
            link(dve.tensor_scalar(groups_f[:, :], offsets_ps[0:1, ROWS:ROWS + 1], 1.0, 0.5,
                                   ALU.max, ALU.subtract))
            link(dve.tensor_scalar(groups_f[:, :], groups_f[:, :], 1.0 / (GB * OVERLAP), 0.5,
                                   ALU.mult, ALU.subtract))
            link(dve.tensor_scalar(groups_f[:, :], groups_f[:, :], ROUND, None, ALU.add))
            link(dve.tensor_scalar(groups_i[:, :], groups_f[:, :], ROUND, 1.0, ALU.subtract, ALU.add))

            dve.wait_ge(x_loaded, 16)
            with dve.Fori(0, OTHERS // TILES) as turn:
                c.loop(turn, 3)
                dve.sem_inc(stats_begun, 1)
                for j in range(TILES):
                    last = dve.bn_stats(stats[:, j, :], x_sb[:, turn * TILES + (FIRSTS + j), :])
                c.link(last)
                dve.sem_inc(stats_begun, 1)
                for j in range(TILES):
                    last = dve.bn_aggr(both[:, j, :], stats[:, j, :])
                c.link(last)
                at = bass.ds(turn * TILES + FIRSTS, TILES)
                dve.tensor_scalar(neg_mean[:, at], both[:, :, 0], -1.0, None, ALU.mult)
                c.mark(dve.tensor_scalar(scale1[:, at], both[:, :, 1], float(D), None, ALU.mult))

        @block.scalar
        def _(act):
            act.wait_ge(turned, K2)
            act.activation(wxt_sb[:, :, :], turn_ps[:, :, :, :].rearrange("p a b d -> p (a b) d"),
                           ACT.Copy).then_inc(turned_copied, 1)
            act.wait_ge(temp_bc, 1)
            act.activation(temp_inv_bc[:, :], spread_ps[:, :], ACT.Copy).then_inc(temp_bc_copied, 1)
            c = Chain(act, act_chain)
            act.wait_ge(reduced, 1)
            act.activation(sine[:, :], th[:, :], ACT.Sin).then_inc(sines, 1)
            act.activation(half_sine[:, :], th[:, :], ACT.Sin, scale=0.5).then_inc(sines, 1)
            act.wait_ge(x_loaded, 16)
            with act.Fori(0, FIRSTS // TILES) as turn:
                c.loop(turn, 1)
                for j in range(TILES):
                    t = turn * TILES + j
                    last = act.activation(squares[:, j, :], x_sb[:, t, :], ACT.Copy,
                                          accum_out=neg_mean[:, bass.ds(t, 1)])
                c.link(last)
            c.close(FIRSTS // TILES)
            act.sem_inc(sums_ready, 1)
            act.wait_ge(mean_ready, 1)
            with act.Fori(0, FIRSTS // TILES) as turn:
                c.loop(turn, 1)
                for j in range(TILES):
                    t = turn * TILES + j
                    last = act.activation(squares[:, j, :], x_sb[:, t, :], ACT.Square,
                                          bias=neg_mean[:, bass.ds(t, 1)], accum_out=scale1[:, bass.ds(t, 1)])
                c.link(last)

        @block.tensor
        def _(pe):
            pe.wait_ge(ident_ready, 1)
            pe.wait_ge(loaded, 16 * LOADS)
            for k in range(K2):
                for pair in range(PAIRS):
                    last = pe.transpose(turn_ps[:, pair // 2, pair % 2, k * P:(k + 1) * P],
                                        wx_sb[:, k, pair * P:(pair + 1) * P], ident[:, :])
                last.then_inc(turned, 1)
            pe.wait_ge(temp_ready, 1)
            pe.matmul(spread_ps[:, :], ones_row[:, :], temp_inv[:, :], start=True, stop=True).then_inc(temp_bc, 1)
            pe.wait_ge(turned_copied, 1)
            for pair in range(PAIRS):
                at = slice(pair * P, (pair + 1) * P)
                for k in range(K2):
                    pe.matmul(wxs_ps[k][:, at], wxt_sb[:, pair, k * P:(k + 1) * P], pair_slice[:, :],
                              start=True, stop=True)
                last = pe.matmul(brow_ps[:, at], bx_col[:, pair:pair + 1], pair_slice[:, :], start=True, stop=True)
            last.then_inc(products, 1)
            pe.wait_ge(totals_ready, 1)
            pe.matmul(offsets_ps[:, 0:ROWS + 1], total_bc[:, :], before[0:ROWS, :], start=True, stop=True)
            pe.matmul(counts_ps[:, 0:ROWS + 1], total_bc[:, :], follows[0:ROWS, :], start=True,
                      stop=True).then_inc(offsets_ready, 1)
            pe.wait_ge(bias_ready, 1)
            pe.wait_ge(temp_bc_copied, 1)
            pe.matmul(spread_ps[:, :], ones_row[:, :], bias_row[:, :], start=True, stop=True).then_inc(bias_spread, 1)


def rotations_phase(nc, v):
    D, GB, K2, ROWS, LEVELS = v["D"], v["GB"], v["K2"], v["ROWS"], v["LEVELS"]
    TABLE, MAX_GROUPS, GROUP_RANKS = v["TABLE"], v["MAX_GROUPS"], v["GROUP_RANKS"]
    iota_row, pcol, ident, mat_t = v["iota_row"], v["pcol"], v["ident"], v["mat_t"]
    ident_bf, strict, neg_sub, same_square = v["ident_bf"], v["strict"], v["neg_sub"], v["same_square"]
    first_mask, second_mask, rank = v["first_mask"], v["second_mask"], v["rank"]
    row_start, row_gap, groups_i = v["row_start"], v["row_gap"], v["groups_i"]
    d_table, term_table = v["d_table"], v["term_table"]
    neg_mean, scale1, shift1, minus_half = v["neg_mean"], v["scale1"], v["shift1"], v["minus_half"]
    UP = LEVELS - 1
    HALF = P // 2
    TARGET, OTHER, AT_TARGET, AT_OTHER = range(4)
    TWOS = GB // 2
    AHEAD = 2
    READ, WRITE = "read", "write"
    SLOTS = [(step, b) for b in range(GB) for step in (READ, (WRITE, 0), (WRITE, 1))]
    assert GB % 2 == 0 and P == 2 * HALF and len(SLOTS) == 2 * UP and K2 == 2

    with ExitStack() as ctx:
        def sb(name, shape, dt=F32):
            return ctx.enter_context(nc.sbuf_tensor(name, shape, dt))

        def ps(name, shape):
            return ctx.enter_context(nc.psum_tensor(name, shape, F32))

        def sem(name):
            return ctx.enter_context(nc.semaphore(name))

        index_f = sb("index_f", [P, GB])
        index_i = sb("index_i", [P, GB], I32)
        gathered_d = sb("gathered_d", [P, GB], I32)
        term_f = sb("term_f", [P, GB])
        term_i = sb("term_i", [P, GB], I32)
        raw = sb("raw", [P, GB, 4])
        look = sb("look", [P, GB, ROWS - 1])
        look_sum = sb("look_sum", [P, GB])
        second = sb("second", [P, GB])
        active = sb("active", [P, GB])
        present = sb("present", [P, GB])
        fresh = sb("fresh", [P, 4, GB])
        held = sb("held", [P, 4, GB])
        target_bc = sb("target_bc", [P, GB, P], BF16)
        vt = sb("vt", [P, GB, D])
        vt_other = sb("vt_other", [P, GB, D])
        lower = sb("lower", [P, GB, P])
        lower_other = sb("lower_other", [P, GB, P])
        lower_mask = sb("lower_mask", [P, GB, P])
        lower_next = sb("lower_next", [P, GB, P])
        lower_left = [sb(f"lower_left{k}", [P, TWOS * P]) for k in range(2)]
        t_sb = sb("t_sb", [P, TWOS, P])
        s_level = [sb(f"s_level{k}", [P, 2, TWOS * P]) for k in range(2)]
        s_sb = sb("s_sb", [P, GB, P])
        y_sb = sb("y_sb", [P, TWOS, P])
        rt_sb = sb("rt_sb", [P, K2, GB, P])
        u_next = sb("u_next", [P, GB, D])
        u_sb = sb("u_sb", [P, GB, D])
        w_sb = sb("w_sb", [P, D])
        m_sb = sb("m_sb", [P, K2, D])

        target_ps = ps("target_ps", [P, GB, P])
        y_ps = ps("y_ps", [P, TWOS, 2 * P])
        s_ps = ps("s_ps", [P, GB * P])
        t_ps = ps("t_ps", [P, TWOS, 2 * P])
        rt_ps = [ps(f"rt_ps{h}", [P, GB, P]) for h in range(K2)]
        w_ps = ps("w_ps", [P, 2, D])
        m_ps = ps("m_ps", [P, K2, D])

        chain, pool_chain, gathers_begun = sem("dve_chain_2"), sem("pool_chain_2"), sem("gathers_begun")
        index_ready, d_gathered = sem("index_ready"), sem("d_gathered")
        term_ready, raw_gathered = sem("term_ready"), sem("raw_gathered")
        decoded, target_bc_ready, targets_done = sem("decoded"), sem("target_bc_ready"), sem("targets_done")
        vt_ready, entries_ready, entries_added = sem("vt_ready"), sem("entries_ready"), sem("entries_added")
        lower_ready, lefts_ready, u_next_ready = sem("lower_ready"), sem("lefts_ready"), sem("u_next_ready")
        gathered, held_ready, others_ready = sem("gathered"), sem("held_ready"), sem("others_ready")
        y_done, s_done, t_done = sem("y_done"), sem("s_done"), sem("t_done")
        y_copied, s_ready, t_copied = sem("y_copied"), sem("s_ready"), sem("t_copied")
        rt_done, rt_ready, u_ready = sem("rt_done"), sem("rt_ready"), sem("u_ready")
        w_done, w_copied, m_done, m_ready = sem("w_done"), sem("w_copied"), sem("m_done"), sem("m_ready")
        mt_done = sem("mt_done")
        block = ctx.enter_context(nc.Block())

        def groups(engine):
            return engine.value_load(groups_i[0:1, 0:1], min_val=1, max_val=MAX_GROUPS)

        def level_columns(a, level, side):
            w = 2 ** level
            return a.rearrange("p (n two w) -> p n two w", two=2, w=w)[:, :, side, :]

        def next_level(level, half):
            w = 2 ** level
            if level < UP:
                return s_level[(level + 1) % 2].rearrange("p side (n half w) -> p n side half w",
                                                          half=2, w=w)[:, :, :, half, :]
            return s_sb.rearrange("p b (half w) -> p b half w", half=2)[:, :, half, :]

        def like_next(a, level):
            w = 2 ** level
            if level < UP:
                return a.rearrange("p (n side w) -> p n side w", side=2, w=w)
            return a.rearrange("p (b w) -> p b w", w=w)

        def ident_columns(parity):
            return (ident.rearrange("p (n side two) -> p n side two", side=2, two=2)[:, :, :, parity]
                    .unsqueeze(1).to_broadcast([P, GB, P // 4, 2]))

        @block.gpsimd
        def _(pool):
            def gather_d(group):
                pool.wait_ge(index_ready, group + 1)
                pool.sem_inc(gathers_begun, 1)
                for b in range(GB):
                    pool.indirect_dma_start(
                        out=gathered_d[:, b:b + 1], out_offset=None, in_=d_table[:, :],
                        in_offset=bass.IndirectOffsetOnAxis(ap=index_i[:, b:b + 1], axis=0)
                    ).then_inc(d_gathered, 16)

            def gather_terms(group):
                pool.wait_ge(term_ready, group + 1)
                if not (isinstance(group, int) and group == 0):
                    pool.wait_ge(decoded, group)
                pool.sem_inc(gathers_begun, 1)
                for b in range(GB):
                    pool.indirect_dma_start(
                        out=raw[:, b, :], out_offset=None, in_=term_table[:, :],
                        in_offset=bass.IndirectOffsetOnAxis(ap=term_i[:, b:b + 1], axis=0)
                    ).then_inc(raw_gathered, 16)

            def vectors_others():
                pool.sem_inc(gathers_begun, 1)
                for b in range(GB):
                    last = pool.tensor_scalar(vt_other[:, b, :], iota_row[:, :], held[:, OTHER, b:b + 1],
                                              held[:, AT_OTHER, b:b + 1], ALU.is_equal, ALU.mult)
                last.then_inc(others_ready, 1)

            n = groups(pool)
            pool.memset(u_next[:, :, :], 0.0).then_inc(u_next_ready, 1)
            pool.memset(rt_sb[:, :, :, :], 0.0).then_inc(rt_ready, 1)
            gather_d(0)
            gather_terms(0)
            gather_d(1)
            gather_terms(1)
            gather_d(2)
            with pool.Fori(0, n) as i:
                pool.wait_ge(held_ready, i + 1)
                vectors_others()
                gather_terms(i + 2)
                gather_d(i + 3)
                pool.wait_ge(entries_ready, i + 1)
                pool.tensor_tensor(lower_next[:, :, :], lower_next[:, :, :], lower_other[:, :, :],
                                   ALU.add).then_inc(entries_added, 1)
                pool.wait_ge(entries_added, i + 1)
                pool.wait_ge(gathered, i * UP + UP)
                pool.tensor_tensor(lower[:, :, :], lower_next[:, :, :], lower_mask[:, :, :],
                                   ALU.mult).then_inc(lower_ready, 1)
            pool.wait_ge(raw_gathered, n * (16 * GB) + 2 * 16 * GB)
            pool.wait_ge(d_gathered, n * (16 * GB) + 3 * 16 * GB)
            pool.sem_inc(gathers_begun, 1)
            pool_link = Chain(pool, pool_chain).link
            pool_link(pool.tensor_scalar(scale1[:, :], scale1[:, :], 1.0 / D, EPS, ALU.mult, ALU.add))
            pool_link(pool.tensor_tensor(scale1[:, :], scale1[:, :], minus_half[:, :], ALU.pow))
            pool_link(pool.tensor_tensor(shift1[:, :], scale1[:, :], neg_mean[:, :], ALU.mult))

        @block.vector
        def _(dve):
            c = Chain(dve, chain)
            link = c.link

            def compare_rows(b):
                return dve.scalar_tensor_tensor(look[:, b, :], row_start[:, 1:ROWS], rank[:, b:b + 1],
                                                row_gap[:, 1:ROWS], ALU.is_le, ALU.mult,
                                                accum_out=look_sum[:, b:b + 1])

            def add_gaps():
                return dve.tensor_tensor(index_f[:, :], look_sum[:, :], rank[:, :], ALU.add)

            def limit_index():
                return dve.tensor_scalar(index_f[:, :], index_f[:, :], float(TABLE - 1), None, ALU.min)

            def index_done():
                dve.tensor_copy(index_i[:, :], index_f[:, :]).then_inc(index_ready, 1)

            def find_index():
                for b in range(GB):
                    last = compare_rows(b)
                link(last)
                link(add_gaps())
                link(limit_index())
                index_done()

            def find_term(group):
                dve.wait_ge(d_gathered, group * (16 * GB) + 16 * GB)
                return dve.tensor_tensor(term_f[:, :], index_f[:, :], gathered_d[:, :], ALU.add)

            def find_term_end():
                dve.tensor_scalar(term_i[:, :], term_f[:, :], float(TABLE - 1), None,
                                  ALU.min).then_inc(term_ready, 1)

            def decode_begin(group):
                dve.wait_ge(raw_gathered, group * (16 * GB) + 16 * GB)
                dve.tensor_scalar(present[:, :], rank[:, :], float(-AHEAD * GROUP_RANKS),
                                  row_start[:, ROWS:ROWS + 1], ALU.add, ALU.is_lt)
                dve.tensor_copy(fresh[:, OTHER, :], raw[:, :, 1])
                return dve.tensor_scalar(second[:, :], raw[:, :, 0], float(D), None, ALU.is_ge)

            def decode_target():
                dve.scalar_tensor_tensor(fresh[:, TARGET, :], second[:, :], float(-D), raw[:, :, 0],
                                         ALU.mult, ALU.add)
                return dve.tensor_scalar(active[:, :], second[:, :], second_mask[:, 0:1], first_mask[:, 0:1],
                                         ALU.mult, ALU.add)

            def decode_active():
                return dve.tensor_tensor(active[:, :], active[:, :], present[:, :], ALU.mult)

            def decode_end(group):
                dve.tensor_tensor(fresh[:, AT_TARGET:AT_OTHER + 1, :].rearrange("p c b -> p b c"),
                                  raw[:, :, 2:4], active[:, :].unsqueeze(2).to_broadcast([P, GB, 2]),
                                  ALU.mult).then_inc(decoded, 1)

            def next_ranks():
                link(dve.tensor_scalar(rank[:, :], rank[:, :], float(GROUP_RANKS), None, ALU.add))

            def lower_entries(b):
                dve.tensor_scalar(lower_next[:, b, :], target_ps[:, b, :], fresh[:, TARGET, b:b + 1],
                                  fresh[:, AT_TARGET, b:b + 1], ALU.is_equal, ALU.mult)
                return dve.tensor_scalar(lower_other[:, b, :], target_ps[:, b, :],
                                         fresh[:, OTHER, b:b + 1], fresh[:, AT_OTHER, b:b + 1],
                                         ALU.is_equal, ALU.mult)

            def lower_masks(b):
                return dve.scalar_tensor_tensor(lower_mask[:, b, :], neg_sub[:, :], second[:, b:b + 1],
                                                strict[:, :], ALU.mult, ALU.add)

            def first_level(i):
                dve.wait_ge(s_done, i * LEVELS + 1)
                odd = next_level(0, 1)[:, :, :, 0].rearrange("p (b n) side -> p b n side", b=GB)
                given = s_ps.rearrange("p (b n side two) -> p b n side two", b=GB, side=2, two=2)[:, :, :, :, 1]
                c.mark(dve.tensor_tensor(odd, given, ident_columns(0), ALU.mult))
                c.mark(dve.tensor_copy(held[:, :, :], fresh[:, :, :]))
                c.settle()
                dve.tensor_tensor(odd, odd, ident_columns(1), ALU.add).then_inc(s_ready, 1)

            def mask_y(i, level):
                dve.wait_ge(y_done, i * UP + level)
                dve.tensor_tensor(y_sb[:, :, :], y_ps[:, :, 0:P],
                                  same_square[:, level - 1, :].unsqueeze(1).to_broadcast([P, TWOS, P]),
                                  ALU.mult).then_inc(y_copied, 1)

            def grow(i, level):
                dve.wait_ge(s_done, i * LEVELS + (level + 1))
                dve.tensor_tensor(next_level(level, 1), like_next(s_level[level % 2][:, 1, :], level),
                                  like_next(s_ps[:, 0:TWOS * P], level), ALU.add).then_inc(s_ready, 1)

            def targets_rows(b):
                return dve.tensor_scalar(u_next[:, b, :], iota_row[:, :], held[:, TARGET, b:b + 1], None,
                                         ALU.is_equal)

            def vectors_rows(b):
                return dve.scalar_tensor_tensor(vt[:, b, :], u_next[:, b, :], held[:, AT_TARGET, b:b + 1],
                                                vt_other[:, b, :], ALU.mult, ALU.add)

            n = groups(dve)
            find_index()
            for h in range(K2):
                last = dve.tensor_scalar(m_sb[:, h, :], iota_row[:, :], float(-h * P), pcol[:, 0:1],
                                         ALU.add, ALU.is_equal)
            last.then_inc(m_ready, K2)
            next_ranks()
            link(find_term(0))
            find_term_end()
            find_index()
            next_ranks()
            link(decode_begin(0))
            link(decode_target())
            link(decode_active())
            decode_end(0)
            dve.wait_ge(decoded, 1)
            link(find_term(1))
            find_term_end()
            for b in range(GB):
                lower_masks(b)
            find_index()
            next_ranks()
            dve.wait_ge(targets_done, 1)
            for b in range(GB):
                last = lower_entries(b)
            link(last)
            link(dve.tensor_tensor(lower_next[:, :, :], lower_next[:, :, :], lower_other[:, :, :], ALU.add))
            link(dve.tensor_tensor(lower[:, :, :], lower_next[:, :, :], lower_mask[:, :, :], ALU.mult))
            dve.sem_inc(lower_ready, 1)
            first_level(0)
            dve.sem_inc(held_ready, 1)
            MARKS = 11
            with dve.Fori(0, n) as i:
                c.loop(i, MARKS)
                c.link(decode_begin(i + 1))
                c.mark(decode_target())
                compare_rows(0)
                c.settle()
                c.mark(decode_active())
                compare_rows(1)
                c.settle()
                decode_end(i + 1)

                mask_y(i, 1)
                c.mark(find_term(i + 2))
                compare_rows(2)
                c.settle()
                find_term_end()
                c.mark(compare_rows(3))
                grow(i, 1)
                dve.wait_ge(lower_ready, i + 1)
                c.settle()
                c.mark(add_gaps())
                lower_masks(0)
                c.settle()
                c.mark(limit_index())
                lower_masks(1)
                c.settle()
                index_done()

                mask_y(i, 2)
                next_ranks()
                lower_masks(2)
                lower_masks(3)
                grow(i, 2)
                dve.wait_ge(targets_done, i + 2)
                lower_entries(0)

                mask_y(i, 3)
                lower_entries(1)
                grow(i, 3)
                lower_entries(2)

                mask_y(i, 4)
                lower_entries(3).then_inc(entries_ready, 1)
                dve.wait_ge(u_ready, i * GB + GB)
                grow(i, 4)
                targets_rows(0)
                targets_rows(1)

                mask_y(i, 5)
                targets_rows(2)
                c.mark(targets_rows(3))
                grow(i, 5)
                c.settle()
                dve.sem_inc(u_next_ready, 1)
                dve.wait_ge(others_ready, i + 1)
                vectors_rows(0)
                vectors_rows(1)

                mask_y(i, 6)
                vectors_rows(2)
                vectors_rows(3).then_inc(vt_ready, 1)
                grow(i, 6)
                first_level(i + 1)
                dve.wait_ge(vt_ready, i + 1)
                dve.sem_inc(held_ready, 1)
                assert c.n == c.per, c.n
            dve.wait_ge(mt_done, 1)
            dve.tensor_copy(mat_t[:, :, :], w_ps[:, :, :])

        @block.scalar
        def _(act):
            def spread_targets(group):
                act.wait_ge(decoded, group + 1)
                act.activation(target_bc[:, :, :], fresh[:, TARGET, :].unsqueeze(2).to_broadcast([P, GB, P]),
                               ACT.Copy).then_inc(target_bc_ready, 1)

            def copy_applied(turn, slot, at_once=False):
                step, b = SLOTS[slot]
                if step == READ:
                    act.wait_ge(w_done, turn * GB + (b + 1))
                    act.activation(w_sb[:, :], w_ps[:, b % 2, :], ACT.Copy).then_inc(w_copied, 1)
                elif at_once:
                    if step == (WRITE, K2 - 1):
                        act.wait_ge(m_done, turn * (K2 * GB) + K2 * (b + 1))
                        act.activation(m_sb[:, :, :], m_ps[:, :, :], ACT.Copy).then_inc(m_ready, K2)
                else:
                    h = step[1]
                    act.wait_ge(m_done, turn * (K2 * GB) + (K2 * b + h + 1))
                    act.activation(m_sb[:, h, :], m_ps[:, h, :], ACT.Copy).then_inc(m_ready, 1)

            def gather_left(level):
                act.activation(lower_left[level % 2].rearrange("p (n w) -> p n w", w=2 ** level),
                               level_columns(lower.rearrange("p b k -> p (b k)"), level, 0),
                               ACT.Copy).then_inc(gathered, 1)

            def copy_u(turn, b):
                if b == 0:
                    act.wait_ge(u_next_ready, turn + 1)
                act.activation(u_sb[:, b, :], u_next[:, b, :], ACT.Copy).then_inc(u_ready, 1)

            def begin_group(group):
                even = next_level(0, 0)[:, :, :, 0].rearrange("p (b n) side -> p b n side", b=GB)
                act.activation(even, ident_columns(0), ACT.Copy).then_inc(lefts_ready, 1)
                act.wait_ge(lower_ready, group + 1)
                gather_left(1)

            def take_lefts(i, level):
                act.wait_ge(t_done, i * UP + level)
                act.activation(t_sb[:, :, :], t_ps[:, :, 0:P], ACT.Copy).then_inc(t_copied, 1)
                act.activation(next_level(level, 0), like_next(s_level[level % 2][:, 0, :], level),
                               ACT.Copy).then_inc(lefts_ready, 1)
                if level < UP:
                    gather_left(level + 1)

            n = groups(act)
            spread_targets(0)
            begin_group(0)
            take_lefts(0, 1)
            with act.Fori(0, n) as i:
                for level in range(1, LEVELS):
                    if level > 1:
                        take_lefts(i, level)
                        copy_applied(i, 2 * level - 3)
                    if level == 1:
                        spread_targets(i + 1)
                        copy_u(i, 0)
                    if level == 2:
                        copy_u(i, 1)
                        copy_u(i, 2)
                    if level == 3:
                        copy_u(i, 3)
                    copy_applied(i, 2 * level - 2)
                begin_group(i + 1)
                for h in range(K2):
                    act.wait_ge(rt_done, i * K2 + (h + 1))
                    last = act.activation(rt_sb[:, h, :, :], rt_ps[h][:, :, :], ACT.Copy)
                last.then_inc(rt_ready, 1)
                take_lefts(i + 1, 1)
                copy_applied(i, 2 * UP - 1)
            for b in range(GB):
                copy_u(n, b)
            for slot in range(2 * UP):
                copy_applied(n, slot, at_once=True)

        @block.tensor
        def _(pe):
            def spread_targets(group):
                pe.wait_ge(target_bc_ready, group + 1)
                for b in range(GB):
                    last = pe.matmul(target_ps[:, b, :], target_bc[:, b, :], ident_bf[:, :],
                                     start=True, stop=True)
                last.then_inc(targets_done, 1)

            def apply(turn, slot, at_once=False):
                step, b = SLOTS[slot]
                if step == READ:
                    if b == 0:
                        pe.wait_ge(rt_ready, turn + 1)
                    pe.wait_ge(m_ready, turn * (K2 * GB) + K2 * (b + 1))
                    for h in range(K2):
                        last = pe.matmul(w_ps[:, b % 2, :], rt_sb[:, h, b, :], m_sb[:, h, :],
                                         start=(h == 0), stop=(h == K2 - 1))
                    last.then_inc(w_done, 1)
                else:
                    h = step[1]
                    if h == 0:
                        pe.wait_ge(u_ready, turn * GB + (b + 1))
                        pe.wait_ge(w_copied, turn * GB + (b + 1))
                    elif not at_once:
                        pe.wait_ge(m_ready, turn * (K2 * GB) + (K2 * (b + 1) + 1))
                    pe.matmul(m_ps[:, h, :], u_sb[:, b, h * P:(h + 1) * P], w_sb[:, :], start=False,
                              stop=True, skip_group_check=True).then_inc(m_done, 1)

            def turn_lower(group):
                pe.wait_ge(lower_ready, group + 1)
                for b in range(GB):
                    last = pe.transpose(s_ps[:, b * P:(b + 1) * P], lower[:, b, :], ident[:, :])
                last.then_inc(s_done, 1)

            def level_products(i, level):
                pe.wait_ge(s_ready, i * LEVELS + level)
                pe.wait_ge(lefts_ready, i * LEVELS + level)
                for two in range(TWOS):
                    last = pe.transpose(t_ps[:, two, 0:P], s_level[level % 2][:, 0, two * P:(two + 1) * P],
                                        ident[:, :])
                last.then_inc(t_done, 1)
                pe.wait_ge(gathered, i * UP + level)
                for two in range(TWOS):
                    at = slice(two * P, (two + 1) * P)
                    last = pe.matmul(y_ps[:, two, 0:P], lower_left[level % 2][:, at],
                                     s_level[level % 2][:, 1, at], start=True, stop=True)
                last.then_inc(y_done, 1)

            def level_growth(i, level):
                pe.wait_ge(y_copied, i * UP + level)
                pe.wait_ge(t_copied, i * UP + level)
                for two in range(TWOS):
                    last = pe.matmul(s_ps[:, two * P:(two + 1) * P], t_sb[:, two, :], y_sb[:, two, :],
                                     start=True, stop=True)
                last.then_inc(s_done, 1)

            n = groups(pe)
            pe.wait_ge(m_ready, K2)
            pe.matmul(m_ps[:, :, :], ident[:, :], m_sb[:, :, :], start=True, stop=True)
            spread_targets(0)
            turn_lower(0)
            level_products(0, 1)
            with pe.Fori(0, n) as i:
                for level in range(1, LEVELS):
                    if level > 1:
                        level_products(i, level)
                    if level > 1:
                        apply(i, 2 * level - 3)
                    level_growth(i, level)
                    apply(i, 2 * level - 2)
                    if level == 2:
                        spread_targets(i + 1)
                pe.wait_ge(s_ready, i * LEVELS + LEVELS)
                turn_lower(i + 1)
                pe.wait_ge(lefts_ready, i * LEVELS + LEVELS)
                pe.wait_ge(vt_ready, i + 1)
                for h in range(K2):
                    for b in range(GB):
                        last = pe.matmul(rt_ps[h][:, b, :], vt[:, b, h * P:(h + 1) * P], s_sb[:, b, :],
                                         start=True, stop=True)
                    last.then_inc(rt_done, 1)
                level_products(i + 1, 1)
                apply(i, 2 * UP - 1)
            for slot in range(2 * UP):
                apply(n, slot, at_once=True)
            pe.wait_ge(m_ready, n * (K2 * GB) + (K2 * GB + K2))
            for h in range(K2):
                for g in range(K2):
                    last = pe.transpose(w_ps[:, g, h * P:(h + 1) * P], m_sb[:, h, g * P:(g + 1) * P],
                                        ident[:, :])
            last.then_inc(mt_done, 1)


def tokens_phase(nc, v):
    D, INNER, G, H, K2, PAIRS, TP, NT = (v[k] for k in ("D", "INNER", "G", "H", "K2", "PAIRS", "TP", "NT"))
    x_sb, ident, mat_t, minus_half = v["x_sb"], v["ident"], v["mat_t"], v["minus_half"]
    scale1, shift1 = v["scale1"], v["shift1"]
    wxs, bias_bc, wt_sb, z_sb, norm_sb = v["wxs"], v["bias_bc"], v["wt_sb"], v["z_sb"], v["norm_sb"]
    TURNS = NT // 2
    assert NT % 2 == 0 and PAIRS % 2 == 0 and TURNS > 5
    with ExitStack() as ctx:
        def sb(name, shape, dt=F32):
            return ctx.enter_context(nc.sbuf_tensor(name, shape, dt))

        def ps(name, shape):
            return ctx.enter_context(nc.psum_tensor(name, shape, F32))

        def sem(name):
            return ctx.enter_context(nc.semaphore(name))

        normed1 = sb("normed1", [TP, 2, D])
        normed1_t = sb("normed1_t", [P, 2, K2 * TP])
        stats = sb("stats", [TP, 2, 6])
        both = sb("both", [TP, 2, 2])
        mean2 = sb("mean2", [TP, NT])
        rstd2 = sb("rstd2", [TP, NT])
        shift2 = sb("shift2", [TP, NT])
        normed2 = sb("normed2", [TP, 2, D])
        normed2_t = sb("normed2_t", [P, 2, K2 * TP])
        normed_z = sb("normed_z", [TP, 2, D])
        logits = sb("logits", [TP, 2, INNER])
        weights = sb("weights", [TP, 2, INNER])
        top = sb("top", [TP, 2, H])
        total = sb("total", [TP, 2, H])
        norm_part = sb("norm_part", [P, PAIRS, NT])
        zeros = sb("zeros", [1, 2 * D], BF16)
        turn_ps = ps("xt_ps", [P, 2, D])
        rotated_ps = ps("rotated_ps", [TP, 2, D])
        logit_ps = [ps(f"logit_ps{j}", [TP, INNER]) for j in range(2)]
        wt_ps = [ps(f"wt_ps{j}", [P, PAIRS * P]) for j in range(2)]
        z_ps = [ps(f"z_ps{k}", [P, 2, D]) for k in range(PAIRS // 2)]
        chain, zeroed, stats_begun = sem("dve_chain_t"), sem("zeroed_t"), sem("stats_begun")
        normed1_ready, turned1, copied1 = sem("normed1_ready"), sem("turned1"), sem("copied1")
        rotated, numbers_ready, rstd_ready = sem("rotated"), sem("numbers_ready"), sem("rstd_ready")
        normed2_ready, turned2, copied2 = sem("normed2_ready"), sem("turned2"), sem("copied2")
        normed_z_ready, shift2_ready = sem("normed_z_ready"), sem("shift2_ready")
        scored, top_ready, shifted, exps = sem("scored"), sem("top_ready"), sem("shifted"), sem("exps")
        total_ready, weights_ready = sem("total_ready"), sem("weights_ready")
        weights_turned, weights_kept = sem("weights_turned"), sem("weights_kept")
        summed = sem("summed")
        block = ctx.enter_context(nc.Block())

        def heads(a):
            return a.rearrange("p (h g) -> p h g", g=G)

        def inside(q):
            return not isinstance(q, int) or 0 <= q < TURNS

        def all_turns(engine, turn, chain_of=None, links=0):
            for r in range(-2, 2):
                turn(r)
            with engine.Fori(2, TURNS - 2) as r:
                if chain_of is not None:
                    chain_of.loop(r - 2, links)
                turn(r)
                if chain_of is not None:
                    assert chain_of.n == links, chain_of.n
            if chain_of is not None:
                chain_of.close(TURNS - 4)
            for r in range(TURNS - 2, TURNS + 2):
                turn(r)

        @block.gpsimd
        def _(pool):
            def inverse_deviation(q):
                pool.wait_ge(numbers_ready, q + 1)
                at = bass.ds(q * 2, 2)
                pool.tensor_tensor(rstd2[:, at], rstd2[:, at], minus_half[:, 0:2], ALU.pow).then_inc(rstd_ready, 1)

            def shift(q, j):
                pool.wait_ge(top_ready, q * 2 + (j + 1))
                pool.tensor_tensor(heads(logits[:, j, :]), heads(logits[:, j, :]),
                                   top[:, j, :].unsqueeze(2).to_broadcast([TP, H, G]),
                                   ALU.subtract).then_inc(shifted, 1)

            def divide(q, j):
                pool.wait_ge(total_ready, q * 2 + (j + 1))
                pool.wait_ge(summed, q * 2 + (j + 1))
                pool.tensor_tensor(heads(weights[:, j, :]), heads(logits[:, j, :]),
                                   total[:, j, :].unsqueeze(2).to_broadcast([TP, H, G]),
                                   ALU.mult).then_inc(weights_ready, 1)

            def turn(r):
                if inside(r - 1):
                    shift(r - 1, 0)
                    shift(r - 1, 1)
                if inside(r + 1):
                    inverse_deviation(r + 1)
                if inside(r - 1):
                    divide(r - 1, 0)
                    divide(r - 1, 1)

            all_turns(pool, turn)

        @block.vector
        def _(dve):
            c = Chain(dve, chain)
            link = c.link

            def rotation(q):
                dve.wait_ge(rotated, q + 1)
                for j in range(2):
                    last = dve.tensor_tensor(x_sb[:, q * 2 + j, :], x_sb[:, q * 2 + j, :], rotated_ps[:, j, :],
                                             ALU.add)
                link(last)
                dve.sem_inc(stats_begun, 1)
                for j in range(2):
                    last = dve.bn_stats(stats[:, j, :], x_sb[:, q * 2 + j, :])
                link(last)
                dve.sem_inc(stats_begun, 1)
                for j in range(2):
                    last = dve.bn_aggr(both[:, j, :], stats[:, j, :])
                link(last)
                at = bass.ds(q * 2, 2)
                dve.tensor_copy(mean2[:, at], both[:, :, 0])
                dve.tensor_scalar(rstd2[:, at], both[:, :, 1], EPS, None, ALU.add).then_inc(numbers_ready, 1)

            def normalise(q):
                for j in range(2):
                    at = bass.ds(q * 2 + j, 1)
                    last = dve.tensor_scalar(normed2[:, j, :], x_sb[:, q * 2 + j, :], mean2[:, at],
                                             rstd2[:, at], ALU.subtract, ALU.mult)
                last.then_inc(normed2_ready, 1)
                at = bass.ds(q * 2, 2)
                dve.scalar_tensor_tensor(shift2[:, at], mean2[:, at], -1.0, rstd2[:, at], ALU.mult,
                                         ALU.mult).then_inc(shift2_ready, 1)

            def bias_and_top(q, j):
                dve.wait_ge(scored, q * 2 + (j + 1))
                if not (isinstance(q, int) and q == 0):
                    dve.wait_ge(weights_ready, q * 2 + (j - 1))
                link(dve.tensor_tensor(logits[:, j, :], logit_ps[j][:, :], bias_bc[0:TP, :], ALU.add))
                dve.tensor_reduce(top[:, j, :], heads(logits[:, j, :]), AX.X, ALU.max).then_inc(top_ready, 1)

            def totals(q, j):
                dve.wait_ge(exps, q * 2 + (j + 1))
                link(dve.tensor_reduce(total[:, j, :], heads(logits[:, j, :]), AX.X, ALU.add))
                dve.reciprocal(total[:, j, :], total[:, j, :]).then_inc(total_ready, 1)

            def turn(r):
                if inside(r - 1):
                    bias_and_top(r - 1, 0)
                    bias_and_top(r - 1, 1)
                if inside(r - 1):
                    totals(r - 1, 0)
                    totals(r - 1, 1)
                if inside(r + 1):
                    rotation(r + 1)
                if inside(r + 1):
                    dve.wait_ge(rstd_ready, r + 2)
                    if not isinstance(r, int) or r >= 0:
                        dve.wait_ge(turned2, r + 1)
                    normalise(r + 1)

            link(dve.memset(zeros[:, :], 0.0))
            dve.sem_inc(zeroed, 1)
            all_turns(dve, turn, c, 7)
            dve.wait_ge(weights_kept, NT)
            dve.tensor_reduce(norm_sb[:, :], norm_part[:, :, :], AX.X, ALU.add)
            dve.wait_ge(summed, NT + 2)
            for k in range(PAIRS // 2):
                dve.tensor_copy(z_sb[:, 2 * k:2 * k + 2, :], z_ps[k][:, :, :])

        @block.scalar
        def _(act):
            def normalise(q):
                if not (isinstance(q, int) and q == 0):
                    act.wait_ge(turned1, q)
                for j in range(2):
                    last = act.activation(normed1[:, j, :], x_sb[:, q * 2 + j, :], ACT.Identity,
                                          bias=shift1[:, bass.ds(q * 2 + j, 1)],
                                          scale=scale1[:, bass.ds(q * 2 + j, 1)])
                last.then_inc(normed1_ready, 1)

            def normalise_again(q):
                act.wait_ge(shift2_ready, q + 1)
                act.wait_ge(summed, q * 2 + 2)
                for j in range(2):
                    at = bass.ds(q * 2 + j, 1)
                    last = act.activation(normed_z[:, j, :], x_sb[:, q * 2 + j, :], ACT.Identity,
                                          bias=shift2[:, at], scale=rstd2[:, at])
                last.then_inc(normed_z_ready, 1)

            def exponentials(q, j):
                act.wait_ge(shifted, q * 2 + (j + 1))
                act.activation(logits[:, j, :], logits[:, j, :], ACT.Exp).then_inc(exps, 1)

            def keep_weights(q, j):
                act.wait_ge(weights_turned, q * 2 + (j + 1))
                for k in range(PAIRS):
                    last = act.activation(wt_sb[:, q * 2 + j, k, :], wt_ps[j][:, k * TP:(k + 1) * TP], ACT.Copy,
                                          accum_out=norm_part[:, k, bass.ds(q * 2 + j, 1)])
                last.then_inc(weights_kept, 1)

            def turn(r):
                if inside(r + 1):
                    act.wait_ge(turned1, r + 2)
                    act.activation(normed1_t[:, :, :], turn_ps[:, :, 0:K2 * TP], ACT.Copy).then_inc(copied1, 1)
                if inside(r - 2):
                    normalise_again(r - 2)
                if inside(r + 2):
                    normalise(r + 2)
                if inside(r):
                    act.wait_ge(turned2, r + 1)
                    act.activation(normed2_t[:, :, :], turn_ps[:, :, 0:K2 * TP], ACT.Copy).then_inc(copied2, 1)
                if inside(r - 1):
                    exponentials(r - 1, 0)
                    exponentials(r - 1, 1)
                if inside(r - 2):
                    keep_weights(r - 2, 0)
                    keep_weights(r - 2, 1)

            all_turns(act, turn)

        @block.tensor
        def _(pe):
            def transposes(normed, done):
                for j in range(2):
                    for k in range(K2):
                        last = pe.transpose(turn_ps[:, j, k * TP:(k + 1) * TP], normed[:, j, k * P:(k + 1) * P],
                                            ident[0:TP, 0:TP])
                last.then_inc(done, 1)

            def rotate(q):
                pe.wait_ge(copied1, q + 1)
                if not (isinstance(q, int) and q == 0):
                    pe.wait_ge(numbers_ready, q)
                for j in range(2):
                    for k in range(K2):
                        last = pe.matmul(rotated_ps[:, j, :], normed1_t[:, j, k * TP:(k + 1) * TP],
                                         mat_t[:, k, :], start=(k == 0), stop=(k == K2 - 1))
                last.then_inc(rotated, 1)

            def score(q):
                pe.wait_ge(copied2, q + 1)
                if not (isinstance(q, int) and q == 0):
                    pe.wait_ge(top_ready, q * 2)
                for j in range(2):
                    for k in range(K2):
                        last = pe.matmul(logit_ps[j][:, :], normed2_t[:, j, k * TP:(k + 1) * TP], wxs[:, k, :],
                                         start=(k == 0), stop=(k == K2 - 1))
                    last.then_inc(scored, 1)

            def turn_weights(q, j):
                pe.wait_ge(weights_ready, q * 2 + (j + 1))
                if not (isinstance(q, int) and q == 0):
                    pe.wait_ge(weights_kept, q * 2)
                for k in range(PAIRS):
                    last = pe.transpose(wt_ps[j][:, k * TP:(k + 1) * TP], weights[:, j, k * P:(k + 1) * P],
                                        ident[0:TP, 0:TP])
                last.then_inc(weights_turned, 1)

            def sum_up(q, j):
                pe.wait_ge(normed_z_ready, q + 1)
                for k in range(PAIRS):
                    last = pe.matmul(z_ps[k // 2][:, k % 2, :], weights[:, j, k * P:(k + 1) * P],
                                     normed_z[:, j, :], start=False, stop=True, skip_group_check=True)
                last.then_inc(summed, 1)

            def turn(r):
                if inside(r + 1):
                    pe.wait_ge(normed1_ready, r + 2)
                    if not isinstance(r, int) or r > 0:
                        pe.wait_ge(copied2, r)
                    transposes(normed1, turned1)
                if inside(r - 1):
                    score(r - 1)
                if inside(r + 1):
                    rotate(r + 1)
                if inside(r):
                    pe.wait_ge(normed2_ready, r + 1)
                    transposes(normed2, turned2)
                if inside(r - 2):
                    turn_weights(r - 2, 0)
                    turn_weights(r - 2, 1)
                    sum_up(r - 2, 0)
                    sum_up(r - 2, 1)

            pe.wait_ge(zeroed, 1)
            for k in range(PAIRS // 2):
                last = pe.matmul(z_ps[k][:, :, :], zeros[:, 0:P], zeros[:, :], start=True, stop=True)
            last.then_inc(summed, 2)
            all_turns(pe, turn)


def slices_phase(nc, v):
    D, INNER, G, H, K2, PAIRS = (v[k] for k in ("D", "INNER", "G", "H", "K2", "PAIRS"))
    z_sb, wfx_sb, bfx_bc, wout_sb, q_sb = v["z_sb"], v["wfx_sb"], v["bfx_bc"], v["wout_sb"], v["q_sb"]
    pair_w, ident, norm_sb = v["pair_w"], v["ident"], v["norm_sb"]
    SCALE = G ** -0.5
    with ExitStack() as ctx:
        def sb(name, shape, dt=F32):
            return ctx.enter_context(nc.sbuf_tensor(name, shape, dt))

        def sem(name):
            return ctx.enter_context(nc.semaphore(name))

        zt_sb = sb("zt_sb", [P, K2, PAIRS, P])
        token = sb("token", [P, PAIRS, P])
        norm_inv = sb("norm_inv", [P, PAIRS])
        token_t = sb("token_t", [P, PAIRS, P])
        query_t, key_t, value = sb("query_t", [P, PAIRS, P]), sb("key_t", [P, PAIRS, P]), sb("value", [P, PAIRS, P])
        score = sb("score", [P, PAIRS, G])
        top, total = sb("top_s", [P, PAIRS]), sb("total_s", [P, PAIRS])
        attn, attn_t = sb("attn", [P, PAIRS, P]), sb("attn_t", [P, PAIRS, P])
        mixed_t = sb("mixed_t", [P, PAIRS, P])
        ps = [ctx.enter_context(nc.psum_tensor(f"slice_ps{k}", [P, PAIRS, P], F32)) for k in range(8)]
        chain, pe_done, act_done, ready = sem("dve_chain_s"), sem("pe_done"), sem("act_done"), sem("ready")
        block = ctx.enter_context(nc.Block())
        HALVES = [slice(0, G), slice(G, 2 * G)]

        @block.vector
        def _(dve):
            link = Chain(dve, chain).link
            dve.memset(attn[:, :, :], 0.0)
            link(dve.memset(token[:, :, :], 0.0))
            link(dve.tensor_scalar(norm_inv[:, :], norm_sb[:, :], 1e-5, None, ALU.add))
            link(dve.reciprocal(norm_inv[:, :], norm_inv[:, :]))
            dve.wait_ge(pe_done, 1)
            for k in range(K2):
                last = dve.tensor_copy(zt_sb[:, k, :, :], ps[k][:, :, :])
            last.then_inc(ready, 1)
            dve.wait_ge(pe_done, 2)
            for pair in range(PAIRS):
                for n, at in enumerate(HALVES):
                    cols = slice(pair * P + n * G, pair * P + (n + 1) * G)
                    last = dve.scalar_tensor_tensor(token[at, pair, at], bfx_bc[at, cols],
                                                    norm_sb[at, pair:pair + 1], ps[2][at, pair, at],
                                                    ALU.mult, ALU.add)
            link(last)
            dve.tensor_tensor(token[:, :, :], token[:, :, :],
                              norm_inv[:, :].unsqueeze(2).to_broadcast([P, PAIRS, P]),
                              ALU.mult).then_inc(ready, 1)
            dve.wait_ge(pe_done, 3)
            dve.tensor_copy(token_t[:, :, :], ps[3][:, :, :]).then_inc(ready, 1)
            dve.wait_ge(pe_done, 4)
            dve.tensor_copy(query_t[:, :, :], ps[4][:, :, :])
            dve.tensor_copy(key_t[:, :, :], ps[5][:, :, :])
            dve.tensor_copy(value[:, :, :], ps[6][:, :, :]).then_inc(ready, 1)
            dve.wait_ge(pe_done, 5)
            for at in HALVES:
                last = dve.tensor_scalar(score[at, :, :], ps[7][at, :, at], SCALE, None, ALU.mult)
            link(last)
            link(dve.tensor_reduce(top[:, :], score[:, :, :], AX.X, ALU.max))
            dve.tensor_tensor(score[:, :, :], score[:, :, :], top[:, :].unsqueeze(2).to_broadcast([P, PAIRS, G]),
                              ALU.subtract).then_inc(ready, 1)
            dve.wait_ge(act_done, 1)
            link(dve.tensor_reduce(total[:, :], score[:, :, :], AX.X, ALU.add))
            link(dve.reciprocal(total[:, :], total[:, :]))
            for at in HALVES:
                last = dve.tensor_tensor(attn[at, :, at], score[at, :, :],
                                         total[at, :].unsqueeze(2).to_broadcast([G, PAIRS, G]), ALU.mult)
            last.then_inc(ready, 1)
            dve.wait_ge(pe_done, 6)
            dve.tensor_copy(attn_t[:, :, :], ps[0][:, :, :]).then_inc(ready, 1)
            dve.wait_ge(pe_done, 7)
            dve.tensor_copy(mixed_t[:, :, :], ps[1][:, :, :]).then_inc(ready, 1)
            dve.wait_ge(pe_done, 8)
            for pair in range(PAIRS):
                dve.tensor_copy(q_sb[:, pair, :],
                                ps[2 + pair // 2][:, :, :].rearrange("p a b -> p (a b)")
                                [:, (pair % 2) * D:(pair % 2 + 1) * D])

        @block.scalar
        def _(act):
            act.wait_ge(ready, 5)
            act.activation(score[:, :, :], score[:, :, :], ACT.Exp).then_inc(act_done, 1)

        @block.tensor
        def _(pe):
            for k in range(K2):
                for pair in range(PAIRS):
                    last = pe.transpose(ps[k][:, pair, :], z_sb[:, pair, k * P:(k + 1) * P], ident[:, :])
            last.then_inc(pe_done, 1)
            pe.wait_ge(ready, 1)
            for pair in range(PAIRS):
                for k in range(K2):
                    last = pe.matmul(ps[2][:, pair, :], zt_sb[:, k, pair, :], wfx_sb[:, k, pair * P:(pair + 1) * P],
                                     start=(k == 0), stop=(k == K2 - 1))
            last.then_inc(pe_done, 1)
            pe.wait_ge(ready, 2)
            for pair in range(PAIRS):
                last = pe.transpose(ps[3][:, pair, :], token[:, pair, :], ident[:, :])
            last.then_inc(pe_done, 1)
            pe.wait_ge(ready, 3)
            for pair in range(PAIRS):
                pe.matmul(ps[4][:, pair, :], pair_w[:, 0, :], token_t[:, pair, :], start=True, stop=True)
                pe.matmul(ps[5][:, pair, :], pair_w[:, 1, :], token_t[:, pair, :], start=True, stop=True)
                last = pe.matmul(ps[6][:, pair, :], token_t[:, pair, :], pair_w[:, 2, :], start=True, stop=True)
            last.then_inc(pe_done, 1)
            pe.wait_ge(ready, 4)
            for pair in range(PAIRS):
                last = pe.matmul(ps[7][:, pair, :], query_t[:, pair, :], key_t[:, pair, :], start=True, stop=True)
            last.then_inc(pe_done, 1)
            pe.wait_ge(ready, 6)
            for pair in range(PAIRS):
                last = pe.transpose(ps[0][:, pair, :], attn[:, pair, :], ident[:, :])
            last.then_inc(pe_done, 1)
            pe.wait_ge(ready, 7)
            for pair in range(PAIRS):
                last = pe.matmul(ps[1][:, pair, :], value[:, pair, :], attn_t[:, pair, :], start=True, stop=True)
            last.then_inc(pe_done, 1)
            pe.wait_ge(ready, 8)
            for pair in range(PAIRS):
                out = ps[2 + pair // 2][:, :, :].rearrange("p a b -> p (a b)")
                last = pe.matmul(out[:, (pair % 2) * D:(pair % 2 + 1) * D], mixed_t[:, pair, :],
                                 wout_sb[:, pair, :], start=True, stop=True)
            last.then_inc(pe_done, 1)


def output_phase(nc, v):
    D, K2, PAIRS, TP, NT = (v[k] for k in ("D", "K2", "PAIRS", "TP", "NT"))
    x_sb, wt_sb, q_sb, bout_bc, out = v["x_sb"], v["wt_sb"], v["q_sb"], v["bout_bc"], v["out"]
    with ExitStack() as ctx:
        def sb(name, shape, dt=F32):
            return ctx.enter_context(nc.sbuf_tensor(name, shape, dt))

        def sem(name):
            return ctx.enter_context(nc.semaphore(name))

        here = sb("here", [P, 2, PAIRS, TP])
        done = sb("done", [TP, 2, D])
        sum_ps = [ctx.enter_context(nc.psum_tensor(f"sum_ps{j}", [TP, D], F32)) for j in range(2)]
        here_ready, mixed, biased, done_ready = sem("here_ready"), sem("mixed"), sem("biased"), sem("done_ready")
        stored = [sem(f"out_stored{j}") for j in range(2)]
        block = ctx.enter_context(nc.Block())

        @block.scalar
        def _(act):
            with act.Fori(0, NT // 2) as turn:
                t = turn * 2
                for j in range(2):
                    act.wait_ge(mixed, t + (j + 1))
                    act.activation(here[:, j, :, :], wt_sb[:, t + j, :, :], ACT.Copy).then_inc(here_ready, 1)

        @block.gpsimd
        def _(pool):
            with pool.Fori(0, NT // 2) as turn:
                t = turn * 2
                for j in range(2):
                    pool.tensor_tensor(x_sb[:, t + j, :], x_sb[:, t + j, :], bout_bc[0:TP, :],
                                       ALU.add).then_inc(biased, 1)

        @block.tensor
        def _(pe):
            pe.nop().then_inc(mixed, 2)
            with pe.Fori(0, NT // 2) as turn:
                t = turn * 2
                for j in range(2):
                    pe.wait_ge(here_ready, t + (j + 1))
                    pe.wait_ge(done_ready, t + (j + 1))
                    for k in range(PAIRS):
                        last = pe.matmul(sum_ps[j][:, :], here[:, j, k, :], q_sb[:, k, :], start=(k == 0),
                                         stop=(k == PAIRS - 1))
                    last.then_inc(mixed, 1)

        @block.vector
        def _(dve):
            dve.nop().then_inc(done_ready, 2)
            with dve.Fori(0, NT // 2) as turn:
                t = turn * 2
                for j in range(2):
                    dve.wait_ge(mixed, t + (j + 3))
                    dve.wait_ge(biased, t + (j + 1))
                    dve.wait_ge(stored[j], t * 8 + 16)
                    dve.tensor_tensor(done[:, j, :], sum_ps[j][:, :], x_sb[:, t + j, :],
                                      ALU.add).then_inc(done_ready, 1)

        @block.sync
        def _(sp):
            for j in range(2):
                sp.nop().then_inc(stored[j], 16)
            with sp.Fori(0, NT // 2) as turn:
                t = turn * 2
                for j in range(2):
                    sp.wait_ge(done_ready, t + (j + 3))
                    sp.dma_start(out[bass.ds(t * TP + j * TP, TP), :], done[:, j, :]).then_inc(stored[j], 16)
            for j in range(2):
                sp.wait_ge(stored[j], 16 * (NT // 2) + 16)


_INS = ["x", "src", "dst", "edge_weight", "L0_ffn_W_fx", "L0_ffn_b_fx", "L0_ffn_W_x", "L0_ffn_b_x",
        "L0_ffn_W_slice", "L0_ffn_b_slice", "L0_ffn_W_q", "L0_ffn_W_k", "L0_ffn_W_v", "L0_ffn_W_out",
        "L0_ffn_b_out", "L0_ffn_temperature"]


def kernel(**inputs):
    import numpy as np
    import concourse.bacc as bacc
    from concourse.bass_utils import run_bass_kernel_spmd

    nc = bacc.Bacc("TRN2", target_bir_lowering=False, num_devices=1)
    arrays, args = {}, []
    for name in _INS:
        a = np.ascontiguousarray(inputs[name])
        arrays["in_" + name] = a
        args.append(nc.dram_tensor("in_" + name, a.shape, mybir.dt.from_np(a.dtype), kind="ExternalInput").ap())
    out = nc.dram_tensor("out_x", inputs["x"].shape, F32, kind="ExternalOutput").ap()
    build(nc, *args, out)
    r = run_bass_kernel_spmd(nc, [arrays], core_ids=[0])
    return r.results[0]["out_x"]
```
